# Optimizing a Trainium2 kernel written in Bass

```python
import numpy as np
import jax
import jax.numpy as jnp

def _softmax(x, axis=-1):
    return jax.nn.softmax(x, axis=axis)

def _gelu(x):
    return jax.nn.gelu(x, approximate=True)

def _silu(x):
    return jax.nn.silu(x)

def _sigmoid(x):
    return jax.nn.sigmoid(x)

def _layernorm(x, axis=-1, eps=1e-05):
    m = jnp.mean(x, axis=axis, keepdims=True)
    v = jnp.var(x, axis=axis, keepdims=True)
    return (x - m) / jnp.sqrt(v + eps)

def _scatter_add(tgt, idx, src, axis=0):
    return tgt.at[idx].add(src)

def _segment_sum(src, seg, n):
    return jax.ops.segment_sum(src, seg, n)
kernel_name = 'mk_sandwich_d2_jaxref_r8_d8c273'

def setup_inputs(seed: int=0):
    np.random.seed(seed)
    _w = jnp.asarray

    def _L0_attn_setup():
        import jax, jax.numpy as jnp
        import numpy as np
        from jax import lax
        D_MODEL = 128
        B, T = (4, 256)
        LN_EPS = 1e-05

        def _ln(x, w, b):
            mu = jnp.mean(x, axis=-1, keepdims=True)
            var = jnp.mean((x - mu) ** 2, axis=-1, keepdims=True)
            return (x - mu) * lax.rsqrt(var + LN_EPS) * w + b

        def _wkv(u, k, v):
            Bb, Tt, C = k.shape

            def step(carry, kv):
                aa, bb = carry
                kk, vv = kv
                p = jnp.maximum(bb, u + kk)
                e1 = jnp.exp(bb - p)
                e2 = jnp.exp(u + kk - p)
                out = (e1 * aa + e2 * vv) / (e1 + e2)
                p2 = jnp.maximum(bb, kk)
                e1b = jnp.exp(bb - p2)
                e2b = jnp.exp(kk - p2)
                return ((e1b * aa + e2b * vv, p2 + jnp.log(e1b + e2b)), out)
            init = (jnp.zeros((Bb, C), k.dtype), jnp.zeros((Bb, C), k.dtype))
            _, outs = lax.scan(step, init, (jnp.swapaxes(k, 0, 1), jnp.swapaxes(v, 0, 1)))
            return jnp.swapaxes(outs, 0, 1)
        key = jax.random.key(seed)
        ks = jax.random.split(key, 12)
        C = D_MODEL
        s = 0.02
        return {'x': jax.random.normal(ks[0], (B, T, C), jnp.float32), 'time_decay': jax.random.normal(ks[1], (C,), jnp.float32), 'time_first': jax.random.normal(ks[2], (C,), jnp.float32) * 0.5, 'time_shift': jax.random.normal(ks[3], (1, 1, C), jnp.float32) * 0.1, 'Wk': jax.random.normal(ks[4], (C, C), jnp.float32) * s, 'Wv': jax.random.normal(ks[5], (C, C), jnp.float32) * s, 'Wr': jax.random.normal(ks[6], (C, C), jnp.float32) * s, 'Wck': jax.random.normal(ks[7], (4 * C, C), jnp.float32) * s, 'Wcv': jax.random.normal(ks[8], (C, 4 * C), jnp.float32) * s, 'Wcr': jax.random.normal(ks[9], (C, C), jnp.float32) * s, 'ln1_w': jnp.ones((C,), jnp.float32), 'ln1_b': jnp.zeros((C,), jnp.float32), 'ln2_w': jnp.ones((C,), jnp.float32), 'ln2_b': jnp.zeros((C,), jnp.float32)}
    _L0_attn_in = _L0_attn_setup()

    def _L0_ffn_setup():
        import jax, jax.numpy as jnp
        import numpy as np
        B, S, H = (2, 128, 128)
        E, F = (16, 64)
        G, TOPK_G, TOPK = (4, 2, 4)
        N_SHARED = 2
        ROUTE_SCALE = 1.0
        FS = N_SHARED * F

        def _gate(x, w_gate):
            T = x.shape[0]
            scores = jax.nn.sigmoid(x @ w_gate.T)
            sv = scores.reshape(T, G, E // G)
            group_scores = jax.lax.top_k(sv, 2)[0].sum(-1)
            top_groups = jax.lax.top_k(group_scores, TOPK_G)[1]
            allowed = jnp.zeros((T, G), dtype=bool).at[jnp.arange(T)[:, None], top_groups].set(True)
            masked = jnp.where(allowed[:, :, None], sv, -jnp.inf).reshape(T, E)
            _, idx = jax.lax.top_k(masked, TOPK)
            w = jnp.take_along_axis(scores, idx, axis=1)
            w = w / (w.sum(-1, keepdims=True) + 1e-06) * ROUTE_SCALE
            return (w, idx)

        def _swiglu(x, w1, w3, w2):
            return jax.nn.silu(x @ w1.T) * (x @ w3.T) @ w2.T
        key = jax.random.key(seed)
        ks = jax.random.split(key, 8)
        scale = 0.02
        return {'hidden_states': jax.random.normal(ks[0], (B, S, H), dtype=jnp.float32), 'w_gate': jax.random.normal(ks[1], (E, H), dtype=jnp.float32) * scale, 'w1_e': jax.random.normal(ks[2], (E, F, H), dtype=jnp.float32) * scale, 'w3_e': jax.random.normal(ks[3], (E, F, H), dtype=jnp.float32) * scale, 'w2_e': jax.random.normal(ks[4], (E, H, F), dtype=jnp.float32) * scale, 'w1_s': jax.random.normal(ks[5], (FS, H), dtype=jnp.float32) * scale, 'w3_s': jax.random.normal(ks[6], (FS, H), dtype=jnp.float32) * scale, 'w2_s': jax.random.normal(ks[7], (H, FS), dtype=jnp.float32) * scale}
    _L0_ffn_in = _L0_ffn_setup()

    def _L1_attn_setup():
        import jax, jax.numpy as jnp
        import numpy as np
        B, S, D, H = (2, 256, 128, 16)
        Dh = D // H
        C = 2
        EPS = 1e-06
        LN_EPS = 1e-05

        def _rope_cache(seq_len, dh):
            half = dh // 2
            inv_freq = 1.0 / 10000.0 ** (jnp.arange(0, 2 * half, 2, dtype=jnp.float32) / dh)
            t = jnp.arange(seq_len, dtype=jnp.float32)
            freqs = t[:, None] * inv_freq[None, :]
            return (jnp.cos(freqs), jnp.sin(freqs))

        def _apply_rope(u, cos, sin):
            half = u.shape[-1] // 2
            c = cos[None, :, None, :]
            s = sin[None, :, None, :]
            u1, u2 = (u[..., :half], u[..., half:2 * half])
            return jnp.concatenate([u1 * c - u2 * s, u1 * s + u2 * c], axis=-1)

        def _deltanet_fwd(x, Wq, Wk, Wv, Wbeta, bbeta, Wo, bo, ln_gamma, ln_beta):
            Bn, Sn, Dm = x.shape
            q = (x @ Wq).reshape(Bn, Sn, H, Dh)
            k = (x @ Wk).reshape(Bn, Sn, H, Dh)
            v = (x @ Wv).reshape(Bn, Sn, H, Dh)
            cos, sin = _rope_cache(Sn, Dh)
            q = _apply_rope(q, cos, sin)
            k = _apply_rope(k, cos, sin)
            phi = lambda u: jax.nn.elu(u) + 1.0
            q_phi, k_phi = (phi(q), phi(k))
            beta = jnp.clip(jax.nn.sigmoid(x @ Wbeta + bbeta).reshape(Bn, Sn, H, C), 0.001, 0.999)

            def tm(u):
                return u.transpose(0, 2, 1, 3).reshape(Bn * H, Sn, -1).transpose(1, 0, 2)
            qs, ks_, vs, bs = (tm(q_phi), tm(k_phi), tm(v), tm(beta))
            BH = Bn * H
            M0 = jnp.zeros((BH, C, Dh, Dh), jnp.float32)
            Z0 = jnp.zeros((BH, C, Dh), jnp.float32)

            def step(carry, inp):
                M, Z = carry
                q_t, k_t, v_t, b_t = inp
                M = M * b_t[:, :, None, None] + (k_t[:, :, None] * v_t[:, None, :])[:, None]
                Z = Z * b_t[:, :, None] + k_t[:, None, :]
                num = jnp.einsum('bd,bcde->be', q_t, M)
                den = jnp.einsum('bd,bcd->b', q_t, Z) + EPS
                return ((M, Z), num / den[:, None])
            _, ys = jax.lax.scan(step, (M0, Z0), (qs, ks_, vs, bs))
            out = ys.transpose(1, 0, 2).reshape(Bn, H, Sn, Dh).transpose(0, 2, 1, 3).reshape(Bn, Sn, Dm)
            out = out @ Wo + bo
            h = x + out
            mu = jnp.mean(h, axis=-1, keepdims=True)
            var = jnp.mean((h - mu) ** 2, axis=-1, keepdims=True)
            return ln_gamma * (h - mu) / jnp.sqrt(var + LN_EPS) + ln_beta
        key = jax.random.key(seed)
        ks = jax.random.split(key, 8)
        w = 0.02
        x = jax.random.normal(ks[0], (B, S, D), jnp.float32)
        Wq = jax.random.normal(ks[1], (D, D), jnp.float32) * w
        Wk = jax.random.normal(ks[2], (D, D), jnp.float32) * w
        Wv = jax.random.normal(ks[3], (D, D), jnp.float32) * w
        Wbeta = jax.random.normal(ks[4], (D, H * C), jnp.float32) * w
        bbeta = jnp.full((H * C,), np.log(0.98 / 0.02), jnp.float32)
        Wo = jax.random.normal(ks[5], (D, D), jnp.float32) * w
        bo = jnp.zeros((D,), jnp.float32)
        ln_gamma = jnp.ones((D,), jnp.float32)
        ln_beta = jnp.zeros((D,), jnp.float32)
        return {'x': x, 'Wq': Wq, 'Wk': Wk, 'Wv': Wv, 'Wbeta': Wbeta, 'bbeta': bbeta, 'Wo': Wo, 'bo': bo, 'ln_gamma': ln_gamma, 'ln_beta': ln_beta}
    _L1_attn_in = _L1_attn_setup()

    def _L1_ffn_setup():
        import jax, jax.numpy as jnp
        import numpy as np
        N_HEADS = 16
        N_KV_HEADS = 4
        N_EMBD = 128
        HEAD_DIM = N_EMBD // N_HEADS
        N_EXPERTS = 8
        TOP_K = 2
        EPS = 1e-06

        def _rmsnorm(x, w):
            xf = x.astype(jnp.float32)
            n = xf * jax.lax.rsqrt(jnp.mean(xf * xf, axis=-1, keepdims=True) + EPS)
            return n.astype(x.dtype) * w

        def _gqa(x, wq, wk, wv, wo):
            B, S, C = x.shape
            n_rep = N_HEADS // N_KV_HEADS
            q = (x @ wq.T).reshape(B, S, N_HEADS, HEAD_DIM)
            k = (x @ wk.T).reshape(B, S, N_KV_HEADS, HEAD_DIM)
            v = (x @ wv.T).reshape(B, S, N_KV_HEADS, HEAD_DIM)
            k = jnp.repeat(k, n_rep, axis=2)
            v = jnp.repeat(v, n_rep, axis=2)
            scale = 1.0 / np.sqrt(HEAD_DIM).astype(np.float32)
            attn = jnp.einsum('bqhd,bkhd->bhqk', q, k) * scale
            causal = jnp.tril(jnp.ones((S, S), dtype=bool))
            attn = jnp.where(causal, attn, jnp.float32(-jnp.inf))
            attn = jax.nn.softmax(attn, axis=-1)
            out = jnp.einsum('bhqk,bkhd->bqhd', attn, v).reshape(B, S, C)
            return out @ wo.T

        def _moe(x, gate_w, expert_w):
            B, S, C = x.shape
            t = x.reshape(B * S, C)
            logits = t @ gate_w.T
            w, sel = jax.lax.top_k(logits, TOP_K)
            w = jax.nn.softmax(w.astype(jnp.float32), axis=1).astype(t.dtype)
            comb = jnp.sum(w[..., None] * jax.nn.one_hot(sel, N_EXPERTS, dtype=t.dtype), axis=1)
            out = jnp.zeros_like(t)
            for e in range(N_EXPERTS):
                out = out + comb[:, e, None] * (t @ expert_w[e].T)
            return out.reshape(B, S, C)
        key = jax.random.key(seed)
        ks = jax.random.split(key, 10)
        B, S, C = (4, 256, N_EMBD)
        s = 0.02
        return {'x': jax.random.normal(ks[0], (B, S, C), dtype=jnp.float32), 'attn_norm_w': jnp.ones((C,), dtype=jnp.float32), 'ffn_norm_w': jnp.ones((C,), dtype=jnp.float32), 'wq': jax.random.normal(ks[1], (C, C), dtype=jnp.float32) * s, 'wk': jax.random.normal(ks[2], (N_KV_HEADS * HEAD_DIM, C), dtype=jnp.float32) * s, 'wv': jax.random.normal(ks[3], (N_KV_HEADS * HEAD_DIM, C), dtype=jnp.float32) * s, 'wo': jax.random.normal(ks[4], (C, C), dtype=jnp.float32) * s, 'gate_w': jax.random.normal(ks[5], (N_EXPERTS, C), dtype=jnp.float32) * s, 'expert_w': jax.random.normal(ks[6], (N_EXPERTS, C, C), dtype=jnp.float32) * s}
    _L1_ffn_in = _L1_ffn_setup()
    _d = {'L0_attn_x': _L0_attn_in['x'], 'L0_attn_time_decay': _L0_attn_in['time_decay'], 'L0_attn_time_first': _L0_attn_in['time_first'], 'L0_attn_time_shift': _L0_attn_in['time_shift'], 'L0_attn_Wk': _L0_attn_in['Wk'], 'L0_attn_Wv': _L0_attn_in['Wv'], 'L0_attn_Wr': _L0_attn_in['Wr'], 'L0_attn_Wck': _L0_attn_in['Wck'], 'L0_attn_Wcv': _L0_attn_in['Wcv'], 'L0_attn_Wcr': _L0_attn_in['Wcr'], 'L0_attn_ln1_w': _L0_attn_in['ln1_w'], 'L0_attn_ln1_b': _L0_attn_in['ln1_b'], 'L0_attn_ln2_w': _L0_attn_in['ln2_w'], 'L0_attn_ln2_b': _L0_attn_in['ln2_b'], 'L0_ffn_w_gate': _L0_ffn_in['w_gate'], 'L0_ffn_w1_e': _L0_ffn_in['w1_e'], 'L0_ffn_w3_e': _L0_ffn_in['w3_e'], 'L0_ffn_w2_e': _L0_ffn_in['w2_e'], 'L0_ffn_w1_s': _L0_ffn_in['w1_s'], 'L0_ffn_w3_s': _L0_ffn_in['w3_s'], 'L0_ffn_w2_s': _L0_ffn_in['w2_s'], 'L1_attn_Wq': _L1_attn_in['Wq'], 'L1_attn_Wk': _L1_attn_in['Wk'], 'L1_attn_Wv': _L1_attn_in['Wv'], 'L1_attn_Wbeta': _L1_attn_in['Wbeta'], 'L1_attn_bbeta': _L1_attn_in['bbeta'], 'L1_attn_Wo': _L1_attn_in['Wo'], 'L1_attn_bo': _L1_attn_in['bo'], 'L1_attn_ln_gamma': _L1_attn_in['ln_gamma'], 'L1_attn_ln_beta': _L1_attn_in['ln_beta'], 'L1_ffn_attn_norm_w': _L1_ffn_in['attn_norm_w'], 'L1_ffn_ffn_norm_w': _L1_ffn_in['ffn_norm_w'], 'L1_ffn_wq': _L1_ffn_in['wq'], 'L1_ffn_wk': _L1_ffn_in['wk'], 'L1_ffn_wv': _L1_ffn_in['wv'], 'L1_ffn_wo': _L1_ffn_in['wo'], 'L1_ffn_gate_w': _L1_ffn_in['gate_w'], 'L1_ffn_expert_w': _L1_ffn_in['expert_w']}
    _x0 = _d['L0_attn_x']
    _d['L0_attn_x'] = jax.random.normal(jax.random.fold_in(jax.random.key(seed), 1), (4, 1024, 128), dtype=_x0.dtype)
    del _x0
    return _d

def reference(L0_attn_x, L0_attn_time_decay, L0_attn_time_first, L0_attn_time_shift, L0_attn_Wk, L0_attn_Wv, L0_attn_Wr, L0_attn_Wck, L0_attn_Wcv, L0_attn_Wcr, L0_attn_ln1_w, L0_attn_ln1_b, L0_attn_ln2_w, L0_attn_ln2_b, L0_ffn_w_gate, L0_ffn_w1_e, L0_ffn_w3_e, L0_ffn_w2_e, L0_ffn_w1_s, L0_ffn_w3_s, L0_ffn_w2_s, L1_attn_Wq, L1_attn_Wk, L1_attn_Wv, L1_attn_Wbeta, L1_attn_bbeta, L1_attn_Wo, L1_attn_bo, L1_attn_ln_gamma, L1_attn_ln_beta, L1_ffn_attn_norm_w, L1_ffn_ffn_norm_w, L1_ffn_wq, L1_ffn_wk, L1_ffn_wv, L1_ffn_wo, L1_ffn_gate_w, L1_ffn_expert_w):

    def _L0_attn_ref(x, time_decay, time_first, time_shift, Wk, Wv, Wr, Wck, Wcv, Wcr, ln1_w, ln1_b, ln2_w, ln2_b):
        import jax, jax.numpy as jnp
        import numpy as np
        from jax import lax
        D_MODEL = 128
        B, T = (4, 256)
        LN_EPS = 1e-05

        def _ln(x, w, b):
            mu = jnp.mean(x, axis=-1, keepdims=True)
            var = jnp.mean((x - mu) ** 2, axis=-1, keepdims=True)
            return (x - mu) * lax.rsqrt(var + LN_EPS) * w + b

        def _wkv(u, k, v):
            Bb, Tt, C = k.shape

            def step(carry, kv):
                aa, bb = carry
                kk, vv = kv
                p = jnp.maximum(bb, u + kk)
                e1 = jnp.exp(bb - p)
                e2 = jnp.exp(u + kk - p)
                out = (e1 * aa + e2 * vv) / (e1 + e2)
                p2 = jnp.maximum(bb, kk)
                e1b = jnp.exp(bb - p2)
                e2b = jnp.exp(kk - p2)
                return ((e1b * aa + e2b * vv, p2 + jnp.log(e1b + e2b)), out)
            init = (jnp.zeros((Bb, C), k.dtype), jnp.zeros((Bb, C), k.dtype))
            _, outs = lax.scan(step, init, (jnp.swapaxes(k, 0, 1), jnp.swapaxes(v, 0, 1)))
            return jnp.swapaxes(outs, 0, 1)
        Bb, Tt, C = x.shape
        ts = time_shift
        h = _ln(x, ln1_w, ln1_b)
        x_shifted = jnp.concatenate([jnp.broadcast_to(ts, (Bb, 1, C)), h[:, :-1, :]], axis=1)
        xxx = h + (h - x_shifted) * ts
        k = jnp.einsum('btc,oc->bto', xxx, Wk)
        v = jnp.einsum('btc,oc->bto', xxx, Wv)
        r = jax.nn.sigmoid(jnp.einsum('btc,oc->bto', xxx, Wr))
        wkv = _wkv(time_first, k, v)
        x = x + r * wkv
        h2 = _ln(x, ln2_w, ln2_b)
        xx2 = jnp.concatenate([h2[:, -1:, :], h2[:, :-1, :]], axis=1)
        xxx2 = h2 + (xx2 - h2) * ts
        kc = jnp.einsum('btc,oc->bto', xxx2, Wck)
        rc = jax.nn.sigmoid(jnp.einsum('btc,oc->bto', xxx2, Wcr))
        vv = jnp.einsum('bth,ch->btc', jax.nn.relu(kc) ** 2, Wcv)
        return x + rc * vv

    def _L0_ffn_ref(hidden_states, w_gate, w1_e, w3_e, w2_e, w1_s, w3_s, w2_s):
        import jax, jax.numpy as jnp
        import numpy as np
        B, S, H = (2, 128, 128)
        E, F = (16, 64)
        G, TOPK_G, TOPK = (4, 2, 4)
        N_SHARED = 2
        ROUTE_SCALE = 1.0
        FS = N_SHARED * F

        def _gate(x, w_gate):
            T = x.shape[0]
            scores = jax.nn.sigmoid(x @ w_gate.T)
            sv = scores.reshape(T, G, E // G)
            group_scores = jax.lax.top_k(sv, 2)[0].sum(-1)
            top_groups = jax.lax.top_k(group_scores, TOPK_G)[1]
            allowed = jnp.zeros((T, G), dtype=bool).at[jnp.arange(T)[:, None], top_groups].set(True)
            masked = jnp.where(allowed[:, :, None], sv, -jnp.inf).reshape(T, E)
            _, idx = jax.lax.top_k(masked, TOPK)
            w = jnp.take_along_axis(scores, idx, axis=1)
            w = w / (w.sum(-1, keepdims=True) + 1e-06) * ROUTE_SCALE
            return (w, idx)

        def _swiglu(x, w1, w3, w2):
            return jax.nn.silu(x @ w1.T) * (x @ w3.T) @ w2.T
        shape = hidden_states.shape
        x = hidden_states.reshape(-1, H)
        weights, idx = _gate(x, w_gate)
        combine = (jax.nn.one_hot(idx, E, dtype=x.dtype) * weights[..., None]).sum(1)
        g = jax.nn.silu(jnp.einsum('th,efh->tef', x, w1_e))
        u = jnp.einsum('th,efh->tef', x, w3_e)
        routed = jnp.einsum('tef,ehf,te->th', g * u, w2_e, combine)
        shared = _swiglu(x, w1_s, w3_s, w2_s)
        return (routed + shared).reshape(shape)

    def _L1_attn_ref(x, Wq, Wk, Wv, Wbeta, bbeta, Wo, bo, ln_gamma, ln_beta):
        import jax, jax.numpy as jnp
        import numpy as np
        B, S, D, H = (2, 256, 128, 16)
        Dh = D // H
        C = 2
        EPS = 1e-06
        LN_EPS = 1e-05

        def _rope_cache(seq_len, dh):
            half = dh // 2
            inv_freq = 1.0 / 10000.0 ** (jnp.arange(0, 2 * half, 2, dtype=jnp.float32) / dh)
            t = jnp.arange(seq_len, dtype=jnp.float32)
            freqs = t[:, None] * inv_freq[None, :]
            return (jnp.cos(freqs), jnp.sin(freqs))

        def _apply_rope(u, cos, sin):
            half = u.shape[-1] // 2
            c = cos[None, :, None, :]
            s = sin[None, :, None, :]
            u1, u2 = (u[..., :half], u[..., half:2 * half])
            return jnp.concatenate([u1 * c - u2 * s, u1 * s + u2 * c], axis=-1)

        def _deltanet_fwd(x, Wq, Wk, Wv, Wbeta, bbeta, Wo, bo, ln_gamma, ln_beta):
            Bn, Sn, Dm = x.shape
            q = (x @ Wq).reshape(Bn, Sn, H, Dh)
            k = (x @ Wk).reshape(Bn, Sn, H, Dh)
            v = (x @ Wv).reshape(Bn, Sn, H, Dh)
            cos, sin = _rope_cache(Sn, Dh)
            q = _apply_rope(q, cos, sin)
            k = _apply_rope(k, cos, sin)
            phi = lambda u: jax.nn.elu(u) + 1.0
            q_phi, k_phi = (phi(q), phi(k))
            beta = jnp.clip(jax.nn.sigmoid(x @ Wbeta + bbeta).reshape(Bn, Sn, H, C), 0.001, 0.999)

            def tm(u):
                return u.transpose(0, 2, 1, 3).reshape(Bn * H, Sn, -1).transpose(1, 0, 2)
            qs, ks_, vs, bs = (tm(q_phi), tm(k_phi), tm(v), tm(beta))
            BH = Bn * H
            M0 = jnp.zeros((BH, C, Dh, Dh), jnp.float32)
            Z0 = jnp.zeros((BH, C, Dh), jnp.float32)

            def step(carry, inp):
                M, Z = carry
                q_t, k_t, v_t, b_t = inp
                M = M * b_t[:, :, None, None] + (k_t[:, :, None] * v_t[:, None, :])[:, None]
                Z = Z * b_t[:, :, None] + k_t[:, None, :]
                num = jnp.einsum('bd,bcde->be', q_t, M)
                den = jnp.einsum('bd,bcd->b', q_t, Z) + EPS
                return ((M, Z), num / den[:, None])
            _, ys = jax.lax.scan(step, (M0, Z0), (qs, ks_, vs, bs))
            out = ys.transpose(1, 0, 2).reshape(Bn, H, Sn, Dh).transpose(0, 2, 1, 3).reshape(Bn, Sn, Dm)
            out = out @ Wo + bo
            h = x + out
            mu = jnp.mean(h, axis=-1, keepdims=True)
            var = jnp.mean((h - mu) ** 2, axis=-1, keepdims=True)
            return ln_gamma * (h - mu) / jnp.sqrt(var + LN_EPS) + ln_beta
        return _deltanet_fwd(x, Wq, Wk, Wv, Wbeta, bbeta, Wo, bo, ln_gamma, ln_beta)

    def _L1_ffn_ref(x, attn_norm_w, ffn_norm_w, wq, wk, wv, wo, gate_w, expert_w):
        import jax, jax.numpy as jnp
        import numpy as np
        N_HEADS = 16
        N_KV_HEADS = 4
        N_EMBD = 128
        HEAD_DIM = N_EMBD // N_HEADS
        N_EXPERTS = 8
        TOP_K = 2
        EPS = 1e-06

        def _rmsnorm(x, w):
            xf = x.astype(jnp.float32)
            n = xf * jax.lax.rsqrt(jnp.mean(xf * xf, axis=-1, keepdims=True) + EPS)
            return n.astype(x.dtype) * w

        def _gqa(x, wq, wk, wv, wo):
            B, S, C = x.shape
            n_rep = N_HEADS // N_KV_HEADS
            q = (x @ wq.T).reshape(B, S, N_HEADS, HEAD_DIM)
            k = (x @ wk.T).reshape(B, S, N_KV_HEADS, HEAD_DIM)
            v = (x @ wv.T).reshape(B, S, N_KV_HEADS, HEAD_DIM)
            k = jnp.repeat(k, n_rep, axis=2)
            v = jnp.repeat(v, n_rep, axis=2)
            scale = 1.0 / np.sqrt(HEAD_DIM).astype(np.float32)
            attn = jnp.einsum('bqhd,bkhd->bhqk', q, k) * scale
            causal = jnp.tril(jnp.ones((S, S), dtype=bool))
            attn = jnp.where(causal, attn, jnp.float32(-jnp.inf))
            attn = jax.nn.softmax(attn, axis=-1)
            out = jnp.einsum('bhqk,bkhd->bqhd', attn, v).reshape(B, S, C)
            return out @ wo.T

        def _moe(x, gate_w, expert_w):
            B, S, C = x.shape
            t = x.reshape(B * S, C)
            logits = t @ gate_w.T
            w, sel = jax.lax.top_k(logits, TOP_K)
            w = jax.nn.softmax(w.astype(jnp.float32), axis=1).astype(t.dtype)
            comb = jnp.sum(w[..., None] * jax.nn.one_hot(sel, N_EXPERTS, dtype=t.dtype), axis=1)
            out = jnp.zeros_like(t)
            for e in range(N_EXPERTS):
                out = out + comb[:, e, None] * (t @ expert_w[e].T)
            return out.reshape(B, S, C)
        h = x + _gqa(_rmsnorm(x, attn_norm_w), wq, wk, wv, wo)
        out = h + _moe(_rmsnorm(h, ffn_norm_w), gate_w, expert_w)
        return out
    x = L0_attn_x
    x = x + _layernorm(_L0_attn_ref(_layernorm(x, axis=-1), L0_attn_time_decay, L0_attn_time_first, L0_attn_time_shift, L0_attn_Wk, L0_attn_Wv, L0_attn_Wr, L0_attn_Wck, L0_attn_Wcv, L0_attn_Wcr, L0_attn_ln1_w, L0_attn_ln1_b, L0_attn_ln2_w, L0_attn_ln2_b), axis=-1)
    x = x + _layernorm(_L0_ffn_ref(_layernorm(x, axis=-1), L0_ffn_w_gate, L0_ffn_w1_e, L0_ffn_w3_e, L0_ffn_w2_e, L0_ffn_w1_s, L0_ffn_w3_s, L0_ffn_w2_s), axis=-1)
    x = x + _layernorm(_L1_attn_ref(_layernorm(x, axis=-1), L1_attn_Wq, L1_attn_Wk, L1_attn_Wv, L1_attn_Wbeta, L1_attn_bbeta, L1_attn_Wo, L1_attn_bo, L1_attn_ln_gamma, L1_attn_ln_beta), axis=-1)
    x = x + _layernorm(_L1_ffn_ref(_layernorm(x, axis=-1), L1_ffn_attn_norm_w, L1_ffn_ffn_norm_w, L1_ffn_wq, L1_ffn_wk, L1_ffn_wv, L1_ffn_wo, L1_ffn_gate_w, L1_ffn_expert_w), axis=-1)
    return x

_drawn_inputs = setup_inputs


def setup_inputs(seed=0):
    import zlib

    import numpy as np

    out = dict(_drawn_inputs(seed))
    spreads = {'L0_attn_ln1_w': (1.0, 0.577),
     'L0_attn_ln1_b': (0.0, 0.1),
     'L0_attn_ln2_w': (1.0, 0.6),
     'L0_attn_ln2_b': (0.0, 0.8),
     'L1_attn_bbeta': (3.891820192337036, 0.6),
     'L1_attn_bo': (0.0, 0.308),
     'L1_attn_ln_gamma': (1.0, 0.2),
     'L1_attn_ln_beta': (0.0, 0.1),
     'L1_ffn_attn_norm_w': (1.0, 0.6),
     'L1_ffn_ffn_norm_w': (1.0, 0.6)}
    factors = {'L0_attn_time_first': 8.0,
     'L0_attn_time_shift': 4.788,
     'L0_attn_Wr': 3.288,
     'L0_attn_Wck': 3.915,
     'L0_attn_Wcv': 3.66,
     'L0_attn_Wcr': 8.0,
     'L1_attn_Wq': 8.0,
     'L1_attn_Wk': 8.0,
     'L1_attn_Wv': 8.0,
     'L1_attn_Wbeta': 8.0,
     'L1_attn_Wo': 8.0,
     'L1_ffn_wq': 8.0,
     'L1_ffn_wk': 8.0,
     'L1_ffn_wv': 8.0,
     'L1_ffn_wo': 8.0,
     'L1_ffn_gate_w': 3.429,
     'L1_ffn_expert_w': 2.787}
    for name, (base, spread) in spreads.items():
        noise = np.random.default_rng([zlib.crc32(name.encode()), seed]).standard_normal(out[name].shape)
        drawn = base * np.exp(spread * noise) if base else spread * noise
        out[name] = jnp.asarray(drawn.astype(out[name].dtype))
    for name, factor in factors.items():
        out[name] = (out[name] * factor).astype(out[name].dtype)
    return out
```

```python
from contextlib import ExitStack

import concourse.bass as bass
from concourse import mybir

F32 = mybir.dt.float32
BF = mybir.dt.bfloat16
ALU = mybir.AluOpType
ACT = mybir.ActivationFunctionType
AX = mybir.AxisListType.X

T = 4096
NT = 32
NG = 8
NB = 4


STOP = 9


class Line:

    def __init__(self, eng, sem):
        self.eng, self.sem, self.n, self.seen = eng, sem, 0, {}

    def on(self, *producers):
        need = {}
        for sem, count in producers:
            need[sem.num] = (sem, max(need.get(sem.num, (sem, 0))[1], count))
        for key, (sem, count) in need.items():
            if self.seen.get(key, 0) < count:
                self.eng.wait_ge(sem, count)
                self.seen[key] = count
        return self.eng

    def did(self, ins):
        self.n += 1
        ins.then_inc(self.sem, 1)
        return (self.sem, self.n)

    def last(self):
        return (self.sem, self.n)


class Ring:

    def __init__(self, bufs):
        self.bufs, self.i, self.freed = bufs, -1, [() for _ in bufs]

    def take(self):
        self.i = (self.i + 1) % len(self.bufs)
        return self.i, self.bufs[self.i], self.freed[self.i]

    def free(self, i, *readers):
        self.freed[i] = readers


def skewed(stages, n):
    most = max(lag for lag, _ in stages)
    for step in range(n + most):
        for lag, stage in reversed(stages):
            if 0 <= step - lag < n:
                stage(step - lag)


def build(nc, I, out, stop=9):
    ctx = ExitStack()
    with ctx:
        semn = [0]

        def sem(name):
            semn[0] += 1
            return ctx.enter_context(nc.semaphore(f"{name}_{semn[0]}"))

        def sb(name, shape, dt=F32):
            return ctx.enter_context(nc.sbuf_tensor(name, shape, dt))

        PE = Line(nc.tensor, sem("s_pe"))
        V = Line(nc.vector, sem("s_v"))
        A = Line(nc.scalar, sem("s_a"))
        G = Line(nc.gpsimd, sem("s_g"))
        SP = Line(nc.sync, sem("s_sp"))

        PS = ctx.enter_context(nc.psum_tensor("PS", [128, 8 * 512], F32))

        def bank(i, n=1):
            return PS[:, 512 * i:512 * (i + n)]

        def dma(dst, src, s, *producers):
            SP.on(*producers).dma_start(dst, src).then_inc(s, 16)
            return (s, 16)

        def barrier():
            marks = [x.last() for x in (PE, V, A, G) if x.n]
            for x in (PE, V, A, G, SP):
                x.on(*marks)

        s_c = sem("s_c")
        loads = [0]

        def load(name, shape, dt=F32, src=None):
            t = sb("w_" + name, shape, dt)
            nc.scalar.dma_start(t[tuple(slice(None) for _ in shape)], I[name] if src is None else src).then_inc(s_c, 16)
            loads[0] += 1
            return t

        X = sb("X", [128, NT, 128])
        XA = sb("XA", [128, NT, 128])
        B = [sb(f"B{i}", [128, 4096 + 4]) for i in range(6)]

        def full(i):
            return B[i][:, 0:4096]

        def tm(i):
            return B[i][:, 0:4096].rearrange("p (i c) -> p i c", c=128)

        def seq(i):
            return B[i][:, 0:4100].rearrange("p (b t) -> p b t", b=4)

        RB = sb("RB", [128, 16, 512])
        xin = I["x"].rearrange("(i p) c -> p i c", p=128)
        s_x = [sem("s_x") for _ in range(NG)]
        for g in range(NG):
            nc.sync.dma_start(X[:, 4 * g:4 * g + 4, :], xin[:, 4 * g:4 * g + 4, :]).then_inc(s_x[g], 16)
        ident = load("ident", [128, 128])
        vecs = load("vecs", [128, 16])
        WW = sb("WW", [128, 14, 128])
        wA, wck, wcv = WW[:, 0:4, :], WW[:, 4:8, :], WW[:, 8:12, :]
        nc.scalar.dma_start(WW[:, 0:12, :], I["wL0"]).then_inc(s_c, 16)
        loads[0] += 1
        gate0 = load("gate0", [128, 16])
        identb = load("identb", [128, 128], BF)
        rst16 = load("rst16", [128, NT * 16])
        rk0 = load("rk0", [128, NT, 4])
        wq4, wvr, wbr = WW[:, 0:4, :], WW[:, 4:12, :], WW[:, 12:14, :]
        wo1 = load("wo1", [128, 128])
        hsum = load("hsum", [128, 128])
        rows = load("rows", [128, 3, 128])
        wqE = load("wqE", [128, 128])
        wkE = load("wkE", [128, 32])
        wvE = load("wvE", [128, 32])
        woE = load("woE", [128, 128])
        gateE = load("gateE", [128, 8])
        wE = WW[:, 0:8, :]
        rst8 = load("rst8", [128, NT * 8])
        msk = load("msk", [128, 2, 128], BF)
        W_READY = (s_c, 16 * loads[0])
        dv = sb("dv", [128, 3])
        (LN1W, LN1B, LN2W, LN2B, TS, _, _, _, ANW, FNW) = [vecs[:, j:j + 1] for j in range(10)]
        HU, HBB0, HBB1 = [dv[:, j:j + 1] for j in range(3)]

        st = sb("st", [128, NT, 6])
        mv = [sb(f"mv{i}", [128, NT, 2]) for i in range(2)]
        rs = [sb(f"rs{i}", [128, NT, 6]) for i in range(2)]
        mhalf = sb("mhalf", [128, 8])
        G_half = G.did(nc.gpsimd.memset(mhalf[:, :], -0.5))
        for x in (PE, V, A, G):
            x.on(W_READY)
        t_dv = V.did(nc.vector.tensor_scalar(dv[:, :], vecs[:, 5:8], 0.5, None, ALU.mult))
        A.on(t_dv)

        def stats(g, src, k, *producers):
            toks = []
            for i in range(4 * g, 4 * g + 4):
                t = V.did(V.on(*producers).bn_stats(st[:, i, :], src(i)))
                toks.append(t)
            for i in range(4 * g, 4 * g + 4):
                t = V.did(V.on(toks[i - 4 * g]).bn_aggr(mv[k][:, i, :], st[:, i, :]))
            return t

        def rstd(g, k, eps, t_stats, then=None):
            s4 = slice(4 * g, 4 * g + 4)
            R = rs[k]
            v = mv[k][:, s4, 1]
            t = G.did(G.on(t_stats).tensor_scalar(R[:, s4, 3], v, eps, None, ALU.add))
            t = G.did(G.on(t, G_half).tensor_tensor(R[:, s4, 0], R[:, s4, 3], mhalf[:, 0:4], ALU.pow))
            t0 = t
            t = G.did(G.on(t).tensor_tensor(R[:, s4, 4], mv[k][:, s4, 0], R[:, s4, 0], ALU.mult))
            t = G.did(G.on(t).tensor_scalar(R[:, s4, 1], R[:, s4, 4], -1.0, None, ALU.mult))
            if then is not None:
                t = G.did(G.on(t0).tensor_tensor(R[:, s4, 5], v, R[:, s4, 0], ALU.mult))
                t = G.did(G.on(t).tensor_tensor(R[:, s4, 2], R[:, s4, 5], R[:, s4, 0], ALU.mult))
                t = G.did(G.on(t).tensor_scalar(R[:, s4, 5], R[:, s4, 2], then, None, ALU.add))
                t = G.did(G.on(t).tensor_tensor(R[:, s4, 2], R[:, s4, 5], mhalf[:, 0:4], ALU.pow))
            return t

        def normed(i, k, dst, src, *producers):
            return A.did(A.on(*producers).activation(dst, src, ACT.Identity, bias=rs[k][:, i, 1:2],
                                                     scale=rs[k][:, i, 0:1]))

        def transposes(dst, src, idn, *producers):
            for j in range(4):
                t = PE.did(PE.on(*producers).transpose(dst[:, 128 * j:128 * j + 128], src(j), idn[:, :]))
            return t

        def rb(i, n=1):
            return RB[:, i:i + n, :]

        HF, XXX, KF, VF, RF, MM = 0, 1, 2, 3, 4, 5
        hf, mm_ = seq(HF), seq(MM)
        SS = ctx.enter_context(nc.sbuf_tensor("SS", [128, 4100], F32))
        ss = SS[:, :].rearrange("p (b t) -> p b t", b=4)
        rHN = Ring([rb(0), rb(1)])
        rD = Ring([rb(2, 2), rb(4, 2)])
        rE = Ring([rb(6, 2), rb(8, 2)])
        pT = Ring([bank(0), bank(1)])
        pP = Ring([bank(i) for i in range(2, 8)])

        def ch(ap4, g, shift=0):
            b, h = g // 2, g % 2
            o = 1 + 512 * h - shift
            return ap4[:, b, o:o + 512]

        def cf(i, g):
            return B[i][:, 512 * g:512 * g + 512]

        t_init = []
        for b in range(4):
            t_init.append(G.did(G.on().tensor_copy(hf[:, b, 0:1], TS)))
            t_init.append(G.did(nc.gpsimd.memset(mm_[:, b, 0:1], 0.0)))
            t_init.append(G.did(nc.gpsimd.memset(ss[:, b, 0:1], 1.0)))
        t_init = t_init[-1]
        K = {}

        def a_stats(g):
            K["st", g] = rstd(g, 0, 1e-5, stats(g, lambda i: X[:, i, :], 0, (s_x[g], 16)), then=1e-5)

        def a_norm(g):
            ib, buf, fr = rHN.take()
            for j in range(4):
                i = 4 * g + j
                t = V.did(V.on(K["st", g]).tensor_scalar(XA[:, i, :], X[:, i, :], mv[0][:, i, 0:1],
                                                         rs[0][:, i, 0:1], ALU.subtract, ALU.mult))
                t = A.did(A.on(t, *fr).activation(buf[:, 0, 128 * j:128 * j + 128], XA[:, i, :], ACT.Copy,
                                                  scale=rs[0][:, i, 2:3]))
            K["hn", g] = (ib, buf, t)

        def a_turn(g):
            ib, buf, t = K["hn", g]
            pi, p, fr = pT.take()
            t = transposes(p, lambda j: buf[:, 0, 128 * j:128 * j + 128], ident, t, *fr)
            rHN.free(ib, t)
            t = V.did(V.on(t, t_init).tensor_scalar(ch(hf, g), p, LN1W, LN1B, ALU.mult, ALU.add))
            pT.free(pi, t)
            K["hf", g] = t

        def a_mix(g):
            ib, buf, fr = rD.take()
            t = V.did(V.on(K["hf", g], *fr).tensor_tensor(buf[:, 0, :], ch(hf, g), ch(hf, g, 1), ALU.subtract))
            t = V.did(V.on(t).scalar_tensor_tensor(cf(XXX, g), buf[:, 0, :], TS, ch(hf, g), ALU.mult, ALU.add))
            rD.free(ib, t)
            K["xxx", g] = t

        def a_proj(g):
            for w in range(3):
                pi, p, fr = pP.take()
                t = PE.did(PE.on(K["xxx", g], *fr).matmul(p, wA[:, w, :], cf(XXX, g), start=True, stop=True))
                if w < 2:
                    t = A.did(A.on(t).activation(cf((KF, VF)[w], g), p, ACT.Copy))
                else:
                    t = A.did(A.on(t).activation(cf(RF, g), p, ACT.Tanh, scale=0.5))
                pP.free(pi, t)
                K["krv"[w], g] = t
            K["kv", g] = t

        def a_scan(g):
            b, h = g // 2, g % 2
            o = 512 * h
            k = cf(KF, g)
            t = V.did(V.on(K["k", g], t_init, *([K["m", g - 1]] if h else [])).tensor_tensor_scan(
                ch(mm_, g), k, k, mm_[:, b, o:o + 1], ALU.max, ALU.max))
            K["m", g] = t
            ib, buf, fr = rD.take()
            V.did(V.on(t, *fr).tensor_tensor(buf[:, 0, :], ch(mm_, g, 1), ch(mm_, g), ALU.subtract))
            t = V.did(V.on(t).tensor_tensor(buf[:, 1, :], k, ch(mm_, g), ALU.subtract))
            ie, eb, fr = rE.take()
            t = A.did(A.on(t, *fr).activation(eb, buf, ACT.Exp))
            rD.free(ib, t)
            t = V.did(V.on(t, *([K["s", g - 1]] if h else [])).tensor_tensor_scan(
                ch(ss, g), eb[:, 0, :], eb[:, 1, :], ss[:, b, o:o + 1], ALU.mult, ALU.add))
            K["s", g] = t
            rE.free(ie, t)

        skewed([(0, a_stats), (1, a_norm), (2, a_turn), (3, a_mix), (4, a_proj), (6, a_scan)], NG)

        for b in range(4):
            t = A.did(A.on(K["s", 2 * b + 1]).activation(ss[:, b, :], ss[:, b, :], ACT.Ln))
            K["bb", b] = V.did(V.on(t, K["m", 2 * b + 1]).tensor_tensor(mm_[:, b, :], mm_[:, b, :], ss[:, b, :], ALU.add))
        t_aa0 = []
        for b in range(4):
            t_aa0 = G.did(G.on(K["bb", b]).memset(ss[:, b, 0:1], 0.0))

        rY = Ring([rb(10), rb(11)])
        rT = Ring([rb(12), rb(13)])
        rHN.freed = [(A.last(),), (A.last(),)]

        def b_decay(g):
            b = g // 2
            ib, buf, fr = rD.take()
            ie, eb, fe = rE.take()
            it, tb, ft = rT.take()
            t = V.did(V.on(K["bb", b], *fe).tensor_tensor(eb[:, 0, :], cf(KF, g), ch(mm_, g, 1), ALU.subtract))
            tt = A.did(A.on(t, *ft).activation(tb[:, 0, :], eb[:, 0, :], ACT.Tanh, scale=0.5, bias=HU))
            V.did(V.on(t, *fr).tensor_scalar(buf[:, 0, :], eb[:, 0, :], 0.0, None, ALU.min))
            t = V.did(V.on(t).tensor_scalar(buf[:, 1, :], eb[:, 0, :], 0.0, -1.0, ALU.max, ALU.mult))
            t = A.did(A.on(t, tt).activation(eb, buf, ACT.Exp))
            rD.free(ib, t)
            K["e", g] = (ie, eb, t, it, tb, tt)

        def b_wkv(g):
            b, h = g // 2, g % 2
            o = 512 * h
            ie, eb, t, it, tb, tt = K["e", g]
            ib, buf, fr = rD.take()
            iy, yb, fy = rY.take()
            t = V.did(V.on(t, *fr).tensor_tensor(buf[:, 0, :], eb[:, 0, :], cf(VF, g), ALU.mult))
            t = V.did(V.on(t, t_aa0, *([K["aa", g - 1]] if h else [])).tensor_tensor_scan(
                ch(ss, g), eb[:, 1, :], buf[:, 0, :], ss[:, b, o:o + 1], ALU.mult, ALU.add))
            K["aa", g] = t
            rE.free(ie, t)
            t = V.did(V.on(t).tensor_tensor(buf[:, 1, :], cf(VF, g), ch(ss, g, 1), ALU.subtract))
            t = V.did(V.on(t, tt).scalar_tensor_tensor(buf[:, 0, :], tb[:, 0, :], 1.0, buf[:, 1, :], ALU.add, ALU.mult))
            rT.free(it, t)
            t = V.did(V.on(t).scalar_tensor_tensor(buf[:, 1, :], buf[:, 0, :], 0.5, ch(ss, g, 1), ALU.mult, ALU.add))
            t = V.did(V.on(t, *fy).scalar_tensor_tensor(yb[:, 0, :], cf(RF, g), 1.0, buf[:, 1, :], ALU.add, ALU.mult))
            rD.free(ib, t)
            K["y", g] = (iy, yb, t)

        def b_res(g):
            iy, yb, t = K["y", g]
            pi, p, fr = pT.take()
            t = transposes(p, lambda j: yb[:, 0, 128 * j:128 * j + 128], ident, t, *fr)
            rY.free(iy, t)
            xa = XA[:, 4 * g:4 * g + 4, :].rearrange("p i c -> p (i c)")
            t = V.did(V.on(t).scalar_tensor_tensor(xa, p, 0.5, xa, ALU.mult, ALU.add))
            pT.free(pi, t)
            K["st", g] = rstd(g, 0, 1e-5, stats(g, lambda i: XA[:, i, :], 0, t))

        def b_norm(g):
            ib, buf, fr = rHN.take()
            for j in range(4):
                i = 4 * g + j
                t = normed(i, 0, buf[:, 0, 128 * j:128 * j + 128], XA[:, i, :], K["st", g], *fr)
            K["hn", g] = (ib, buf, t)

        def b_turn(g):
            ib, buf, t = K["hn", g]
            pi, p, fr = pT.take()
            t = transposes(p, lambda j: buf[:, 0, 128 * j:128 * j + 128], ident, t, *fr)
            rHN.free(ib, t)
            t = V.did(V.on(t).tensor_scalar(ch(hf, g), p, LN2W, LN2B, ALU.mult, ALU.add))
            pT.free(pi, t)
            if g % 2:
                b = g // 2
                t = V.did(V.on(t).tensor_copy(hf[:, b, 0:1], hf[:, b, 1024:1025]))
            K["hf", g] = t

        def b_mix(g):
            ib, buf, fr = rD.take()
            t = V.did(V.on(K["hf", g | 1], *fr).tensor_tensor(buf[:, 0, :], ch(hf, g, 1), ch(hf, g), ALU.subtract))
            t = V.did(V.on(t).scalar_tensor_tensor(cf(XXX, g), buf[:, 0, :], TS, ch(hf, g), ALU.mult, ALU.add))
            rD.free(ib, t)
            K["xxx", g] = t

        def b_kc(g):
            o = (g % 2) * 2048
            rl = B[KF][:, o:o + 2048]
            sq = B[VF][:, o:o + 2048]
            for c in range(4):
                pi, p, fr = pP.take()
                t = PE.did(PE.on(K["xxx", g], *fr).matmul(p, wck[:, c, :], cf(XXX, g), start=True, stop=True))
                t = A.did(A.on(t, K["aa", NG - 1], *K.get(("sqd", g - 2), ())).activation(
                    rl[:, 512 * c:512 * c + 512], p, ACT.Relu))
                pP.free(pi, t)
                t = G.did(G.on(t, K["y", NG - 1][2], *K.get(("vvd", g - 2), ())).tensor_tensor(
                    sq[:, 512 * c:512 * c + 512], rl[:, 512 * c:512 * c + 512], rl[:, 512 * c:512 * c + 512], ALU.mult))
                K["sq", g, c] = t
            K["sqd", g] = (t,)
            pi, p, fr = pP.take()
            t = PE.did(PE.on(*fr).matmul(p, wA[:, 3, :], cf(XXX, g), start=True, stop=True))
            it, tb, ft = rT.take()
            t = A.did(A.on(t, *ft).activation(tb[:, 0, :], p, ACT.Tanh, scale=0.5))
            pP.free(pi, t)
            K["rc", g] = (it, tb, t)

        def b_vv(g):
            o = (g % 2) * 2048
            sq = B[VF][:, o:o + 2048]
            pi, p, fr = pP.take()
            for c in range(4):
                t = PE.did(PE.on(K["sq", g, c], *fr).matmul(p, wcv[:, c, :], sq[:, 512 * c:512 * c + 512],
                                                            start=(c == 0), stop=(c == 3)))
            K["vvd", g] = (t,)
            it, tb, tt = K["rc", g]
            iy, yb, fy = rY.take()
            t = V.did(V.on(t, tt, *fy).scalar_tensor_tensor(yb[:, 0, :], tb[:, 0, :], 1.0, p, ALU.add, ALU.mult))
            pP.free(pi, t)
            rT.free(it, t)
            K["y", g] = (iy, yb, t)

        def b_ret(g):
            iy, yb, t = K["y", g]
            pi, p, fr = pT.take()
            t = transposes(p, lambda j: yb[:, 0, 128 * j:128 * j + 128], ident, t, *fr)
            rY.free(iy, t)
            xa = XA[:, 4 * g:4 * g + 4, :].rearrange("p i c -> p (i c)")
            t = V.did(V.on(t).scalar_tensor_tensor(xa, p, 0.5, xa, ALU.mult, ALU.add))
            pT.free(pi, t)
            K["st", g] = rstd(g, 1, 1e-5, stats(g, lambda i: XA[:, i, :], 1, t))

        rX = Ring([rb(14), rb(15)])

        def add_normed(g, k, src, *producers):
            ix, xb, fr = rX.take()
            for j in range(4):
                t = normed(4 * g + j, k, xb[:, 0, 128 * j:128 * j + 128], src(4 * g + j), *producers, *fr)
            ta = t
            x = X[:, 4 * g:4 * g + 4, :].rearrange("p i c -> p (i c)")
            t = G.did(G.on(t).tensor_tensor(x, x, xb[:, 0, :], ALU.add))
            rX.free(ix, t)
            K["x", g] = t
            return ta

        def b_add(g):
            add_normed(g, 1, lambda i: XA[:, i, :], K["st", g])

        skewed([(0, b_decay), (1, b_wkv), (2, b_res), (3, b_norm), (4, b_turn)], NG)
        s_wm = sem("s_wm")
        for i, name in enumerate(("w1", "w3", "w2")):
            dma(B[4][:, 1152 * i:1152 * i + 1152], I[name], s_wm, K["y", NG - 1][2])
        dma(B[4][0:96, 3456:3968].bitcast(BF), I["sel"], s_wm)
        T_WM = (s_wm, 64)
        skewed([(0, b_mix), (1, b_kc), (2, b_vv), (3, b_ret), (4, b_add)], NG)
        barrier()

        def finish():
            s_o = [sem("s_o") for _ in range(NG)]
            oo = out.rearrange("(i p) c -> p i c", p=128)
            for g in range(NG):
                dma(oo[:, 4 * g:4 * g + 4, :], X[:, 4 * g:4 * g + 4, :], s_o[g], K["x", g])
            for g in range(NG):
                SP.on((s_o[g], 16))

        if stop == 1:
            finish()
            return

        XF = 0
        t_ww = dma(WW[:, :, :], I["wL1"], sem("s_ww"))
        rHN = Ring([rb(0), rb(1)])
        pT = Ring([bank(0), bank(1)])

        def n_stats(g):
            K["st", g] = rstd(g, 0, 1e-5, stats(g, lambda i: X[:, i, :], 0, K["x", g]))

        def n_norm(g):
            ib, buf, fr = rHN.take()
            for j in range(4):
                i = 4 * g + j
                t = normed(i, 0, buf[:, 0, 128 * j:128 * j + 128], X[:, i, :], K["st", g], *fr)
            K["hn", g] = (ib, buf, t)

        def n_turn(g):
            ib, buf, t = K["hn", g]
            pi, p, fr = pT.take()
            t = transposes(p, lambda j: buf[:, 0, 128 * j:128 * j + 128], ident, t, *fr)
            rHN.free(ib, t)
            t = A.did(A.on(t).activation(cf(XF, g), p, ACT.Copy))
            pT.free(pi, t)
            K["xf", g] = t

        SC = sb("SC", [128, NT, 16])
        small = [B[3][:, 512 * i:512 * i + 512].rearrange("p (i e) -> p i e", e=16) for i in range(4)]
        sv = B[3][:, 2048:3584].rearrange("p (n i q) -> p n i q", i=NT, q=4)
        T8 = B[3][:, 3584:3840].rearrange("p (i e) -> p i e", e=8)
        C3 = B[2][:, 0:1536].bitcast(BF).rearrange("p (i a e) -> p i a e", a=3, e=32)
        CFb = B[1][0:96, 0:2048].bitcast(BF)
        wm = [B[4][:, 1152 * i:1152 * i + 1152].rearrange("p (j c) -> p j c", c=128) for i in range(3)]
        w1, w3, w2 = wm
        sel = B[4][0:96, 3456:3968].bitcast(BF).rearrange("p (j c) -> p j c", c=128)
        t_c3 = G.did(G.on().memset(C3[:, :, :, :].rearrange("p i a e -> p (i a e)"), 0.0))

        def n_gate(g):
            for j in range(4):
                t = PE.did(PE.on(K["xf", g]).matmul(bank(2)[:, 16 * (4 * g + j):16 * (4 * g + j) + 16],
                                                    cf(XF, g)[:, 128 * j:128 * j + 128], gate0[:, :],
                                                    start=True, stop=True, skip_group_check=True))
            K["lg", g] = t

        skewed([(0, n_stats), (1, n_norm), (2, n_turn), (3, n_gate)], NG)
        t = A.did(A.on(K["lg", NG - 1]).activation(SC[:, :, :].rearrange("p i e -> p (i e)"), bank(2), ACT.Sigmoid))
        t_sc = t

        def vt(o, a, b, op, *w):
            return V.did(V.on(*w).tensor_tensor(o, a, b, op))

        def pick(S, th, k, E, reset, tmp, t):
            f = lambda z: z.rearrange("p i e -> p (i e)")
            thb = th.to_broadcast([128, NT, E])
            gt, eq, pc = tmp
            t = vt(gt, S, thb, ALU.is_gt, t)
            t = V.did(V.on(t).tensor_reduce(sv[:, 10, :, 0:1].rearrange("p i a -> p (i a)"), gt, AX, ALU.add))
            need = sv[:, 11, :, 0:1]
            t = V.did(V.on(t).tensor_scalar(need, sv[:, 10, :, 0:1], -1.0, float(k), ALU.mult, ALU.add))
            t2 = vt(eq, S, thb, ALU.is_equal, t)
            t = V.did(V.on(t2).tensor_tensor_scan(f(pc), reset[:, :], f(eq), 0.0, ALU.mult, ALU.add))
            t = vt(pc, pc, need.to_broadcast([128, NT, E]), ALU.is_le, t)
            t = vt(eq, eq, pc, ALU.mult, t)
            return vt(gt, gt, eq, ALU.add, t)

        sp = SC[:, :, :].rearrange("p i (q a b) -> p (i q) a b", a=2, b=2)
        pr = small[0][:, :, :].rearrange("p i e -> p (i e)")
        hi = pr[:, 0:256].rearrange("p (n a) -> p n a", a=2)
        lo = pr[:, 256:512].rearrange("p (n a) -> p n a", a=2)
        svf = lambda n: sv[:, n, :, :].rearrange("p i q -> p (i q)")
        vt(hi, sp[:, :, :, 0], sp[:, :, :, 1], ALU.max, t_sc)
        t = vt(lo, sp[:, :, :, 0], sp[:, :, :, 1], ALU.min, t_sc)
        vt(svf(0), hi[:, :, 0], hi[:, :, 1], ALU.max, t)
        vt(svf(1), hi[:, :, 0], hi[:, :, 1], ALU.min, t)
        t = vt(svf(2), lo[:, :, 0], lo[:, :, 1], ALU.max, t)
        t = vt(svf(3), svf(1), svf(2), ALU.max, t)
        t = vt(svf(4), svf(0), svf(3), ALU.add, t)
        gs = sv[:, 4, :, :]
        for d in (1, 2, 3):
            t = vt(sv[:, 4 + d, :, 0:4 - d], gs[:, :, 0:4 - d], gs[:, :, d:4], ALU.is_ge, t)
        cnt = sv[:, 8, :, :]
        t = V.did(V.on(t).tensor_copy(cnt, rk0[:, :, :]))
        for d in (1, 2, 3):
            t = vt(sv[:, 8, :, d:4], sv[:, 8, :, d:4], sv[:, 4 + d, :, 0:4 - d], ALU.add, t)
            t = vt(sv[:, 8, :, 0:4 - d], sv[:, 8, :, 0:4 - d], sv[:, 4 + d, :, 0:4 - d], ALU.subtract, t)
        t = V.did(V.on(t).tensor_scalar(svf(9), svf(8), 2.0, None, ALU.is_lt))
        t = V.did(V.on(t).tensor_scalar(svf(0), svf(9), -1.0, None, ALU.add))
        four = lambda z: z.rearrange("p i (q e) -> p (i q) e", e=4)
        bc4 = lambda n: svf(n).unsqueeze(2).to_broadcast([128, NT * 4, 4])
        t = vt(four(small[1][:, :, :]), four(SC[:, :, :]), bc4(9), ALU.mult, t)
        t = vt(four(small[1][:, :, :]), four(small[1][:, :, :]), bc4(0), ALU.add, t)
        for i in range(NT):
            tm8 = V.did(V.on(t).max(T8[:, i, :], small[1][:, i, :]))
        t = pick(small[1][:, :, :], T8[:, :, 3:4], 4, 16, rst16,
                 (small[0][:, :, :], small[2][:, :, :], small[3][:, :, :]), tm8)
        t = vt(small[2][:, :, :], small[0][:, :, :], SC[:, :, :], ALU.mult, t)
        wsum = sv[:, 0, :, 0:1]
        t = V.did(V.on(t).tensor_reduce(wsum.rearrange("p i a -> p (i a)"), small[2][:, :, :], AX, ALU.add))
        t = V.did(V.on(t).tensor_scalar(sv[:, 1, :, 0:1], wsum, 1e-6, None, ALU.add))
        t = V.did(V.on(t).reciprocal(sv[:, 2, :, 0:1], sv[:, 1, :, 0:1]))
        t = vt(small[1][:, :, :], small[2][:, :, :], sv[:, 2, :, 0:1].to_broadcast([128, NT, 16]), ALU.mult, t)
        t = V.did(V.on(t, t_c3).tensor_copy(C3[:, :, 0, 0:16], small[1][:, :, :]))
        t = vt(small[2][:, :, :], small[1][:, :, :], C3[:, :, 0, 0:16], ALU.subtract, t)
        t = V.did(V.on(t).tensor_copy(C3[:, :, 1, 0:16], small[2][:, :, :]))
        t = vt(small[3][:, :, :], small[2][:, :, :], C3[:, :, 1, 0:16], ALU.subtract, t)
        t = V.did(V.on(t).tensor_copy(C3[:, :, 2, 0:16], small[3][:, :, :]))
        t_c3 = t
        for g in range(NG):
            pi, p, fr = pT.take()
            pb = p.bitcast(BF)
            for j in range(4):
                i = 4 * g + j
                t = PE.did(PE.on(t_c3, *fr).transpose(pb[0:96, 128 * j:128 * j + 128],
                                                      C3[:, i, :, :].rearrange("p a e -> p (a e)"), identb[:, :]))
            t = V.did(V.on(t).tensor_copy(CFb[:, 512 * g:512 * g + 512], pb[0:96, 0:512]))
            pT.free(pi, t)
            K["cf", g] = t

        pG = Ring([bank(2), bank(3)])
        pG.freed = [(t_sc,), (t_sc,)]
        pU = Ring([bank(4), bank(5)])
        pC = Ring([bank(0), bank(1)])
        pC.freed = [(t,), (t,)]
        pO = Ring([bank(6), bank(7)])
        rS = Ring([rb(0), rb(1), rb(2)])
        rS.freed = [(PE.last(),)] * 3
        rT1 = Ring([rb(3), rb(4)])
        rT2 = Ring([rb(5), rb(6), rb(7)])

        def m_gu(n):
            g, j = divmod(n, 9)
            gi, pg, fr = pG.take()
            tg = PE.did(PE.on(T_WM, *fr).matmul(pg, w1[:, j, :], cf(XF, g), start=True, stop=True))
            ui, pu, fr = pU.take()
            tu = PE.did(PE.on(*fr).matmul(pu, w3[:, j, :], cf(XF, g), start=True, stop=True))
            si, sbuf, fr = rS.take()
            t = A.did(A.on(tg, *fr).activation(sbuf[:, 0, :], pg, ACT.Silu))
            pG.free(gi, t)
            if j < 8:
                ci, pc, fr = pC.take()
                tc = PE.did(PE.on(K["cf", g], *fr).matmul(pc, sel[:, j, :], CFb[:, 512 * g:512 * g + 512],
                                                          start=True, stop=True))
                i1, b1, f1 = rT1.take()
                t = V.did(V.on(t, tu, *f1).tensor_tensor(b1[:, 0, :], sbuf[:, 0, :], pu, ALU.mult))
                rS.free(si, t)
                pU.free(ui, t)
                i2, b2, f2 = rT2.take()
                t = V.did(V.on(t, tc, *f2).tensor_tensor(b2[:, 0, :], b1[:, 0, :], pc, ALU.mult))
                pC.free(ci, t)
            else:
                i2, b2, f2 = rT2.take()
                t = V.did(V.on(t, tu, *f2).tensor_tensor(b2[:, 0, :], sbuf[:, 0, :], pu, ALU.mult))
                rS.free(si, t)
                pU.free(ui, t)
            K["t2", n] = (i2, b2, t)

        def m_out(n):
            g, j = divmod(n, 9)
            if j == 0:
                K["o", g] = pO.take()
            oi, po, fr = K["o", g]
            i2, b2, t = K["t2", n]
            for q in range(4):
                tp = PE.did(PE.on(t, *(fr if j == 0 else ())).matmul(
                    po[:, 128 * q:128 * q + 128], b2[:, 0, 128 * q:128 * q + 128], w2[:, j, :],
                    start=(j == 0 and q == 0), stop=(j == 8), skip_group_check=True))
            rT2.free(i2, tp)
            if j == 8:
                ts_ = stats(g, lambda i: po[:, 128 * (i - 4 * g):128 * (i - 4 * g) + 128], 1, tp)
                t = rstd(g, 1, 1e-5, ts_)
                t = add_normed(g, 1, lambda i: po[:, 128 * (i - 4 * g):128 * (i - 4 * g) + 128], t)
                pO.free(oi, t)

        skewed([(0, m_gu), (2, m_out)], 9 * NG)
        barrier()
        if stop == 2:
            finish()
            return

        rHN = Ring([rb(0), rb(1)])
        pT = Ring([bank(0), bank(1)])
        pP = Ring([bank(i) for i in range(2, 8)])
        QF, KF, B0, B1, NUM = 1, 2, 3, 4, 5
        cs = SS[:, 0:2048].rearrange("p (a t) -> p a t", a=2)
        s_cs = sem("s_cs")
        t_cs = dma(cs, I["rope"], s_cs)
        for x in (PE,):
            x.on(t_ww)

        def d_norm(g):
            n_norm(g)
            ib, buf, t = K["hn", g]
            for j in range(4):
                t = G.did(G.on(t).tensor_tensor(XA[:, 4 * g + j, :], buf[:, 0, 128 * j:128 * j + 128],
                                                rows[:, 0, :], ALU.add))
            K["xb", g] = t

        def d_turn(g):
            n_turn(g)
            ib = K["hn", g][0]
            rHN.free(ib, PE.last(), K["xb", g])

        rq = Ring([rb(2, 4), rb(6, 4)])

        def d_proj(g):
            h = g % 2
            for w in range(2):
                iq, qb, fq = rq.take()
                pi, p, fr = pP.take()
                t = PE.did(PE.on(K["xf", g], *fr).matmul(p, wq4[:, 2 * w, :], cf(XF, g), start=True, stop=True))
                t1 = vt(qb[:, 0, :], p, cs[:, 0, 512 * h:512 * h + 512], ALU.mult, t, t_cs, *fq)
                pP.free(pi, t1)
                pi, p, fr = pP.take()
                t = PE.did(PE.on(*fr).matmul(p, wq4[:, 2 * w + 1, :], cf(XF, g), start=True, stop=True))
                t2 = vt(qb[:, 1, :], p, cs[:, 1, 512 * h:512 * h + 512], ALU.mult, t)
                pP.free(pi, t2)
                t = vt(qb[:, 2, :], qb[:, 0, :], qb[:, 1, :], ALU.add, t1, t2)
                A.did(A.on(t).activation(qb[:, 0, :], qb[:, 2, :], ACT.Exp))
                t = A.did(A.on(t).activation(qb[:, 3, :], qb[:, 2, :], ACT.Relu))
                t = V.did(V.on(t).scalar_tensor_tensor(cf((QF, KF)[w], g), qb[:, 0, :], 1.0, qb[:, 3, :],
                                                       ALU.min, ALU.add))
                rq.free(iq, t)
            for w in range(2):
                pi, p, fr = pP.take()
                t = PE.did(PE.on(*fr).matmul(p, wbr[:, w, :], cf(XF, g), start=True, stop=True))
                d = cf((B0, B1)[w], g)
                t = A.did(A.on(t).activation(d, p, ACT.Tanh, scale=0.5, bias=(HBB0, HBB1)[w]))
                pP.free(pi, t)
                t = V.did(V.on(t).tensor_scalar(d, d, 0.5, 0.5, ALU.mult, ALU.add))
                t = V.did(V.on(t).tensor_scalar(d, d, 0.001, 0.999, ALU.max, ALU.min))
            K["qk", g] = t

        skewed([(0, n_stats), (1, d_norm), (2, d_turn), (3, d_proj)], NG)

        num = full(NUM).rearrange("p (i h e) -> p i h e", h=16, e=8)
        DEN = SC
        ring2 = lambda a: Ring([rb(a, 2).rearrange("p a t -> p (a t)"), rb(a + 2, 2).rearrange("p a t -> p (a t)")])
        rO = Ring([rb(0, 2).rearrange("p a t -> p (a t)"), rb(2, 2).rearrange("p a t -> p (a t)")])
        rM0 = ring2(4)
        rM1 = ring2(8)
        rP = Ring([rb(12, 2).rearrange("p a t -> p (a t)"), rb(14, 2).rearrange("p a t -> p (a t)")])
        rQ = Ring([SS[:, 2048:3072], SS[:, 3072:4096]])
        pV = Ring([bank(4, 2), bank(6, 2)])
        pN = Ring([bank(0, 2), bank(2, 2)])
        barrier()

        def d_value(n):
            e, b = divmod(n, 4)
            if e == 8:
                return
            pi, p, fr = pV.take()
            for h in range(2):
                t = PE.did(PE.on(*fr).matmul(p[:, 512 * h:512 * h + 512], wvr[:, e, :],
                                             B[XF][:, 1024 * b + 512 * h:1024 * b + 512 * h + 512],
                                             start=True, stop=True))
            K["vr", n] = (pi, p, t)

        def d_outer(n):
            e, b = divmod(n, 4)
            c = slice(1024 * b, 1024 * b + 1024)
            if e < 8:
                pi, p, t = K["vr", n]
                io, ob, fo = rO.take()
                t = vt(ob, B[KF][:, c], p, ALU.mult, t, *fo)
                pV.free(pi, t)
            else:
                io, ob, t = None, B[KF][:, c], (V.sem, 0)
            i0, m0, f0 = rM0.take()
            i1, m1, f1 = rM1.take()
            V.did(V.on(t, *f0).tensor_tensor_scan(m0, B[B0][:, c], ob, 0.0, ALU.mult, ALU.add))
            t = V.did(V.on(t, *f1).tensor_tensor_scan(m1, B[B1][:, c], ob, 0.0, ALU.mult, ALU.add))
            if io is not None:
                rO.free(io, t)
            ip, pb, fp = rP.take()
            t = G.did(G.on(t, *fp).tensor_tensor(pb, m0, m1, ALU.add))
            rM0.free(i0, t)
            rM1.free(i1, t)
            K["sum", n] = (ip, pb, t)

        def d_query(n):
            e, b = divmod(n, 4)
            c = slice(1024 * b, 1024 * b + 1024)
            ip, pb, t = K["sum", n]
            iq, qb, fq = rQ.take()
            t = vt(qb, pb, B[QF][:, c], ALU.mult, t, *fq)
            rP.free(ip, t)
            pi, p, fr = pN.take()
            for q in range(8):
                tp = PE.did(PE.on(t, *fr).matmul(p[:, 128 * q:128 * q + 128], qb[:, 128 * q:128 * q + 128], hsum[:, :],
                                                 start=True, stop=True, skip_group_check=True))
            rQ.free(iq, tp)
            src = p.rearrange("p (i h) -> p i h", h=128)[:, :, 0:16]
            dst = num[:, 8 * b:8 * b + 8, :, e] if e < 8 else DEN[:, 8 * b:8 * b + 8, :]
            t = A.did(A.on(tp).activation(dst, src, ACT.Copy))
            pN.free(pi, t)
            K["num", n] = t

        skewed([(0, d_value), (1, d_outer), (3, d_query)], 36)
        barrier()
        t_we = dma(WW[:, 0:8, :], I["wE"], sem("s_we"))
        rHN = Ring([rb(0), rb(1)])
        pT = Ring([bank(0), bank(1)])
        pP = Ring([bank(i) for i in range(2, 8)])
        rYF = Ring([rb(2), rb(3)])
        rZ = Ring([rb(4), rb(5)])
        t = V.did(V.on().tensor_scalar(small[0][:, :, :], DEN[:, :, :], 1e-6, None, ALU.add))
        t_rd = V.did(V.on(t).reciprocal(small[1][:, :, :], small[0][:, :, :]))

        def f_div(g):
            s4 = slice(4 * g, 4 * g + 4)
            ib, buf, fr = rHN.take()
            o = buf[:, 0, :].rearrange("p (n e) -> p n e", e=8)
            a = num[:, s4, :, :].rearrange("p i h e -> p (i h) e")
            r = small[1][:, s4, :].rearrange("p i h -> p (i h)").unsqueeze(2).to_broadcast([128, 64, 8])
            t = vt(o, a, r, ALU.mult, t_rd, *fr)
            pi, p, fr = pT.take()
            t = transposes(p, lambda j: buf[:, 0, 128 * j:128 * j + 128], ident, t, *fr)
            rHN.free(ib, t)
            iy, yb, fy = rYF.take()
            t = A.did(A.on(t, *fy).activation(yb[:, 0, :], p, ACT.Copy))
            pT.free(pi, t)
            K["yf", g] = (iy, yb, t)

        def out_proj(g, w):
            iy, yb, t = K["yf", g]
            pi, p, fr = pP.take()
            for j in range(4):
                t = PE.did(PE.on(t, *fr).matmul(p[:, 128 * j:128 * j + 128], yb[:, 0, 128 * j:128 * j + 128], w[:, :],
                                                start=True, stop=True, skip_group_check=True))
            rYF.free(iy, t)
            xa = XA[:, 4 * g:4 * g + 4, :].rearrange("p i c -> p (i c)")
            t = vt(xa, xa, p, ALU.add, t)
            pP.free(pi, t)
            return t

        def f_out(g):
            t = out_proj(g, wo1)
            K["st", g] = rstd(g, 0, 1e-5, stats(g, lambda i: XA[:, i, :], 0, t))

        def f_aff(g):
            iz, zb, fz = rZ.take()
            for j in range(4):
                i = 4 * g + j
                z = zb[:, 0, 128 * j:128 * j + 128]
                t = normed(i, 0, z, XA[:, i, :], K["st", g], *fz)
                t = vt(z, z, rows[:, 1, :], ALU.mult, t)
                t = vt(XA[:, i, :], z, rows[:, 2, :], ALU.add, t)
            rZ.free(iz, t)
            K["st1", g] = rstd(g, 1, 1e-5, stats(g, lambda i: XA[:, i, :], 1, t))

        def f_add(g):
            add_normed(g, 1, lambda i: XA[:, i, :], K["st1", g])

        skewed([(0, f_div), (1, f_out), (2, f_aff), (3, f_add)], NG)
        barrier()
        if stop == 3:
            finish()
            return

        rHN = Ring([rb(0), rb(1)])
        pT = Ring([bank(0), bank(1)])
        pP = Ring([bank(i) for i in range(2, 8)])
        XF = 0
        scrQ = nc.dram_tensor("scrQ", [4, 3, 128, 1024], BF, kind="Internal").ap()
        scrK = nc.dram_tensor("scrK", [3, 32, T], BF, kind="Internal").ap()
        scrM = nc.dram_tensor("scrM", [8, 24, 1024], BF, kind="Internal").ap()
        qs = [B[i][0:96, 0:4096].bitcast(BF).rearrange("p (h t) -> p h t", h=8) for i in (1, 5, 3)]
        kst = [B[2][0:96, 2048 * i:2048 * i + 2048].bitcast(BF).rearrange("p (k t) -> p k t", k=4) for i in range(2)]
        VA = B[4][:, 0:4096].rearrange("p (i k e) -> p i k e", k=4, e=32)
        t_va = V.did(V.on().memset(B[4][:, 0:4096], 0.0))
        t_va = V.did(V.on(t_va).memset(VA[:, :, :, 8:9].rearrange("p i k e -> p (i k) e"), 1.0))
        for z in qs:
                t_q0 = V.did(V.on().memset(z.rearrange("p h t -> p (h t)"), 0.0))
        for z in kst:
            t_k1 = G.did(G.on().memset(z.rearrange("p k t -> p (k t)"), 1.0))
        parts = lambda a, np_: RB[0:np_, :, :].rearrange("p n t -> p (n t)")[:, 768 * a:768 * a + 768].bitcast(
            BF).rearrange("p (a t) -> p a t", a=3)
        base = 10 * 512 // 256
        rB = [RB[:, :, :].rearrange("p n t -> p (n t)")[:, 5120 + 768 * i:5888 + 768 * i].bitcast(BF).rearrange(
            "p (a t) -> p a t", a=3) for i in range(2)]
        rKb = [RB[0:32, :, :].rearrange("p n t -> p (n t)")[:, 6656 + 768 * i:7424 + 768 * i].bitcast(BF).rearrange(
            "p (a t) -> p a t", a=3) for i in range(2)]
        rBq, rBk = Ring([z for z in rB]), Ring([z for z in rKb])
        rR = Ring([rb(2, 4), rb(6, 4)])

        def e_stats(g):
            K["st", g] = rstd(g, 0, 1e-5, stats(g, lambda i: X[:, i, :], 0, K["x", g]), then=1e-6)

        def e_norm(g):
            ib, buf, fr = rHN.take()
            for j in range(4):
                i = 4 * g + j
                t = V.did(V.on(K["st", g]).tensor_scalar(XA[:, i, :], X[:, i, :], mv[0][:, i, 0:1],
                                                         rs[0][:, i, 0:1], ALU.subtract, ALU.mult))
                t = A.did(A.on(t, *fr).activation(buf[:, 0, 128 * j:128 * j + 128], XA[:, i, :], ACT.Copy,
                                                  scale=rs[0][:, i, 2:3]))
            K["hn", g] = (ib, buf, t)

        def turn_scaled(g, col):
            ib, buf, t = K["hn", g]
            pi, p, fr = pT.take()
            t = transposes(p, lambda j: buf[:, 0, 128 * j:128 * j + 128], ident, t, *fr)
            rHN.free(ib, t)
            t = A.did(A.on(t).activation(cf(XF, g), p, ACT.Copy, scale=col))
            pT.free(pi, t)
            K["xf", g] = t

        def e_turn(g):
            turn_scaled(g, ANW)

        def split3(ring, p, np_, scale, t, out_dma, g):
            ir, r, fr = rR.take()
            ib, o, fo = ring.take()
            P_ = slice(0, np_)
            t = A.did(A.on(t, *fr).activation(r[P_, 0, :], p, ACT.Copy, scale=scale))
            tp = t
            t = V.did(V.on(t, *fo).tensor_copy(o[P_, 0, :], r[P_, 0, :]))
            t = vt(r[P_, 1, :], r[P_, 0, :], o[P_, 0, :], ALU.subtract, t)
            t = V.did(V.on(t).tensor_copy(o[P_, 1, :], r[P_, 1, :]))
            t = vt(r[P_, 2, :], r[P_, 1, :], o[P_, 1, :], ALU.subtract, t)
            t = V.did(V.on(t).tensor_copy(o[P_, 2, :], r[P_, 2, :]))
            rR.free(ir, t)
            td = out_dma(o, t)
            ring.free(ib, td)
            return tp, td

        def e_proj(g):
            b, h = g // 2, g % 2
            c = slice(512 * h, 512 * h + 512)
            pi, p, fr = pP.take()
            t = PE.did(PE.on(K["xf", g], *fr).matmul(p, wqE[:, :], cf(XF, g), start=True, stop=True))
            tp, K["dq", g] = split3(rBq, p, 128, 8.0 ** -0.5, t, lambda o, t: dma(
                scrQ[b, :, :, c].rearrange("a p t -> p a t"), o[:, :, :], sem("s_sq"), t), g)
            pP.free(pi, tp)
            pi, p, fr = pP.take()
            t = PE.did(PE.on(*fr).matmul(p[0:32, :], wkE[:, :], cf(XF, g), start=True, stop=True))
            tp, K["dk", g] = split3(rBk, p[0:32, :], 32, 1.0, t, lambda o, t: dma(
                scrK[:, :, 512 * g:512 * g + 512].rearrange("a p t -> p a t"), o[:, :, :], sem("s_sk"), t), g)
            pP.free(pi, tp)
            pi, p, fr = pP.take()
            for j in range(4):
                t = PE.did(PE.on(*fr).matmul(p[:, 32 * j:32 * j + 32], cf(XF, g)[:, 128 * j:128 * j + 128], wvE[:, :],
                                             start=True, stop=True, skip_group_check=True))
            for j in range(4):
                t2 = A.did(A.on(t, t_va).activation(VA[:, 4 * g + j, :, 0:8],
                                                    p[:, 32 * j:32 * j + 32].rearrange("p (k e) -> p k e", e=8),
                                                    ACT.Copy))
            pP.free(pi, t2)
            K["v", g] = t2

        skewed([(0, e_stats), (1, e_norm), (2, e_turn), (3, e_proj)], NG)

        def load_k(b, *producers):
            s_ks = sem("s_ks")
            for a in range(3):
                for c in range(3):
                    SP.on(t_k1, K["dk", 2 * b], K["dk", 2 * b + 1], *producers).dma_start(
                        kst[b % 2][32 * a + 8 * c:32 * a + 8 * c + 8, :, :],
                        scrK[c, :, 1024 * b:1024 * b + 1024].rearrange("(k d) t -> d k t", d=8)).then_inc(s_ks, 16)
            K["k", b] = (s_ks, 144)

        def load_q(u, *producers):
            s, n, b, hh = sem("s_q"), 0, u // 2, u % 2
            for a in range(3):
                for c in range(3):
                    SP.on(t_q0, K["dq", 2 * b], K["dq", 2 * b + 1], *producers).dma_start(
                        qs[u % 3][32 * a + 8 * c:32 * a + 8 * c + 8, :, :],
                        scrQ[b, a, 64 * hh:64 * hh + 64, :].rearrange("(h d) t -> d h t", d=8)).then_inc(s, 16)
                    n += 16
            if u >= 3:
                SP.eng.dma_start(qs[u % 3][24:27, :, :], I["zrow"]).then_inc(s, 16)
                n += 16
            K["q", u] = (s, n)

        MX = SS[:, 0:256].rearrange("p (r i h c) -> p r i h c", r=2, i=8, c=2)
        NM = SS[:, 256:640].rearrange("p (r a n) -> p r a n", r=2, a=3)
        M3 = SS[:, 640:832].bitcast(BF).rearrange("p (r i n) -> p r i n", r=2, i=8)
        RC = SS[:, 832:896].rearrange("p (r n) -> p r n", r=4)
        MF = SS[0:24, 1024:2048].bitcast(BF).rearrange("p (r t) -> p r t", r=2)
        p1 = Ring([bank(4), bank(5)])
        pS2 = Ring([bank(0, 2), bank(2, 2)])
        pOE = Ring([bank(6)])
        pX = Ring([bank(7)])
        barrier()

        def head(u, h):
            b, hh = u // 2, u % 2
            return qs[u % 3][:, h, :], kst[b % 2][:, 2 * hh + h // 4, :]

        def pass1(u):
            mx = MX[:, u % 2, :, :, :]
            for h in range(8):
                Q, Kk = head(u, h)
                for i in range(8):
                    for c in range(i // 4 + 1):
                        pi, p, fr = p1.take()
                        n = 512 if c < i // 4 else 128 * (i % 4 + 1)
                        dg = c == i // 4
                        t = PE.did(PE.on(K["q", u], K["k", u // 2], *fr).matmul(
                            p[:, 0:n], Q[:, 128 * i:128 * i + 128], Kk[:, 512 * c:512 * c + n],
                            start=True, stop=not dg))
                        if dg:
                            t = PE.did(PE.on().matmul(p[:, n - 128:n], identb[:, :], msk[:, 0, :],
                                                      start=False, stop=True))
                        t = V.did(V.on(t).tensor_reduce(mx[:, i, h, c:c + 1], p[:, 0:n], AX, ALU.max))
                        p1.free(pi, t)
                    yield
            nm = NM[:, u % 2, :, :]
            v = lambda a: nm[:, a, :].rearrange("p (i h) -> p i h", h=8)
            m3 = M3[:, u % 2, :, :].rearrange("p i (a h) -> p i a h", a=3)
            t = V.did(V.on(t).tensor_scalar(v(0)[:, 0:4, :], mx[:, 0:4, :, 0], -1.0, None, ALU.mult))
            t = vt(v(1)[:, 4:8, :], mx[:, 4:8, :, 0], mx[:, 4:8, :, 1], ALU.max, t)
            t = V.did(V.on(t).tensor_scalar(v(0)[:, 4:8, :], v(1)[:, 4:8, :], -1.0, None, ALU.mult))
            t = V.did(V.on(t).tensor_copy(m3[:, :, 0, :], v(0)))
            t = vt(v(1), v(0), m3[:, :, 0, :], ALU.subtract, t)
            t = V.did(V.on(t).tensor_copy(m3[:, :, 1, :], v(1)))
            t = vt(v(2), v(1), m3[:, :, 1, :], ALU.subtract, t)
            t = V.did(V.on(t).tensor_copy(m3[:, :, 2, :], v(2)))
            yield
            pi, p, fr = pX.take()
            pb = p.bitcast(BF)
            for i in range(8):
                tp = PE.did(PE.on(t, *fr).transpose(pb[0:24, 128 * i:128 * i + 128], M3[:, u % 2, i, :], identb[:, :]))
            t = V.did(V.on(tp, *K.get(("md", u - 2), ())).tensor_copy(MF[:, u % 2, :], pb[0:24, 0:1024]))
            pX.free(pi, t)
            td = dma(scrM[u, :, :], MF[:, u % 2, :], sem("s_sm"), t)
            K["md", u] = (td,)
            K["m", u] = dma(qs[u % 3][24:27, :, :], scrM[u, :, :].rearrange("(a h) t -> a h t", h=8),
                            sem("s_m"), td, tp)
            yield

        rP4 = Ring([rb(0, 4), rb(4, 4), rb(8, 4)])
        rOS = Ring([rb(12), rb(13)])
        AT = XF

        def normalise(u, kl, qc, oi, po, tp):
            b, kv = u // 2, 2 * (u % 2) + kl
            io, ob, fr = rOS.take()
            t = V.did(V.on(tp, *fr).tensor_copy(ob[:, 0, :], po))
            pOE.free(oi, t)
            yield
            pi, p, fr = pX.take()
            t = transposes(p, lambda j: ob[:, 0, 128 * j:128 * j + 128], ident, t, *fr)
            rOS.free(io, t)
            yield
            p3 = p.rearrange("p (n e) -> p n e", e=32)
            rc = RC[:, (2 * kl + qc), :].unsqueeze(2)
            t = V.did(V.on(t).reciprocal(rc, p3[:, :, 8:9]))
            dst = B[AT][:, 1024 * b + 512 * qc:1024 * b + 512 * qc + 512].rearrange(
                "p (i k j e) -> p k i j e", i=4, k=4, j=4)[:, kv, :, :, :]
            for i in range(4):
                t2 = vt(dst[:, i, :, :], p3[:, 4 * i:4 * i + 4, 0:8],
                        rc[:, 4 * i:4 * i + 4, :].to_broadcast([128, 4, 8]), ALU.mult, t)
            pX.free(pi, t2)
            yield

        trailing = []

        def trail():
            for z in list(trailing):
                if next(z, "end") == "end":
                    trailing.remove(z)

        def pass2(u):
            b, hh = u // 2, u % 2
            if u == 0:
                for x in (A, V):
                    x.on(*[K["dq", g] for g in range(NG)], *[K["dk", g] for g in range(NG)])
            for kl in range(2):
                kv = 2 * hh + kl
                for qc in range(2):
                    oi, po, fo = pOE.take()
                    pend = None
                    nk = 4 * qc + 4
                    for kt in range(nk + 1):
                        cur = None
                        if kt < nk:
                            off = max(0, 128 * (kt - 4 * qc))
                            n = 512 - off
                            ip, pb, fp = rP4.take()
                            for hp in range(2):
                                si, ps, fr = pS2.take()
                                for z in range(2):
                                    Q, Kk = head(u, 4 * kl + 2 * hp + z)
                                    dg = kt >= 4 * qc
                                    o = 512 * z
                                    t = PE.did(PE.on(K["m", u], *fr).matmul(
                                        ps[:, o:o + n], Kk[:, 128 * kt:128 * kt + 128],
                                        Q[:, 512 * qc + off:512 * qc + 512], start=True, stop=not dg))
                                    if dg:
                                        t = PE.did(PE.on().matmul(ps[:, o:o + 128], identb[:, :], msk[:, 1, :],
                                                                  start=False, stop=True))
                                t = A.did(A.on(t, *fp).activation(
                                    pb[:, 2 * hp:2 * hp + 2, 0:n],
                                    ps.rearrange("p (a t) -> p a t", a=2)[:, :, 0:n], ACT.Exp))
                                pS2.free(si, t)
                            cur = (ip, pb, t, off, n, kt)
                        yield
                        trail()
                        if pend is not None:
                            ip, pb, t, off, n, k0 = pend
                            if k0 == 0:
                                fo = pOE.freed[oi]
                            for j in range(4):
                                tp = PE.did(PE.on(t, *fo).matmul(
                                    po[32 * j:32 * j + 32, off:off + n], VA[:, 8 * b + k0, kv, :], pb[:, j, 0:n],
                                    start=(k0 == 0), stop=(k0 == nk - 1), skip_group_check=True))
                            rP4.free(ip, tp)
                        pend = cur
                        yield
                    trailing.append(normalise(u, kl, qc, oi, po, tp))
            K["p2", u] = PE.last()
            if u + 3 < 8:
                load_q(u + 3, K["p2", u])
            if hh == 1 and b + 2 < 4:
                load_k(b + 2, K["p2", u])

        for u in range(3):
            if u % 2 == 0:
                load_k(u // 2)
            load_q(u)
        first = (z for u in range(8) for z in pass1(u))
        second = (z for u in range(8) for z in pass2(u))
        n1, n2, ahead = 8 * 66, 8 * 2 * (5 + 9 + 5 + 9), 66 + 8
        for _ in range(ahead):
            next(first, None)
        done1 = ahead
        for i in range(n2):
            next(second, None)
            while done1 < n1 and (done1 - ahead) * n2 < (i + 1) * n1:
                next(first, None)
                done1 += 1
        for _ in first:
            pass
        for _ in second:
            pass
        while trailing:
            trail()
        barrier()

        rHN = Ring([rb(0), rb(1)])
        pT = Ring([bank(0), bank(1)])
        pP = Ring([bank(i) for i in range(2, 7)])
        rYF = Ring([rb(2), rb(3)])
        HB = 1
        PE.on(t_we)
        LG = B[2][:, 0:256].rearrange("p (i e) -> p i e", e=8)

        def g_turn(g):
            pi, p, fr = pT.take()
            t = transposes(p, lambda j: cf(AT, g)[:, 128 * j:128 * j + 128], ident, *fr)
            iy, yb, fy = rYF.take()
            t = A.did(A.on(t, *fy).activation(yb[:, 0, :], p, ACT.Copy))
            pT.free(pi, t)
            K["yf", g] = (iy, yb, t)

        def g_out(g):
            t = out_proj(g, woE)
            t = stats(g, lambda i: XA[:, i, :], 0, t)
            s4 = slice(4 * g, 4 * g + 4)
            R = rs[0]
            t = G.did(G.on(t).tensor_tensor(R[:, s4, 3], mv[0][:, s4, 0], mv[0][:, s4, 0], ALU.mult))
            t = G.did(G.on(t).tensor_tensor(R[:, s4, 4], R[:, s4, 3], mv[0][:, s4, 1], ALU.add))
            t = G.did(G.on(t).tensor_scalar(R[:, s4, 5], R[:, s4, 4], 1e-6, None, ALU.add))
            K["st", g] = G.did(G.on(t).tensor_tensor(R[:, s4, 0], R[:, s4, 5], mhalf[:, 0:4], ALU.pow))

        def g_norm(g):
            ib, buf, fr = rHN.take()
            for j in range(4):
                i = 4 * g + j
                t = A.did(A.on(K["st", g], *fr).activation(buf[:, 0, 128 * j:128 * j + 128], XA[:, i, :], ACT.Copy,
                                                           scale=rs[0][:, i, 0:1]))
            K["hn", g] = (ib, buf, t)

        def g_hf(g):
            ib, buf, t = K["hn", g]
            pi, p, fr = pT.take()
            t = transposes(p, lambda j: buf[:, 0, 128 * j:128 * j + 128], ident, t, *fr)
            rHN.free(ib, t)
            t = A.did(A.on(t).activation(cf(HB, g), p, ACT.Copy, scale=FNW))
            pT.free(pi, t)
            K["xf", g] = t

        def g_gate(g):
            for j in range(4):
                t = PE.did(PE.on(K["xf", g]).matmul(bank(7)[:, 8 * (4 * g + j):8 * (4 * g + j) + 8],
                                                    cf(HB, g)[:, 128 * j:128 * j + 128], gateE[:, :],
                                                    start=True, stop=True, skip_group_check=True))
            K["lg", g] = t

        skewed([(0, g_turn), (1, g_out), (2, g_norm), (3, g_hf), (4, g_gate)], NG)
        t = V.did(V.on(K["lg", NG - 1]).tensor_copy(LG[:, :, :].rearrange("p i e -> p (i e)"), bank(7)[:, 0:256]))
        s8 = [small[q][:, :, :].rearrange("p i e -> p (i e)")[:, 0:256].rearrange("p (i e) -> p i e", e=8)
              for q in range(4)]
        t_lg = t
        for i in range(NT):
            t = V.did(V.on(t_lg).max(T8[:, i, :], LG[:, i, :]))
        t_m = t
        bc8 = lambda z: z.to_broadcast([128, NT, 8])
        tx = vt(s8[3], LG[:, :, :], bc8(T8[:, :, 0:1]), ALU.subtract, t_m)
        ty = vt(sv[:, 0, :, 0:1], T8[:, :, 1:2], T8[:, :, 0:1], ALU.subtract, t_m)
        comb = B[2][:, 256:512].rearrange("p (i e) -> p i e", e=8)
        tx = A.did(A.on(tx).activation(comb[:, :, :], s8[3], ACT.Exp))
        ty = A.did(A.on(ty).activation(sv[:, 1, :, 0:1], sv[:, 0, :, 0:1], ACT.Exp))
        t = pick(LG[:, :, :], T8[:, :, 1:2], 2, 8, rst8, (s8[0], s8[1], s8[2]), t_m)
        t = V.did(V.on(t, ty).tensor_scalar(sv[:, 2, :, 0:1], sv[:, 1, :, 0:1], 1.0, None, ALU.add))
        t = V.did(V.on(t).reciprocal(sv[:, 3, :, 0:1], sv[:, 2, :, 0:1]))
        t = vt(s8[1], s8[0], comb[:, :, :], ALU.mult, t, tx)
        t_cb = vt(comb[:, :, :], s8[1], bc8(sv[:, 3, :, 0:1]), ALU.mult, t)

        def h_exp(i):
            g, j = divmod(i, 4)
            x = XA[:, i, :]
            t = t_cb
            for half in range(2):
                pi, p, fr = pP.take()
                tp = PE.did(PE.on(*fr).matmul(p, cf(HB, g)[:, 128 * j:128 * j + 128],
                                              wE[:, 4 * half:4 * half + 4, :].rearrange("p e c -> p (e c)"),
                                              start=True, stop=True))
                for q in range(4):
                    e = 4 * half + q
                    t = V.did(V.on(t, tp).scalar_tensor_tensor(x, p[:, 128 * q:128 * q + 128], comb[:, i, e:e + 1], x,
                                                               ALU.mult, ALU.add))
                pP.free(pi, t)
            if j == 3:
                K["st1", g] = rstd(g, 1, 1e-5, stats(g, lambda i: XA[:, i, :], 1, t))

        def h_fin(i):
            g, j = divmod(i, 4)
            if j == 3:
                add_normed(g, 1, lambda i: XA[:, i, :], K["st1", g])

        skewed([(0, h_exp), (2, h_fin)], NT)
        finish()


def arrays(inputs):
    import numpy as np

    bf = mybir.dt.np(BF)
    a = {k: np.asarray(v) for k, v in inputs.items()}
    L = lambda n: a["L0_attn_" + n]
    M = lambda n: a["L0_ffn_" + n]
    N = lambda n: a["L1_attn_" + n]
    E = lambda n: a["L1_ffn_" + n]
    D = {"x": L("x").reshape(4096, 128)}
    eye = np.eye(128, dtype=np.float32)
    D["ident"], D["identb"] = eye, eye.astype(bf)
    z = np.zeros(128, np.float32)
    rep = lambda v: np.repeat(v, 8)
    bb = N("bbeta").reshape(16, 2)
    cols = [L("ln1_w"), L("ln1_b"), L("ln2_w"), L("ln2_b"), L("time_shift").reshape(128), L("time_first"),
            rep(bb[:, 0]), rep(bb[:, 1]), E("attn_norm_w"), E("ffn_norm_w")] + [z] * 6
    D["vecs"] = np.stack(cols, axis=1)
    stack = lambda ws: np.stack(ws, axis=1)
    wck = L("Wck").T.reshape(128, 4, 128)
    wcv = L("Wcv").T.reshape(4, 128, 128).transpose(1, 0, 2)
    D["wL0"] = np.concatenate([stack([L("Wk").T, L("Wv").T, L("Wr").T, L("Wcr").T]), wck, wcv], axis=1)
    D["gate0"] = M("w_gate").T
    w1 = np.concatenate([M("w1_e").reshape(1024, 128), M("w1_s")]).T
    w3 = np.concatenate([M("w3_e").reshape(1024, 128), M("w3_s")]).T
    w2 = np.concatenate([M("w2_e").transpose(0, 2, 1).reshape(1024, 128), M("w2_s").T])
    D["w1"], D["w3"] = w1, w3
    D["w2"] = w2.reshape(9, 128, 128).transpose(1, 0, 2).reshape(128, 1152)
    sel = np.zeros((96, 8, 128), np.float32)
    for p in range(3):
        for e in range(16):
            sel[32 * p + e, e // 2, 64 * (e % 2):64 * (e % 2) + 64] = 1
    D["sel"] = sel.reshape(96, 1024).astype(bf)
    r = np.ones((128, 32, 16), np.float32)
    r[:, :, 0] = 0
    D["rst16"] = r.reshape(128, 512)
    D["rst8"] = r[:, :, :8].reshape(128, 256)
    D["rk0"] = np.broadcast_to(np.array([3, 2, 1, 0], np.float32), (128, 32, 4))
    perm = np.arange(128).reshape(16, 2, 4)[:, ::-1, :].reshape(128)
    wv = N("Wv").reshape(128, 16, 8)
    wvr = [np.repeat(wv[:, :, e], 8, axis=1) for e in range(8)]
    wb = N("Wbeta").reshape(128, 16, 2)
    wbr = [np.repeat(wb[:, :, c], 8, axis=1) for c in range(2)]
    D["wL1"] = stack([N("Wq"), N("Wq")[:, perm], N("Wk"), N("Wk")[:, perm]] + wvr + wbr)
    D["wo1"] = N("Wo")
    D["hsum"] = np.repeat(np.eye(16, 128, dtype=np.float32), 8, axis=0)
    D["rows"] = np.stack([np.broadcast_to(v, (128, 128)) for v in (N("bo"), N("ln_gamma"), N("ln_beta"))], axis=1)
    inv = (1.0 / 10000.0 ** (np.arange(0, 8, 2, dtype=np.float32) / np.float32(8))).astype(np.float32)
    fr = (np.arange(1024, dtype=np.float32)[:, None] * inv[None, :]).astype(np.float32)
    c, s = np.cos(fr).T, np.sin(fr).T
    D["rope"] = np.stack([np.tile(np.concatenate([c, c]), (16, 1)), np.tile(np.concatenate([-s, s]), (16, 1))],
                         axis=1).astype(np.float32)
    D["wqE"], D["wkE"], D["wvE"], D["woE"] = E("wq").T, E("wk").T, E("wv").T, E("wo").T
    D["gateE"] = E("gate_w").T
    D["wE"] = E("expert_w").transpose(2, 0, 1)
    low = np.arange(128)[:, None] >= np.arange(128)[None, :]
    D["msk"] = np.stack([np.where(low, 0, -1e30), np.where(low.T, 0, -1e30)], axis=1).astype(bf)
    D["zrow"] = np.zeros((3, 8, 1024), bf)
    return {k: np.ascontiguousarray(v) for k, v in D.items()}


def kernel(**inputs):
    import concourse.bacc as bacc
    from concourse import mybir as mb
    from concourse.bass_utils import run_bass_kernel_spmd

    D = arrays(inputs)
    nc = bacc.Bacc("TRN2", target_bir_lowering=False, num_devices=1)
    I = {k: nc.dram_tensor(f"in_{k}", v.shape, mb.dt.from_np(v.dtype), kind="ExternalInput").ap()
         for k, v in D.items()}
    out = nc.dram_tensor("out_0_dram", (4096, 128), F32, kind="ExternalOutput").ap()
    build(nc, I, out, STOP)
    r = run_bass_kernel_spmd(nc, [{f"in_{k}": v for k, v in D.items()}], core_ids=[0])
    return r.results[0]["out_0_dram"].reshape(4, 1024, 128)
```

```python
from contextlib import ExitStack

import concourse.bass as bass
from concourse import mybir

F32 = mybir.dt.float32
BF = mybir.dt.bfloat16
ALU = mybir.AluOpType
ACT = mybir.ActivationFunctionType
AX = mybir.AxisListType.X

T = 4096
NT = 32
NG = 8
NB = 4


STOP = 9
LEAD = 8000
SPEED = 1.2
PLAG = 2
P1B = [2, 3, 4, 5]
PSB = [0, 1]
OEB = [6]
EVAC_A = True
POOLMASK = True
LAT = 200
FIRST = 0
POSTS = 0
BIAS = 1
GC = 950
SLACK = [0] * 2


class Line:

    def __init__(self, eng, sem):
        self.eng, self.sem, self.n, self.seen = eng, sem, 0, {}

    def on(self, *producers):
        need = {}
        for sem, count in producers:
            need[sem.num] = (sem, max(need.get(sem.num, (sem, 0))[1], count))
        for key, (sem, count) in need.items():
            if self.seen.get(key, 0) < count:
                self.eng.wait_ge(sem, count)
                self.seen[key] = count
        return self.eng

    def did(self, ins):
        self.n += 1
        ins.then_inc(self.sem, 1)
        return (self.sem, self.n)

    def last(self):
        return (self.sem, self.n)


class Ring:

    def __init__(self, bufs):
        self.bufs, self.i, self.freed = bufs, -1, [() for _ in bufs]
        self.when = [0.0] * len(bufs)

    def take(self):
        self.i = (self.i + 1) % len(self.bufs)
        return self.i, self.bufs[self.i], self.freed[self.i]

    def free(self, i, *readers, when=0.0):
        self.freed[i] = readers
        self.when[i] = when

    def next_free(self):
        return self.when[(self.i + 1) % len(self.bufs)]


def skewed(stages, n):
    most = max(lag for lag, _ in stages)
    for step in range(n + most):
        for lag, stage in reversed(stages):
            if 0 <= step - lag < n:
                stage(step - lag)


def build(nc, I, out, stop=9):
    ctx = ExitStack()
    with ctx:
        semn = [0]

        def sem(name):
            semn[0] += 1
            return ctx.enter_context(nc.semaphore(f"{name}_{semn[0]}"))

        def sb(name, shape, dt=F32):
            return ctx.enter_context(nc.sbuf_tensor(name, shape, dt))

        PE = Line(nc.tensor, sem("s_pe"))
        V = Line(nc.vector, sem("s_v"))
        A = Line(nc.scalar, sem("s_a"))
        G = Line(nc.gpsimd, sem("s_g"))
        SP = Line(nc.sync, sem("s_sp"))

        PS = ctx.enter_context(nc.psum_tensor("PS", [128, 8 * 512], F32))

        def bank(i, n=1):
            return PS[:, 512 * i:512 * (i + n)]

        def dma(dst, src, s, *producers):
            SP.on(*producers).dma_start(dst, src).then_inc(s, 16)
            return (s, 16)

        def barrier():
            marks = [x.last() for x in (PE, V, A, G) if x.n]
            for x in (PE, V, A, G, SP):
                x.on(*marks)

        s_c = sem("s_c")
        loads = [0]

        def load(name, shape, dt=F32, src=None):
            t = sb("w_" + name, shape, dt)
            nc.scalar.dma_start(t[tuple(slice(None) for _ in shape)], I[name] if src is None else src).then_inc(s_c, 16)
            loads[0] += 1
            return t

        X = sb("X", [128, NT, 128])
        XA = sb("XA", [128, NT, 128])
        B = [sb(f"B{i}", [128, 4096 + 4]) for i in range(6)]

        def full(i):
            return B[i][:, 0:4096]

        def tm(i):
            return B[i][:, 0:4096].rearrange("p (i c) -> p i c", c=128)

        def seq(i):
            return B[i][:, 0:4100].rearrange("p (b t) -> p b t", b=4)

        RB = sb("RB", [128, 16, 512])
        xin = I["x"].rearrange("(i p) c -> p i c", p=128)
        s_x = [sem("s_x") for _ in range(NG)]
        for g in range(NG):
            nc.sync.dma_start(X[:, 4 * g:4 * g + 4, :], xin[:, 4 * g:4 * g + 4, :]).then_inc(s_x[g], 16)
        ident = load("ident", [128, 128])
        vecs = load("vecs", [128, 16])
        WW = sb("WW", [128, 14, 128])
        wA, wck, wcv = WW[:, 0:4, :], WW[:, 4:8, :], WW[:, 8:12, :]
        nc.scalar.dma_start(WW[:, 0:12, :], I["wL0"]).then_inc(s_c, 16)
        loads[0] += 1
        gate0 = load("gate0", [128, 16])
        identb = load("identb", [128, 128], BF)
        rst16 = load("rst16", [128, NT * 16])
        rk0 = load("rk0", [128, NT, 4])
        wq4, wvr, wbr = WW[:, 0:4, :], WW[:, 4:12, :], WW[:, 12:14, :]
        wo1 = load("wo1", [128, 128])
        hsum = load("hsum", [128, 128])
        rows = load("rows", [128, 3, 128])
        wqE = load("wqE", [128, 128])
        wkE = load("wkE", [128, 32])
        wvE = load("wvE", [128, 32])
        woE = load("woE", [128, 128])
        gateE = load("gateE", [128, 8])
        wE = WW[:, 0:8, :]
        rst8 = load("rst8", [128, NT * 8])
        msk = load("msk", [128, 2, 128], BF)
        W_READY = (s_c, 16 * loads[0])
        dv = sb("dv", [128, 3])
        (LN1W, LN1B, LN2W, LN2B, TS, _, _, _, ANW, FNW) = [vecs[:, j:j + 1] for j in range(10)]
        HU, HBB0, HBB1 = [dv[:, j:j + 1] for j in range(3)]

        st = sb("st", [128, NT, 6])
        mv = [sb(f"mv{i}", [128, NT, 2]) for i in range(2)]
        rs = [sb(f"rs{i}", [128, NT, 6]) for i in range(2)]
        mhalf = sb("mhalf", [128, 8])
        G_half = G.did(nc.gpsimd.memset(mhalf[:, :], -0.5))
        for x in (PE, V, A, G):
            x.on(W_READY)
        t_dv = V.did(nc.vector.tensor_scalar(dv[:, :], vecs[:, 5:8], 0.5, None, ALU.mult))
        A.on(t_dv)

        def stats(g, src, k, *producers):
            toks = []
            for i in range(4 * g, 4 * g + 4):
                t = V.did(V.on(*producers).bn_stats(st[:, i, :], src(i)))
                toks.append(t)
            for i in range(4 * g, 4 * g + 4):
                t = V.did(V.on(toks[i - 4 * g]).bn_aggr(mv[k][:, i, :], st[:, i, :]))
            return t

        def rstd(g, k, eps, t_stats, then=None):
            s4 = slice(4 * g, 4 * g + 4)
            R = rs[k]
            v = mv[k][:, s4, 1]
            t = G.did(G.on(t_stats).tensor_scalar(R[:, s4, 3], v, eps, None, ALU.add))
            t = G.did(G.on(t, G_half).tensor_tensor(R[:, s4, 0], R[:, s4, 3], mhalf[:, 0:4], ALU.pow))
            t0 = t
            t = G.did(G.on(t).tensor_tensor(R[:, s4, 4], mv[k][:, s4, 0], R[:, s4, 0], ALU.mult))
            t = G.did(G.on(t).tensor_scalar(R[:, s4, 1], R[:, s4, 4], -1.0, None, ALU.mult))
            if then is not None:
                t = G.did(G.on(t0).tensor_tensor(R[:, s4, 5], v, R[:, s4, 0], ALU.mult))
                t = G.did(G.on(t).tensor_tensor(R[:, s4, 2], R[:, s4, 5], R[:, s4, 0], ALU.mult))
                t = G.did(G.on(t).tensor_scalar(R[:, s4, 5], R[:, s4, 2], then, None, ALU.add))
                t = G.did(G.on(t).tensor_tensor(R[:, s4, 2], R[:, s4, 5], mhalf[:, 0:4], ALU.pow))
            return t

        def normed(i, k, dst, src, *producers):
            return A.did(A.on(*producers).activation(dst, src, ACT.Identity, bias=rs[k][:, i, 1:2],
                                                     scale=rs[k][:, i, 0:1]))

        def transposes(dst, src, idn, *producers):
            for j in range(4):
                t = PE.did(PE.on(*producers).transpose(dst[:, 128 * j:128 * j + 128], src(j), idn[:, :]))
            return t

        def rb(i, n=1):
            return RB[:, i:i + n, :]

        HF, XXX, KF, VF, RF, MM = 0, 1, 2, 3, 4, 5
        hf, mm_ = seq(HF), seq(MM)
        SS = ctx.enter_context(nc.sbuf_tensor("SS", [128, 4100], F32))
        ss = SS[:, :].rearrange("p (b t) -> p b t", b=4)
        rHN = Ring([rb(0), rb(1)])
        rD = Ring([rb(2, 2), rb(4, 2)])
        rE = Ring([rb(6, 2), rb(8, 2)])
        pT = Ring([bank(0), bank(1)])
        pP = Ring([bank(i) for i in range(2, 8)])

        def ch(ap4, g, shift=0):
            b, h = g // 2, g % 2
            o = 1 + 512 * h - shift
            return ap4[:, b, o:o + 512]

        def cf(i, g):
            return B[i][:, 512 * g:512 * g + 512]

        t_init = []
        for b in range(4):
            t_init.append(G.did(G.on().tensor_copy(hf[:, b, 0:1], TS)))
            t_init.append(G.did(nc.gpsimd.memset(mm_[:, b, 0:1], 0.0)))
            t_init.append(G.did(nc.gpsimd.memset(ss[:, b, 0:1], 1.0)))
        t_init = t_init[-1]
        K = {}

        def a_stats(g):
            K["st", g] = rstd(g, 0, 1e-5, stats(g, lambda i: X[:, i, :], 0, (s_x[g], 16)), then=1e-5)

        def a_norm(g):
            ib, buf, fr = rHN.take()
            for j in range(4):
                i = 4 * g + j
                t = V.did(V.on(K["st", g]).tensor_scalar(XA[:, i, :], X[:, i, :], mv[0][:, i, 0:1],
                                                         rs[0][:, i, 0:1], ALU.subtract, ALU.mult))
                t = A.did(A.on(t, *fr).activation(buf[:, 0, 128 * j:128 * j + 128], XA[:, i, :], ACT.Copy,
                                                  scale=rs[0][:, i, 2:3]))
            K["hn", g] = (ib, buf, t)

        def a_turn(g):
            ib, buf, t = K["hn", g]
            pi, p, fr = pT.take()
            t = transposes(p, lambda j: buf[:, 0, 128 * j:128 * j + 128], ident, t, *fr)
            rHN.free(ib, t)
            t = V.did(V.on(t, t_init).tensor_scalar(ch(hf, g), p, LN1W, LN1B, ALU.mult, ALU.add))
            pT.free(pi, t)
            K["hf", g] = t

        def a_mix(g):
            ib, buf, fr = rD.take()
            t = V.did(V.on(K["hf", g], *fr).tensor_tensor(buf[:, 0, :], ch(hf, g), ch(hf, g, 1), ALU.subtract))
            t = V.did(V.on(t).scalar_tensor_tensor(cf(XXX, g), buf[:, 0, :], TS, ch(hf, g), ALU.mult, ALU.add))
            rD.free(ib, t)
            K["xxx", g] = t

        def a_proj(g):
            for w in range(3):
                pi, p, fr = pP.take()
                t = PE.did(PE.on(K["xxx", g], *fr).matmul(p, wA[:, w, :], cf(XXX, g), start=True, stop=True))
                if w < 2:
                    t = A.did(A.on(t).activation(cf((KF, VF)[w], g), p, ACT.Copy))
                else:
                    t = A.did(A.on(t).activation(cf(RF, g), p, ACT.Tanh, scale=0.5))
                pP.free(pi, t)
                K["krv"[w], g] = t
            K["kv", g] = t

        def a_scan(g):
            b, h = g // 2, g % 2
            o = 512 * h
            k = cf(KF, g)
            t = V.did(V.on(K["k", g], t_init, *([K["m", g - 1]] if h else [])).tensor_tensor_scan(
                ch(mm_, g), k, k, mm_[:, b, o:o + 1], ALU.max, ALU.max))
            K["m", g] = t
            ib, buf, fr = rD.take()
            V.did(V.on(t, *fr).tensor_tensor(buf[:, 0, :], ch(mm_, g, 1), ch(mm_, g), ALU.subtract))
            t = V.did(V.on(t).tensor_tensor(buf[:, 1, :], k, ch(mm_, g), ALU.subtract))
            ie, eb, fr = rE.take()
            t = A.did(A.on(t, *fr).activation(eb, buf, ACT.Exp))
            rD.free(ib, t)
            t = V.did(V.on(t, *([K["s", g - 1]] if h else [])).tensor_tensor_scan(
                ch(ss, g), eb[:, 0, :], eb[:, 1, :], ss[:, b, o:o + 1], ALU.mult, ALU.add))
            K["s", g] = t
            rE.free(ie, t)

        skewed([(0, a_stats), (1, a_norm), (2, a_turn), (3, a_mix), (4, a_proj), (6, a_scan)], NG)

        for b in range(4):
            t = A.did(A.on(K["s", 2 * b + 1]).activation(ss[:, b, :], ss[:, b, :], ACT.Ln))
            K["bb", b] = V.did(V.on(t, K["m", 2 * b + 1]).tensor_tensor(mm_[:, b, :], mm_[:, b, :], ss[:, b, :], ALU.add))
        t_aa0 = []
        for b in range(4):
            t_aa0 = G.did(G.on(K["bb", b]).memset(ss[:, b, 0:1], 0.0))

        rY = Ring([rb(10), rb(11)])
        rT = Ring([rb(12), rb(13)])
        rHN.freed = [(A.last(),), (A.last(),)]

        def b_decay(g):
            b = g // 2
            ib, buf, fr = rD.take()
            ie, eb, fe = rE.take()
            it, tb, ft = rT.take()
            t = V.did(V.on(K["bb", b], *fe).tensor_tensor(eb[:, 0, :], cf(KF, g), ch(mm_, g, 1), ALU.subtract))
            tt = A.did(A.on(t, *ft).activation(tb[:, 0, :], eb[:, 0, :], ACT.Tanh, scale=0.5, bias=HU))
            V.did(V.on(t, *fr).tensor_scalar(buf[:, 0, :], eb[:, 0, :], 0.0, None, ALU.min))
            t = V.did(V.on(t).tensor_scalar(buf[:, 1, :], eb[:, 0, :], 0.0, -1.0, ALU.max, ALU.mult))
            t = A.did(A.on(t, tt).activation(eb, buf, ACT.Exp))
            rD.free(ib, t)
            K["e", g] = (ie, eb, t, it, tb, tt)

        def b_wkv(g):
            b, h = g // 2, g % 2
            o = 512 * h
            ie, eb, t, it, tb, tt = K["e", g]
            ib, buf, fr = rD.take()
            iy, yb, fy = rY.take()
            t = V.did(V.on(t, *fr).tensor_tensor(buf[:, 0, :], eb[:, 0, :], cf(VF, g), ALU.mult))
            t = V.did(V.on(t, t_aa0, *([K["aa", g - 1]] if h else [])).tensor_tensor_scan(
                ch(ss, g), eb[:, 1, :], buf[:, 0, :], ss[:, b, o:o + 1], ALU.mult, ALU.add))
            K["aa", g] = t
            rE.free(ie, t)
            t = V.did(V.on(t).tensor_tensor(buf[:, 1, :], cf(VF, g), ch(ss, g, 1), ALU.subtract))
            t = V.did(V.on(t, tt).scalar_tensor_tensor(buf[:, 0, :], tb[:, 0, :], 1.0, buf[:, 1, :], ALU.add, ALU.mult))
            rT.free(it, t)
            t = V.did(V.on(t).scalar_tensor_tensor(buf[:, 1, :], buf[:, 0, :], 0.5, ch(ss, g, 1), ALU.mult, ALU.add))
            t = V.did(V.on(t, *fy).scalar_tensor_tensor(yb[:, 0, :], cf(RF, g), 1.0, buf[:, 1, :], ALU.add, ALU.mult))
            rD.free(ib, t)
            K["y", g] = (iy, yb, t)

        def b_res(g):
            iy, yb, t = K["y", g]
            pi, p, fr = pT.take()
            t = transposes(p, lambda j: yb[:, 0, 128 * j:128 * j + 128], ident, t, *fr)
            rY.free(iy, t)
            xa = XA[:, 4 * g:4 * g + 4, :].rearrange("p i c -> p (i c)")
            t = V.did(V.on(t).scalar_tensor_tensor(xa, p, 0.5, xa, ALU.mult, ALU.add))
            pT.free(pi, t)
            K["st", g] = rstd(g, 0, 1e-5, stats(g, lambda i: XA[:, i, :], 0, t))

        def b_norm(g):
            ib, buf, fr = rHN.take()
            for j in range(4):
                i = 4 * g + j
                t = normed(i, 0, buf[:, 0, 128 * j:128 * j + 128], XA[:, i, :], K["st", g], *fr)
            K["hn", g] = (ib, buf, t)

        def b_turn(g):
            ib, buf, t = K["hn", g]
            pi, p, fr = pT.take()
            t = transposes(p, lambda j: buf[:, 0, 128 * j:128 * j + 128], ident, t, *fr)
            rHN.free(ib, t)
            t = V.did(V.on(t).tensor_scalar(ch(hf, g), p, LN2W, LN2B, ALU.mult, ALU.add))
            pT.free(pi, t)
            if g % 2:
                b = g // 2
                t = V.did(V.on(t).tensor_copy(hf[:, b, 0:1], hf[:, b, 1024:1025]))
            K["hf", g] = t

        def b_mix(g):
            ib, buf, fr = rD.take()
            t = V.did(V.on(K["hf", g | 1], *fr).tensor_tensor(buf[:, 0, :], ch(hf, g, 1), ch(hf, g), ALU.subtract))
            t = V.did(V.on(t).scalar_tensor_tensor(cf(XXX, g), buf[:, 0, :], TS, ch(hf, g), ALU.mult, ALU.add))
            rD.free(ib, t)
            K["xxx", g] = t
            K["mixed", max(g - 1, 0)] = K["mixed", g] = (t,)

        def b_kc(g):
            o = (g % 2) * 2048
            rl = B[KF][:, o:o + 2048]
            sq = B[VF][:, o:o + 2048]
            for c in range(4):
                pi, p, fr = pP.take()
                t = PE.did(PE.on(K["xxx", g], *fr).matmul(p, wck[:, c, :], cf(XXX, g), start=True, stop=True))
                t = A.did(A.on(t, K["aa", NG - 1], *K.get(("sqd", g - 2), ())).activation(
                    rl[:, 512 * c:512 * c + 512], p, ACT.Relu))
                pP.free(pi, t)
                t = G.did(G.on(t, K["y", NG - 1][2], *K.get(("vvd", g - 2), ())).tensor_tensor(
                    sq[:, 512 * c:512 * c + 512], rl[:, 512 * c:512 * c + 512], rl[:, 512 * c:512 * c + 512], ALU.mult))
                K["sq", g, c] = t
            K["sqd", g] = (t,)
            pi, p, fr = pP.take()
            t = PE.did(PE.on(*fr).matmul(p, wA[:, 3, :], cf(XXX, g), start=True, stop=True))
            it, tb, ft = rT.take()
            t = A.did(A.on(t, *ft).activation(tb[:, 0, :], p, ACT.Tanh, scale=0.5))
            pP.free(pi, t)
            K["rc", g] = (it, tb, t)

        def b_vv(g):
            o = (g % 2) * 2048
            sq = B[VF][:, o:o + 2048]
            pi, p, fr = pP.take()
            for c in range(4):
                t = PE.did(PE.on(K["sq", g, c], *fr).matmul(p, wcv[:, c, :], sq[:, 512 * c:512 * c + 512],
                                                            start=(c == 0), stop=(c == 3)))
            K["vvd", g] = (t,)
            it, tb, tt = K["rc", g]
            iy, yb, fy = rY.take()
            t = V.did(V.on(t, tt, *fy).scalar_tensor_tensor(yb[:, 0, :], tb[:, 0, :], 1.0, p, ALU.add, ALU.mult))
            pP.free(pi, t)
            rT.free(it, t)
            K["y", g] = (iy, yb, t)

        def b_ret(g):
            iy, yb, t = K["y", g]
            pi, p, fr = pT.take()
            t = transposes(p, lambda j: yb[:, 0, 128 * j:128 * j + 128], ident, t, *fr)
            rY.free(iy, t)
            xa = XA[:, 4 * g:4 * g + 4, :].rearrange("p i c -> p (i c)")
            t = V.did(V.on(t).scalar_tensor_tensor(xa, p, 0.5, xa, ALU.mult, ALU.add))
            pT.free(pi, t)
            K["st", g] = rstd(g, 1, 1e-5, stats(g, lambda i: XA[:, i, :], 1, t))

        rX = Ring([rb(14), rb(15)])

        def add_normed(g, k, src, *producers):
            ix, xb, fr = rX.take()
            for j in range(4):
                t = normed(4 * g + j, k, xb[:, 0, 128 * j:128 * j + 128], src(4 * g + j), *producers, *fr)
            ta = t
            x = X[:, 4 * g:4 * g + 4, :].rearrange("p i c -> p (i c)")
            t = G.did(G.on(t).tensor_tensor(x, x, xb[:, 0, :], ALU.add))
            rX.free(ix, t)
            K["x", g] = t
            return ta

        def b_add(g):
            add_normed(g, 1, lambda i: XA[:, i, :], K["st", g])

        skewed([(0, b_decay), (1, b_wkv), (2, b_res), (3, b_norm), (4, b_turn)], NG)
        s_wm = sem("s_wm")
        for i, name in enumerate(("w1", "w3", "w2")):
            dma(B[4][:, 1152 * i:1152 * i + 1152], I[name], s_wm, K["y", NG - 1][2])
        dma(B[4][0:96, 3456:3968].bitcast(BF), I["sel"], s_wm)
        T_WM = (s_wm, 64)
        def finish():
            s_o = [sem("s_o") for _ in range(NG)]
            oo = out.rearrange("(i p) c -> p i c", p=128)
            for g in range(NG):
                dma(oo[:, 4 * g:4 * g + 4, :], X[:, 4 * g:4 * g + 4, :], s_o[g], K["x", g])
            for g in range(NG):
                SP.on((s_o[g], 16))

        if stop == 1:
            skewed([(0, b_mix), (1, b_kc), (2, b_vv), (3, b_ret), (4, b_add)], NG)
            finish()
            return

        XF = 0
        t_lg = [pP.freed[0], pP.freed[1]]
        freed = pP.freed[2:]
        pP = Ring([bank(i) for i in range(4, 8)])
        pP.freed = freed

        def n_stats(g):
            K["st", g] = rstd(g, 0, 1e-5, stats(g, lambda i: X[:, i, :], 0, K["x", g]))

        def n_norm(g):
            ib, buf, fr = rHN.take()
            for j in range(4):
                i = 4 * g + j
                t = normed(i, 0, buf[:, 0, 128 * j:128 * j + 128], X[:, i, :], K["st", g], *fr)
            K["hn", g] = (ib, buf, t)

        def n_turn(g):
            ib, buf, t = K["hn", g]
            pi, p, fr = pT.take()
            t = transposes(p, lambda j: buf[:, 0, 128 * j:128 * j + 128], ident, t, *fr)
            rHN.free(ib, t)
            t = A.did(A.on(t, *K.get(("mixed", g), ())).activation(cf(XF, g), p, ACT.Copy))
            pT.free(pi, t)
            K["xf", g] = t

        SC = sb("SC", [128, NT, 16])
        small = [SS[:, 512 * i:512 * i + 512].rearrange("p (i e) -> p i e", e=16) for i in range(4)]
        sv = SS[:, 2048:3584].rearrange("p (n i q) -> p n i q", i=NT, q=4)
        T8 = SS[:, 3584:3840].rearrange("p (i e) -> p i e", e=8)
        C3 = B[5][:, 0:1536].bitcast(BF).rearrange("p (i a e) -> p i a e", a=3, e=32)
        CFb = B[5][0:96, 1536:3584].bitcast(BF)
        wm = [B[4][:, 1152 * i:1152 * i + 1152].rearrange("p (j c) -> p j c", c=128) for i in range(3)]
        w1, w3, w2 = wm
        sel = B[4][0:96, 3456:3968].bitcast(BF).rearrange("p (j c) -> p j c", c=128)
        t_c3 = G.did(G.on().memset(C3[:, :, :, :].rearrange("p i a e -> p (i a e)"), 0.0))

        def n_gate(g):
            for j in range(4):
                t = PE.did(PE.on(K["xf", g], *t_lg[g // 4]).matmul(
                                                    bank(2 + g // 4)[:, 16 * (4 * (g % 4) + j):][:, 0:16],
                                                    cf(XF, g)[:, 128 * j:128 * j + 128], gate0[:, :],
                                                    start=True, stop=True, skip_group_check=True))
            K["lg", g] = t

        def vt(o, a, b, op, *w):
            return V.did(V.on(*w).tensor_tensor(o, a, b, op))

        def pick(S, th, k, E, reset, tmp, left, need, t, nt=NT):
            f = lambda z: z.rearrange("p i e -> p (i e)")
            thb = th.to_broadcast([128, nt, E])
            gt, eq, pc = tmp
            t = vt(gt, S, thb, ALU.is_gt, t)
            t = V.did(V.on(t).tensor_reduce(left.rearrange("p i a -> p (i a)"), gt, AX, ALU.add))
            t = V.did(V.on(t).tensor_scalar(need, left, -1.0, float(k), ALU.mult, ALU.add))
            t2 = vt(eq, S, thb, ALU.is_equal, t)
            t = V.did(V.on(t2).tensor_tensor_scan(f(pc), reset[:, 0:nt * E], f(eq), 0.0, ALU.mult, ALU.add))
            t = vt(pc, pc, need.to_broadcast([128, nt, E]), ALU.is_le, t)
            t = vt(eq, eq, pc, ALU.mult, t)
            return vt(gt, gt, eq, ALU.add, t)

        def route(r):
            sl = slice(16 * r, 16 * r + 16)
            S = SC[:, sl, :]
            fl = lambda z: z.rearrange("p i e -> p (i e)")
            t_sc = A.did(A.on(K["lg", 4 * r + 3]).activation(fl(S), bank(2 + r)[:, 0:256], ACT.Sigmoid))
            K["sc", r] = t_sc
            yield
            sm = [small[q][:, sl, :] for q in range(4)]
            sp = S.rearrange("p i (q a b) -> p (i q) a b", a=2, b=2)
            pr = fl(sm[0])
            hi = pr[:, 0:128].rearrange("p (n a) -> p n a", a=2)
            lo = pr[:, 128:256].rearrange("p (n a) -> p n a", a=2)
            svf = lambda n: sv[:, n, sl, :].rearrange("p i q -> p (i q)")
            vt(hi, sp[:, :, :, 0], sp[:, :, :, 1], ALU.max, t_sc)
            t = vt(lo, sp[:, :, :, 0], sp[:, :, :, 1], ALU.min, t_sc)
            vt(svf(0), hi[:, :, 0], hi[:, :, 1], ALU.max, t)
            vt(svf(1), hi[:, :, 0], hi[:, :, 1], ALU.min, t)
            t = vt(svf(2), lo[:, :, 0], lo[:, :, 1], ALU.max, t)
            yield
            t = vt(svf(3), svf(1), svf(2), ALU.max, t)
            t = vt(svf(4), svf(0), svf(3), ALU.add, t)
            gs = sv[:, 4, sl, :]
            for d in (1, 2, 3):
                t = vt(sv[:, 4 + d, sl, 0:4 - d], gs[:, :, 0:4 - d], gs[:, :, d:4], ALU.is_ge, t)
            yield
            t = V.did(V.on(t).tensor_copy(sv[:, 8, sl, :], rk0[:, 0:16, :]))
            for d in (1, 2, 3):
                t = vt(sv[:, 8, sl, d:4], sv[:, 8, sl, d:4], sv[:, 4 + d, sl, 0:4 - d], ALU.add, t)
                t = vt(sv[:, 8, sl, 0:4 - d], sv[:, 8, sl, 0:4 - d], sv[:, 4 + d, sl, 0:4 - d], ALU.subtract, t)
                yield
            t = V.did(V.on(t).tensor_scalar(svf(9), svf(8), 2.0, None, ALU.is_lt))
            t = V.did(V.on(t).tensor_scalar(svf(0), svf(9), -1.0, None, ALU.add))
            four = lambda z: z.rearrange("p i (q e) -> p (i q) e", e=4)
            bc4 = lambda n: svf(n).unsqueeze(2).to_broadcast([128, 64, 4])
            t = vt(four(sm[1]), four(S), bc4(9), ALU.mult, t)
            t = vt(four(sm[1]), four(sm[1]), bc4(0), ALU.add, t)
            for i in range(16):
                if i % 4 == 0:
                    yield
                tm8 = V.did(V.on(t).max(T8[:, 16 * r + i, :], sm[1][:, i, :]))
            yield
            t = pick(sm[1], T8[:, sl, 3:4], 4, 16, rst16, (sm[0], sm[2], sm[3]),
                     sv[:, 10, sl, 0:1], sv[:, 11, sl, 0:1], tm8, nt=16)
            yield
            t = vt(sm[2], sm[0], S, ALU.mult, t)
            wsum = sv[:, 0, sl, 0:1]
            t = V.did(V.on(t).tensor_reduce(wsum.rearrange("p i a -> p (i a)"), sm[2], AX, ALU.add))
            t = V.did(V.on(t).tensor_scalar(sv[:, 1, sl, 0:1], wsum, 1e-6, None, ALU.add))
            t = V.did(V.on(t).reciprocal(sv[:, 2, sl, 0:1], sv[:, 1, sl, 0:1]))
            t = vt(sm[1], sm[2], sv[:, 2, sl, 0:1].to_broadcast([128, 16, 16]), ALU.mult, t)
            yield
            t = V.did(V.on(t, t_c3).tensor_copy(C3[:, sl, 0, 0:16], sm[1]))
            t = vt(sm[2], sm[1], C3[:, sl, 0, 0:16], ALU.subtract, t)
            t = V.did(V.on(t).tensor_copy(C3[:, sl, 1, 0:16], sm[2]))
            t = vt(sm[3], sm[2], C3[:, sl, 1, 0:16], ALU.subtract, t)
            t_cut = V.did(V.on(t).tensor_copy(C3[:, sl, 2, 0:16], sm[3]))
            yield
            for g in range(4 * r, 4 * r + 4):
                ring = pC if "moe" in K else pT
                pi, p, fr = ring.take()
                pb = p.bitcast(BF)
                for j in range(4):
                    i = 4 * g + j
                    t = PE.did(PE.on(t_cut, *fr).transpose(pb[0:96, 128 * j:128 * j + 128],
                                                           C3[:, i, :, :].rearrange("p a e -> p (a e)"), identb[:, :]))
                t = V.did(V.on(t).tensor_copy(CFb[:, 512 * g:512 * g + 512], pb[0:96, 0:512]))
                ring.free(pi, t)
                K["cf", g] = t
                yield

        routes = [route(0), route(1)]

        def n_route(g):
            if g >= 3:
                for _ in range(4):
                    next(routes[0], None)

        skewed([(0, b_mix), (1, b_kc), (2, b_vv), (3, b_ret), (4, b_add),
                (5, n_stats), (6, n_norm), (7, n_turn), (8, n_gate), (9, n_route)], NG)
        t_ww = dma(WW[:, :, :], I["wL1"], sem("s_ww"), PE.last())
        for _ in routes[0]:
            pass
        next(routes[1])
        barrier()
        K["moe"] = True

        pG = Ring([bank(2), bank(3)])
        pU = Ring([bank(4), bank(5)])
        pC = Ring([bank(0), bank(1)])
        pO = Ring([bank(6), bank(7)])
        rS = Ring([rb(0), rb(1), rb(2)])
        rT1 = Ring([rb(3), rb(4)])
        rT2 = Ring([rb(5), rb(6), rb(7)])

        def m_gu(n):
            g, j = divmod(n, 9)
            gi, pg, fr = pG.take()
            tg = PE.did(PE.on(T_WM, *fr).matmul(pg, w1[:, j, :], cf(XF, g), start=True, stop=True))
            ui, pu, fr = pU.take()
            tu = PE.did(PE.on(*fr).matmul(pu, w3[:, j, :], cf(XF, g), start=True, stop=True))
            si, sbuf, fr = rS.take()
            t = A.did(A.on(tg, *fr).activation(sbuf[:, 0, :], pg, ACT.Silu))
            pG.free(gi, t)
            if j < 8:
                ci, pc, fr = pC.take()
                tc = PE.did(PE.on(K["cf", g], *fr).matmul(pc, sel[:, j, :], CFb[:, 512 * g:512 * g + 512],
                                                          start=True, stop=True))
                i1, b1, f1 = rT1.take()
                t = V.did(V.on(t, tu, *f1).tensor_tensor(b1[:, 0, :], sbuf[:, 0, :], pu, ALU.mult))
                rS.free(si, t)
                pU.free(ui, t)
                i2, b2, f2 = rT2.take()
                t = V.did(V.on(t, tc, *f2).tensor_tensor(b2[:, 0, :], b1[:, 0, :], pc, ALU.mult))
                pC.free(ci, t)
            else:
                i2, b2, f2 = rT2.take()
                t = V.did(V.on(t, tu, *f2).tensor_tensor(b2[:, 0, :], sbuf[:, 0, :], pu, ALU.mult))
                rS.free(si, t)
                pU.free(ui, t)
            K["t2", n] = (i2, b2, t)

        def m_out(n):
            g, j = divmod(n, 9)
            if j == 0:
                K["o", g] = pO.take()
            oi, po, fr = K["o", g]
            i2, b2, t = K["t2", n]
            for q in range(4):
                tp = PE.did(PE.on(t, *(fr if j == 0 else ())).matmul(
                    po[:, 128 * q:128 * q + 128], b2[:, 0, 128 * q:128 * q + 128], w2[:, j, :],
                    start=(j == 0 and q == 0), stop=(j == 8), skip_group_check=True))
            rT2.free(i2, tp)
            if j == 8:
                ts_ = stats(g, lambda i: po[:, 128 * (i - 4 * g):128 * (i - 4 * g) + 128], 1, tp)
                t = rstd(g, 1, 1e-5, ts_)
                t = add_normed(g, 1, lambda i: po[:, 128 * (i - 4 * g):128 * (i - 4 * g) + 128], t)
                pO.free(oi, t)

        def m_route(n):
            if n >= 4:
                next(routes[1], None)

        skewed([(0, m_gu), (1, m_route), (2, m_out)], 9 * NG)
        barrier()
        if stop == 2:
            finish()
            return

        rHN = Ring([rb(0), rb(1)])
        pT = Ring([bank(0), bank(1)])
        pP = Ring([bank(i) for i in range(2, 8)])
        QF, KF, B0, B1, NUM = 1, 2, 3, 4, 5
        cs = SS[:, 0:2048].rearrange("p (a t) -> p a t", a=2)
        s_cs = sem("s_cs")
        t_cs = dma(cs, I["rope"], s_cs)
        for x in (PE,):
            x.on(t_ww)

        def d_norm(g):
            n_norm(g)
            ib, buf, t = K["hn", g]
            for j in range(4):
                t = G.did(G.on(t).tensor_tensor(XA[:, 4 * g + j, :], buf[:, 0, 128 * j:128 * j + 128],
                                                rows[:, 0, :], ALU.add))
            K["xb", g] = t

        def d_turn(g):
            n_turn(g)
            ib = K["hn", g][0]
            rHN.free(ib, PE.last(), K["xb", g])

        rq = Ring([rb(2, 4), rb(6, 4)])

        def d_proj(g):
            h = g % 2
            for w in range(2):
                iq, qb, fq = rq.take()
                pi, p, fr = pP.take()
                t = PE.did(PE.on(K["xf", g], *fr).matmul(p, wq4[:, 2 * w, :], cf(XF, g), start=True, stop=True))
                t1 = vt(qb[:, 0, :], p, cs[:, 0, 512 * h:512 * h + 512], ALU.mult, t, t_cs, *fq)
                pP.free(pi, t1)
                pi, p, fr = pP.take()
                t = PE.did(PE.on(*fr).matmul(p, wq4[:, 2 * w + 1, :], cf(XF, g), start=True, stop=True))
                t2 = vt(qb[:, 1, :], p, cs[:, 1, 512 * h:512 * h + 512], ALU.mult, t)
                pP.free(pi, t2)
                t = vt(qb[:, 2, :], qb[:, 0, :], qb[:, 1, :], ALU.add, t1, t2)
                A.did(A.on(t).activation(qb[:, 0, :], qb[:, 2, :], ACT.Exp))
                t = A.did(A.on(t).activation(qb[:, 3, :], qb[:, 2, :], ACT.Relu))
                t = V.did(V.on(t).scalar_tensor_tensor(cf((QF, KF)[w], g), qb[:, 0, :], 1.0, qb[:, 3, :],
                                                       ALU.min, ALU.add))
                rq.free(iq, t)
            for w in range(2):
                pi, p, fr = pP.take()
                t = PE.did(PE.on(*fr).matmul(p, wbr[:, w, :], cf(XF, g), start=True, stop=True))
                d = cf((B0, B1)[w], g)
                t = A.did(A.on(t).activation(d, p, ACT.Tanh, scale=0.5, bias=(HBB0, HBB1)[w]))
                pP.free(pi, t)
                t = V.did(V.on(t).tensor_scalar(d, d, 0.5, 0.5, ALU.mult, ALU.add))
                t = V.did(V.on(t).tensor_scalar(d, d, 0.001, 0.999, ALU.max, ALU.min))
            K["qk", g] = t

        skewed([(0, n_stats), (1, d_norm), (2, d_turn), (3, d_proj)], NG)

        num = full(NUM).rearrange("p (i h e) -> p i h e", h=16, e=8)
        DEN = SC
        ring2 = lambda a: Ring([rb(a, 2).rearrange("p a t -> p (a t)"), rb(a + 2, 2).rearrange("p a t -> p (a t)")])
        rO = Ring([rb(0, 2).rearrange("p a t -> p (a t)"), rb(2, 2).rearrange("p a t -> p (a t)")])
        rM0 = ring2(4)
        rM1 = ring2(8)
        rP = Ring([rb(12, 2).rearrange("p a t -> p (a t)"), rb(14, 2).rearrange("p a t -> p (a t)")])
        rQ = Ring([SS[:, 2048:3072], SS[:, 3072:4096]])
        pV = Ring([bank(4, 2), bank(6, 2)])
        pN = Ring([bank(0, 2), bank(2, 2)])
        barrier()

        def d_value(n):
            e, b = divmod(n, 4)
            if e == 8:
                return
            pi, p, fr = pV.take()
            for h in range(2):
                t = PE.did(PE.on(*fr).matmul(p[:, 512 * h:512 * h + 512], wvr[:, e, :],
                                             B[XF][:, 1024 * b + 512 * h:1024 * b + 512 * h + 512],
                                             start=True, stop=True))
            K["vr", n] = (pi, p, t)

        def d_outer(n):
            e, b = divmod(n, 4)
            c = slice(1024 * b, 1024 * b + 1024)
            if e < 8:
                pi, p, t = K["vr", n]
                io, ob, fo = rO.take()
                t = vt(ob, B[KF][:, c], p, ALU.mult, t, *fo)
                pV.free(pi, t)
            else:
                io, ob, t = None, B[KF][:, c], (V.sem, 0)
            i0, m0, f0 = rM0.take()
            i1, m1, f1 = rM1.take()
            V.did(V.on(t, *f0).tensor_tensor_scan(m0, B[B0][:, c], ob, 0.0, ALU.mult, ALU.add))
            t = V.did(V.on(t, *f1).tensor_tensor_scan(m1, B[B1][:, c], ob, 0.0, ALU.mult, ALU.add))
            if io is not None:
                rO.free(io, t)
            ip, pb, fp = rP.take()
            t = G.did(G.on(t, *fp).tensor_tensor(pb, m0, m1, ALU.add))
            rM0.free(i0, t)
            rM1.free(i1, t)
            K["sum", n] = (ip, pb, t)

        def d_query(n):
            e, b = divmod(n, 4)
            c = slice(1024 * b, 1024 * b + 1024)
            ip, pb, t = K["sum", n]
            iq, qb, fq = rQ.take()
            t = vt(qb, pb, B[QF][:, c], ALU.mult, t, *fq)
            rP.free(ip, t)
            pi, p, fr = pN.take()
            for q in range(8):
                tp = PE.did(PE.on(t, *fr).matmul(p[:, 128 * q:128 * q + 128], qb[:, 128 * q:128 * q + 128], hsum[:, :],
                                                 start=True, stop=True, skip_group_check=True))
            rQ.free(iq, tp)
            src = p.rearrange("p (i h) -> p i h", h=128)[:, :, 0:16]
            dst = num[:, 8 * b:8 * b + 8, :, e] if e < 8 else DEN[:, 8 * b:8 * b + 8, :]
            t = A.did(A.on(tp).activation(dst, src, ACT.Copy))
            pN.free(pi, t)
            K["num", n] = t

        skewed([(0, d_value), (1, d_outer), (3, d_query)], 36)
        barrier()
        t_we = dma(WW[:, 0:8, :], I["wE"], sem("s_we"))
        one = lambda z: z.rearrange("p (a t) -> p a t", a=1)
        unit = lambda n: one(SS[:, 512 * n:512 * n + 512])
        pT = Ring([bank(0), bank(1)])
        pP = Ring([bank(i) for i in range(2, 8)])
        rHF = Ring([unit(2), unit(3)])
        rYF = Ring([unit(4), unit(5)])
        rZ = Ring([unit(6), unit(7)])
        den = [SS[:, 512 * n:512 * n + 512].rearrange("p (i e) -> p i e", e=16) for n in range(2)]
        t = V.did(V.on().tensor_scalar(den[0], DEN[:, :, :], 1e-6, None, ALU.add))
        t_rd = V.did(V.on(t).reciprocal(den[1], den[0]))
        rX = Ring([rb(15), one(SC[:, :, :].rearrange("p i e -> p (i e)"))])
        rX.freed = [(), (t,)]

        def f_div(g):
            s4 = slice(4 * g, 4 * g + 4)
            ib, buf, fr = rHF.take()
            o = buf[:, 0, :].rearrange("p (n e) -> p n e", e=8)
            a = num[:, s4, :, :].rearrange("p i h e -> p (i h) e")
            r = den[1][:, s4, :].rearrange("p i h -> p (i h)").unsqueeze(2).to_broadcast([128, 64, 8])
            t = vt(o, a, r, ALU.mult, t_rd, *fr)
            K["div", g] = t
            pi, p, fr = pT.take()
            t = transposes(p, lambda j: buf[:, 0, 128 * j:128 * j + 128], ident, t, *fr)
            rHF.free(ib, t)
            iy, yb, fy = rYF.take()
            t = A.did(A.on(t, *fy).activation(yb[:, 0, :], p, ACT.Copy))
            pT.free(pi, t)
            K["yf", g] = (iy, yb, t)

        def out_proj(g, w):
            iy, yb, t = K["yf", g]
            pi, p, fr = pP.take()
            for j in range(4):
                t = PE.did(PE.on(t, *fr).matmul(p[:, 128 * j:128 * j + 128], yb[:, 0, 128 * j:128 * j + 128], w[:, :],
                                                start=True, stop=True, skip_group_check=True))
            rYF.free(iy, t)
            xa = XA[:, 4 * g:4 * g + 4, :].rearrange("p i c -> p (i c)")
            t = vt(xa, xa, p, ALU.add, t)
            pP.free(pi, t)
            return t

        def f_out(g):
            t = out_proj(g, wo1)
            K["st", g] = rstd(g, 0, 1e-5, stats(g, lambda i: XA[:, i, :], 0, t))

        def f_aff(g):
            iz, zb, fz = rZ.take()
            for j in range(4):
                i = 4 * g + j
                z = zb[:, 0, 128 * j:128 * j + 128]
                t = normed(i, 0, z, XA[:, i, :], K["st", g], *fz)
                t = vt(z, z, rows[:, 1, :], ALU.mult, t)
                t = vt(XA[:, i, :], z, rows[:, 2, :], ALU.add, t)
            rZ.free(iz, t)
            K["st1", g] = rstd(g, 1, 1e-5, stats(g, lambda i: XA[:, i, :], 1, t))

        def f_add(g):
            add_normed(g, 1, lambda i: XA[:, i, :], K["st1", g])

        if stop == 3:
            skewed([(0, f_div), (1, f_out), (2, f_aff), (3, f_add)], NG)
            finish()
            return

        rHN = Ring([rb(0), rb(1)])
        XF = 0
        scrQ = nc.dram_tensor("scrQ", [4, 3, 128, 1024], BF, kind="Internal").ap()
        scrK = nc.dram_tensor("scrK", [3, 32, T], BF, kind="Internal").ap()
        scrM = nc.dram_tensor("scrM", [8, 24, 1024], BF, kind="Internal").ap()
        qs = [B[i][0:96, 0:4096].bitcast(BF).rearrange("p (h t) -> p h t", h=8) for i in (1, 5, 3)]
        kst = [B[2][0:96, 2048 * i:2048 * i + 2048].bitcast(BF).rearrange("p (k t) -> p k t", k=4) for i in range(2)]
        VA = B[4][:, 0:4096].rearrange("p (i k e) -> p i k e", k=4, e=32)
        s_fill = sem("s_fill")

        def fill(z, src, *producers):
            for a in range(3):
                dma(z[32 * a + 24:32 * a + 32, :, :], src, s_fill, *producers)

        for z in (qs[0], qs[2]):
            fill(z, I["zeros"])
        for z in kst:
            fill(z, I["ones"])

        def e_values(g):
            t = V.did(V.on().memset(cf(4, g), 0.0))
            K["va", g] = V.did(V.on(t).memset(VA[:, 4 * g:4 * g + 4, :, 8:9].rearrange("p i k e -> p (i k) e"), 1.0))

        rB = [RB[:, :, :].rearrange("p n t -> p (n t)")[:, 5120 + 768 * i:5888 + 768 * i].bitcast(BF).rearrange(
            "p (a t) -> p a t", a=3) for i in range(2)]
        rKb = [RB[0:32, :, :].rearrange("p n t -> p (n t)")[:, 6656 + 768 * i:7424 + 768 * i].bitcast(BF).rearrange(
            "p (a t) -> p a t", a=3) for i in range(1)]
        rBq, rBk = Ring([z for z in rB]), Ring([z for z in rKb])
        rR = Ring([rb(2, 4), rb(6, 4)])

        def e_stats(g):
            K["st", g] = rstd(g, 0, 1e-5, stats(g, lambda i: X[:, i, :], 0, K["x", g]), then=1e-6)

        def e_norm(g):
            ib, buf, fr = rHN.take()
            for j in range(4):
                i = 4 * g + j
                t = V.did(V.on(K["st", g]).tensor_scalar(XA[:, i, :], X[:, i, :], mv[0][:, i, 0:1],
                                                         rs[0][:, i, 0:1], ALU.subtract, ALU.mult))
                t = A.did(A.on(t, *fr).activation(buf[:, 0, 128 * j:128 * j + 128], XA[:, i, :], ACT.Copy,
                                                  scale=rs[0][:, i, 2:3]))
            K["hn", g] = (ib, buf, t)

        def turn_scaled(g, col):
            ib, buf, t = K["hn", g]
            pi, p, fr = pT.take()
            t = transposes(p, lambda j: buf[:, 0, 128 * j:128 * j + 128], ident, t, *fr)
            rHN.free(ib, t)
            t = A.did(A.on(t).activation(cf(XF, g), p, ACT.Copy, scale=col))
            pT.free(pi, t)
            K["xf", g] = t

        def e_turn(g):
            turn_scaled(g, ANW)

        def split3(ring, p, np_, scale, t, out_dma, g):
            ir, r, fr = rR.take()
            ib, o, fo = ring.take()
            P_ = slice(0, np_)
            t = A.did(A.on(t, *fr).activation(r[P_, 0, :], p, ACT.Copy, scale=scale))
            tp = t
            t = V.did(V.on(t, *fo).tensor_copy(o[P_, 0, :], r[P_, 0, :]))
            t = vt(r[P_, 1, :], r[P_, 0, :], o[P_, 0, :], ALU.subtract, t)
            t = V.did(V.on(t).tensor_copy(o[P_, 1, :], r[P_, 1, :]))
            t = vt(r[P_, 2, :], r[P_, 1, :], o[P_, 1, :], ALU.subtract, t)
            t = V.did(V.on(t).tensor_copy(o[P_, 2, :], r[P_, 2, :]))
            rR.free(ir, t)
            td = out_dma(o, t)
            ring.free(ib, td)
            return tp, td

        def e_proj(g):
            b, h = g // 2, g % 2
            c = slice(512 * h, 512 * h + 512)
            pi, p, fr = pP.take()
            t = PE.did(PE.on(K["xf", g], *fr).matmul(p, wqE[:, :], cf(XF, g), start=True, stop=True))
            tp, K["dq", g] = split3(rBq, p, 128, 8.0 ** -0.5, t, lambda o, t: dma(
                scrQ[b, :, :, c].rearrange("a p t -> p a t"), o[:, :, :], sem("s_sq"), t), g)
            pP.free(pi, tp)
            pi, p, fr = pP.take()
            t = PE.did(PE.on(*fr).matmul(p[0:32, :], wkE[:, :], cf(XF, g), start=True, stop=True))
            tp, K["dk", g] = split3(rBk, p[0:32, :], 32, 1.0, t, lambda o, t: dma(
                scrK[:, :, 512 * g:512 * g + 512].rearrange("a p t -> p a t"), o[:, :, :], sem("s_sk"), t), g)
            pP.free(pi, tp)
            pi, p, fr = pP.take()
            for j in range(4):
                t = PE.did(PE.on(*fr).matmul(p[:, 32 * j:32 * j + 32], cf(XF, g)[:, 128 * j:128 * j + 128], wvE[:, :],
                                             start=True, stop=True, skip_group_check=True))
            for j in range(4):
                t2 = A.did(A.on(t, K["va", g]).activation(VA[:, 4 * g + j, :, 0:8],
                                                    p[:, 32 * j:32 * j + 32].rearrange("p (k e) -> p k e", e=8),
                                                    ACT.Copy))
            pP.free(pi, t2)
            K["v", g] = t2

        skewed([(0, f_div), (1, f_out), (2, f_aff), (3, f_add), (4, e_stats), (4, e_values), (5, e_norm), (6, e_turn),
                (7, e_proj)], NG)
        fill(qs[1], I["zeros"], K["div", NG - 1])
        T_FILL = (s_fill, 16 * 15)

        def load_k(b, *producers):
            s_ks = sem("s_ks")
            for a in range(3):
                for c in range(3):
                    SP.on(K["dk", 2 * b], K["dk", 2 * b + 1], *producers).dma_start(
                        kst[b % 2][32 * a + 8 * c:32 * a + 8 * c + 8, :, :],
                        scrK[c, :, 1024 * b:1024 * b + 1024].rearrange("(k d) t -> d k t", d=8)).then_inc(s_ks, 16)
            K["keys", b] = (s_ks, 144)

        clock = {"PE": 0.0, "V": 0.0, "A": 0.0, "G": 0.0}

        def load_q(u, *producers):
            s, n, b, hh = sem("s_q"), 0, u // 2, u % 2
            for a in range(3):
                for c in range(3):
                    SP.on(K["dq", 2 * b], K["dq", 2 * b + 1], *producers).dma_start(
                        qs[u % 3][32 * a + 8 * c:32 * a + 8 * c + 8, :, :],
                        scrQ[b, a, 64 * hh:64 * hh + 64, :].rearrange("(h d) t -> d h t", d=8)).then_inc(s, 16)
                    n += 16
            if u >= 3:
                SP.eng.dma_start(qs[u % 3][24:27, :, :], I["zrow"]).then_inc(s, 16)
                n += 16
            K["queries", u] = (s, n)
            K["queries at", u] = clock["PE"] + 5000

        MX = SS[:, 0:256].rearrange("p (r i h c) -> p r i h c", r=2, i=8, c=2)
        NM = SS[:, 256:640].rearrange("p (r a n) -> p r a n", r=2, a=3)
        M3 = SS[:, 640:832].bitcast(BF).rearrange("p (r i n) -> p r i n", r=2, i=8)
        RC = SS[:, 832:896].rearrange("p (r n) -> p r n", r=4)
        MF = SS[0:24, 1024:2048].bitcast(BF).rearrange("p (r t) -> p r t", r=2)
        p1 = Ring([bank(i) for i in P1B])
        pS2 = Ring([bank(i) for i in PSB])
        pOE = Ring([bank(i) for i in OEB])
        pX = Ring([bank(7)])
        barrier()

        def head(u, h):
            b, hh = u // 2, u % 2
            return qs[u % 3][:, h, :], kst[b % 2][:, 2 * hh + h // 4, :]

        def spend(engine, ns, after=0.0):
            clock[engine] = max(clock[engine], after) + ns
            return clock[engine]


        def pass1(u):
            mx = MX[:, u % 2, :, :, :]
            while ("queries", u) not in K or ("keys", u // 2) not in K:
                yield None
            for h in range(8):
                Q, Kk = head(u, h)
                for i in range(8):
                    for c in range(i // 4 + 1):
                        yield max(p1.next_free(), K["queries at", u])
                        pi, p, fr = p1.take()
                        n = 512 if c < i // 4 else 128 * (i % 4 + 1)
                        dg = c == i // 4
                        t = PE.did(PE.on(T_FILL, K["queries", u], K["keys", u // 2], *fr).matmul(
                            p[:, 0:n], Q[:, 128 * i:128 * i + 128], Kk[:, 512 * c:512 * c + n],
                            start=True, stop=not dg))
                        if dg:
                            t = PE.did(PE.on().matmul(p[:, n - 128:n], identb[:, :], msk[:, 0, :],
                                                      start=False, stop=True))
                        t = V.did(V.on(t).tensor_reduce(mx[:, i, h, c:c + 1], p[:, 0:n], AX, ALU.max))
                        w = spend("PE", 0.417 * n + 3 + 56 * dg)
                        p1.free(pi, t, when=spend("V", 1.04 * n + 65, w + LAT) + LAT)
            nm = NM[:, u % 2, :, :]
            v = lambda a: nm[:, a, :].rearrange("p (i h) -> p i h", h=8)
            m3 = M3[:, u % 2, :, :].rearrange("p i (a h) -> p i a h", a=3)
            t = V.did(V.on(t).tensor_scalar(v(0)[:, 0:4, :], mx[:, 0:4, :, 0], -1.0, None, ALU.mult))
            t = vt(v(1)[:, 4:8, :], mx[:, 4:8, :, 0], mx[:, 4:8, :, 1], ALU.max, t)
            t = V.did(V.on(t).tensor_scalar(v(0)[:, 4:8, :], v(1)[:, 4:8, :], -1.0, None, ALU.mult))
            t = V.did(V.on(t).tensor_copy(m3[:, :, 0, :], v(0)))
            t = vt(v(1), v(0), m3[:, :, 0, :], ALU.subtract, t)
            t = V.did(V.on(t).tensor_copy(m3[:, :, 1, :], v(1)))
            t = vt(v(2), v(1), m3[:, :, 1, :], ALU.subtract, t)
            t = V.did(V.on(t).tensor_copy(m3[:, :, 2, :], v(2)))
            tasks.append(guard(u, t, spend("V", 900)))

        def guard(u, t, at):
            while held:
                yield None
            held.append(u)
            yield max(at + LAT, pX.next_free())
            pi, p, fr = pX.take()
            pb = p.bitcast(BF)
            for i in range(8):
                tp = PE.did(PE.on(t, *fr).transpose(pb[0:24, 128 * i:128 * i + 128], M3[:, u % 2, i, :], identb[:, :]))
            t = V.did(V.on(tp, *K.get(("md", u - 2), ())).tensor_copy(MF[:, u % 2, :], pb[0:24, 0:1024]))
            w = spend("V", 1130, spend("PE", 8 * 60) + LAT)
            pX.free(pi, t, when=w + LAT)
            held.pop()
            td = dma(scrM[u, :, :], MF[:, u % 2, :], sem("s_sm"), t)
            K["md", u] = (td,)
            K["guard", u] = dma(qs[u % 3][24:27, :, :], scrM[u, :, :].rearrange("(a h) t -> a h t", h=8),
                            sem("s_m"), td, tp)
            K["guard at", u] = w + 5000

        rP4 = Ring([rb(0, 4), rb(4, 4), rb(8, 4)])
        rOS = Ring([rb(12), rb(13)])
        AT = XF

        def normalise(u, kl, qc, oi, po, tp, at):
            b, kv = u // 2, 2 * (u % 2) + kl
            io, ob, fr = rOS.take()
            if EVAC_A:
                t = A.did(A.on(tp, *fr).activation(ob[:, 0, :], po, ACT.Copy))
                w = spend("A", 480, at + LAT)
            else:
                t = V.did(V.on(tp, *fr).tensor_copy(ob[:, 0, :], po))
                w = spend("V", 600, at + LAT)
            pOE.free(oi, t, when=w + LAT)
            yield w
            while held:
                yield None
            held.append(u)
            yield max(w + LAT, pX.next_free())
            pi, p, fr = pX.take()
            t = transposes(p, lambda j: ob[:, 0, 128 * j:128 * j + 128], ident, t, *fr)
            w = spend("PE", 4 * 218)
            rOS.free(io, t)
            yield w
            p3 = p.rearrange("p (n e) -> p n e", e=32)
            rc = RC[:, (2 * kl + qc), :].unsqueeze(2)
            t = V.did(V.on(t).reciprocal(rc, p3[:, :, 8:9]))
            dst = B[AT][:, 1024 * b + 512 * qc:1024 * b + 512 * qc + 512].rearrange(
                "p (i k j e) -> p k i j e", i=4, k=4, j=4)[:, kv, :, :, :]
            for i in range(4):
                t2 = vt(dst[:, i, :, :], p3[:, 4 * i:4 * i + 4, 0:8],
                        rc[:, 4 * i:4 * i + 4, :].to_broadcast([128, 4, 8]), ALU.mult, t)
            pX.free(pi, t2, when=spend("V", 650, w + LAT) + LAT)
            held.pop()
            if u % 2 == 1 and kl == 1:
                K["at", 2 * b + qc] = t2
                ready.append(2 * b + qc)

        tasks, held, ready = [], [], []

        GROUPS = [(u, kl, qc) for u in range(8) for qc in range(2) for kl in range(2)]
        STEPS = [(n, kt) for n, (u, kl, qc) in enumerate(GROUPS) for kt in range(4 * qc + 4)]

        def scores(n, kt):
            u, kl, qc = GROUPS[n]
            while ("guard", u) not in K:
                yield None
            if (n, kt) == (0, 0):
                for x in (A, V):
                    x.on(*[K["dq", g] for g in range(NG)], *[K["dk", g] for g in range(NG)])
            off = max(0, 128 * (kt - 4 * qc))
            w = 512 - off
            for z in range(4):
                ring = pS6 if done1 else pS2
                yield max(ring.next_free(), K["guard at", u])
                ring = pS6 if done1 else pS2
                if z == 0:
                    ip, pb, fp = rP4.take()
                si, ps, fr = ring.take()
                Q, Kk = head(u, 4 * kl + z)
                dg = kt >= 4 * qc
                onpe = dg and not POOLMASK
                t = PE.did(PE.on(K["guard", u], *fr).matmul(
                    ps[:, 0:w], Kk[:, 128 * kt:128 * kt + 128],
                    Q[:, 512 * qc + off:512 * qc + 512], start=True, stop=not onpe))
                if onpe:
                    t = PE.did(PE.on().matmul(ps[:, 0:128], identb[:, :], msk[:, 1, :], start=False, stop=True))
                t = A.did(A.on(t, *fp).activation(pb[:, z, 0:w], ps[:, 0:w], ACT.Exp))
                at = spend("A", 0.83 * w + 53, spend("PE", 0.417 * w + 3 + 56 * onpe) + LAT)
                ring.free(si, t, when=at + LAT)
            if dg and POOLMASK:
                t = G.did(G.on(t).affine_select(
                    out=pb[:, :, 0:128], in_=pb[:, :, 0:128], compare_op=ALU.is_ge, fill=0.0, base=0,
                    pattern=[[0, 4], [1, 128]], channel_multiplier=-1))
                at = spend("G", GC, at + LAT)
            K["exp", n, kt] = (ip, pb, t, off, w, at)
            if (kl, qc, kt) == (1, 1, 7):
                K["p2", u] = PE.last()
                if u + 3 < 8:
                    load_q(u + 3, K["p2", u])
                if u % 2 == 1 and u // 2 + 2 < 4:
                    load_k(u // 2 + 2, K["p2", u])

        def products(n, kt):
            u, kl, qc = GROUPS[n]
            b, kv = u // 2, 2 * (u % 2) + kl
            at = K["exp", n, kt][5] + LAT
            yield max(at, pOE.next_free()) if kt == 0 else at
            if kt == 0:
                K["oe"] = pOE.take()
            oi, po, fo = K["oe"]
            ip, pb, t, off, w, _ = K["exp", n, kt]
            for j in range(4):
                tp = PE.did(PE.on(t, *fo).matmul(
                    po[32 * j:32 * j + 32, off:off + w], VA[:, 8 * b + kt, kv, :], pb[:, j, 0:w],
                    start=(kt == 0), stop=(kt == 4 * qc + 3), skip_group_check=True))
            rP4.free(ip, tp)
            at = spend("PE", 1.667 * w + 60)
            if kt == 4 * qc + 3:
                tasks.append(normalise(u, kl, qc, oi, po, tp, at))

        def pass2():
            for s in range(len(STEPS) + PLAG):
                if s < len(STEPS):
                    yield from scores(*STEPS[s])
                if s >= PLAG:
                    yield from products(*STEPS[s - PLAG])

        for u in range(3):
            if u % 2 == 0:
                load_k(u // 2)
            load_q(u)
        pS6 = Ring([bank(i) for i in PSB + P1B])
        done1 = []

        rYF = Ring([unit(4), unit(5)])
        rHN = Ring([unit(6), unit(7)])
        rX = Ring([rb(14), rb(15)])
        HB = XF
        scf = SC[:, :, :].rearrange("p i e -> p (i e)")
        K["hx", -2] = K["hx", -1] = (V.sem, 0)
        flat8 = lambda z: z.rearrange("p i e -> p (i e)")

        def banks():
            return pS6 if done1 else p1

        def post(g):
            s4 = slice(4 * g, 4 * g + 4)
            scr = lambda o, e: scf[:, 256 * (g % 2) + o:256 * (g % 2) + o + 4 * e].rearrange("p (i e) -> p i e", e=e)
            LG, comb, T8, s0, s1, s2, s3 = [scr(32 * q, 8) for q in range(7)]
            c0, c1, c2, c3, left, need = [scr(224 + 4 * q, 1) for q in range(6)]
            yield banks().next_free()
            ring = banks()
            pi, p, fr = ring.take()
            t = transposes(p, lambda j: cf(AT, g)[:, 128 * j:128 * j + 128], ident, K["at", g], *fr)
            iy, yb, fy = rYF.take()
            t = A.did(A.on(t, *fy).activation(yb[:, 0, :], p, ACT.Copy))
            w = spend("A", 480, spend("PE", 4 * 218) + LAT)
            ring.free(pi, t, when=w + LAT)
            yield max(w + LAT, banks().next_free())
            ring = banks()
            pi, p, fr = ring.take()
            for j in range(4):
                t = PE.did(PE.on(t, *fr).matmul(p[:, 128 * j:128 * j + 128], yb[:, 0, 128 * j:128 * j + 128],
                                                woE[:, :], start=True, stop=True, skip_group_check=True))
            rYF.free(iy, t)
            xa = XA[:, s4, :].rearrange("p i c -> p (i c)")
            t = vt(xa, xa, p, ALU.add, t)
            w = spend("V", 600, spend("PE", 4 * 218) + LAT)
            ring.free(pi, t, when=w + LAT)
            yield w
            t = stats(g, lambda i: XA[:, i, :], 0, t)
            R = rs[0]
            t = G.did(G.on(t).tensor_tensor(R[:, s4, 3], mv[0][:, s4, 0], mv[0][:, s4, 0], ALU.mult))
            t = G.did(G.on(t).tensor_tensor(R[:, s4, 4], R[:, s4, 3], mv[0][:, s4, 1], ALU.add))
            t = G.did(G.on(t).tensor_scalar(R[:, s4, 5], R[:, s4, 4], 1e-6, None, ALU.add))
            t = G.did(G.on(t).tensor_tensor(R[:, s4, 0], R[:, s4, 5], mhalf[:, 0:4], ALU.pow))
            yield spend("V", 1300) + 2500
            ib, buf, fr = rHN.take()
            for j in range(4):
                i = 4 * g + j
                t2 = A.did(A.on(t, *fr).activation(buf[:, 0, 128 * j:128 * j + 128], XA[:, i, :], ACT.Copy,
                                                   scale=rs[0][:, i, 0:1]))
            w = spend("A", 4 * 250)
            yield max(w + LAT, banks().next_free())
            ring = banks()
            pi, p, fr = ring.take()
            t = transposes(p, lambda j: buf[:, 0, 128 * j:128 * j + 128], ident, t2, *fr)
            rHN.free(ib, t)
            t = A.did(A.on(t).activation(cf(HB, g), p, ACT.Copy, scale=FNW))
            w = spend("A", 570, spend("PE", 4 * 218) + LAT)
            ring.free(pi, t, when=w + LAT)
            yield max(w + LAT, banks().next_free())
            ring = banks()
            pi, p, fr = ring.take()
            for j in range(4):
                t = PE.did(PE.on(t, *fr).matmul(p[:, 8 * j:8 * j + 8], cf(HB, g)[:, 128 * j:128 * j + 128],
                                                gateE[:, :], start=True, stop=True, skip_group_check=True))
            t = V.did(V.on(t).tensor_copy(flat8(LG), p[:, 0:32]))
            ring.free(pi, t, when=spend("V", 100, spend("PE", 4 * 430) + LAT) + LAT)
            for j in range(4):
                tm = V.did(V.on(t).max(T8[:, j, :], LG[:, j, :]))
            bc8 = lambda z: z.to_broadcast([128, 4, 8])
            tx = vt(s3, LG, bc8(T8[:, :, 0:1]), ALU.subtract, tm)
            ty = vt(c0, T8[:, :, 1:2], T8[:, :, 0:1], ALU.subtract, tm)
            tx = A.did(A.on(tx, K["hx", g - 2]).activation(comb, s3, ACT.Exp))
            ty = A.did(A.on(ty).activation(c1, c0, ACT.Exp))
            yield spend("A", 200, spend("V", 900) + LAT) + LAT
            t = pick(LG, T8[:, :, 1:2], 2, 8, rst8, (s0, s1, s2), left, need, tm, nt=4)
            yield spend("V", 1900)
            t = V.did(V.on(t, ty).tensor_scalar(c2, c1, 1.0, None, ALU.add))
            t = V.did(V.on(t).reciprocal(c3, c2))
            t = vt(s1, s0, comb, ALU.mult, t, tx)
            t = vt(comb, s1, bc8(c3), ALU.mult, t)
            spend("V", 900)
            for j in range(4):
                x = XA[:, 4 * g + j, :]
                for half in range(2):
                    yield banks().next_free()
                    ring = banks()
                    pi, p, fr = ring.take()
                    tp = PE.did(PE.on(t_we, *fr).matmul(p, cf(HB, g)[:, 128 * j:128 * j + 128],
                                                        wE[:, 4 * half:4 * half + 4, :].rearrange("p e c -> p (e c)"),
                                                        start=True, stop=True))
                    for q in range(4):
                        e = 4 * half + q
                        t = V.did(V.on(t, tp).scalar_tensor_tensor(x, p[:, 128 * q:128 * q + 128], comb[:, j, e:e + 1],
                                                                   x, ALU.mult, ALU.add))
                    ring.free(pi, t, when=spend("V", 4 * 263, spend("PE", 856) + LAT) + LAT)
            K["hx", g] = t
            t = rstd(g, 1, 1e-5, stats(g, lambda i: XA[:, i, :], 1, t))
            yield spend("V", 1300) + 2500
            add_normed(g, 1, lambda i: XA[:, i, :], t)
            spend("A", 4 * 340)

        first = (z for u in range(8) for z in pass1(u))
        second = (z for s in range(len(STEPS) + PLAG) for z in [
            *([scores(*STEPS[s])] if s < len(STEPS) else []), *([products(*STEPS[s - PLAG])] if s >= PLAG else [])])
        second = (z for stream in second for z in stream)
        END = object()
        heads = {}

        def look(stream):
            if stream not in heads or heads[stream] is None:
                heads[stream] = next(stream, END)
            return heads[stream]

        posts = []
        live = [second, first]
        while live or tasks or posts or ready:
            if ready and len(posts) < 2:
                posts.append(post(ready.pop(0)))
            best = None
            for z in [*tasks, *(live if BIAS == 0 else live[::-1]), *posts]:
                at = look(z)
                if at is END:
                    for group in (tasks, live, posts):
                        if z in group:
                            group.remove(z)
                    if z is first:
                        done1.append(True)
                        pS6.freed, pS6.when = pS2.freed + p1.freed, pS2.when + p1.when
                    best = None
                    break
                if at is None:
                    continue
                if z is first:
                    at += FIRST
                if z in posts:
                    at += POSTS
                at = max(at, clock["PE"])
                if best is None or at < best[0]:
                    best = (at, z)
            if best is not None:
                at, z = best
                clock["PE"] = max(clock["PE"], heads[z])
                heads[z] = None
                look(z)
        finish()


def arrays(inputs):
    import numpy as np

    bf = mybir.dt.np(BF)
    a = {k: np.asarray(v) for k, v in inputs.items()}
    L = lambda n: a["L0_attn_" + n]
    M = lambda n: a["L0_ffn_" + n]
    N = lambda n: a["L1_attn_" + n]
    E = lambda n: a["L1_ffn_" + n]
    D = {"x": L("x").reshape(4096, 128)}
    eye = np.eye(128, dtype=np.float32)
    D["ident"], D["identb"] = eye, eye.astype(bf)
    z = np.zeros(128, np.float32)
    rep = lambda v: np.repeat(v, 8)
    bb = N("bbeta").reshape(16, 2)
    cols = [L("ln1_w"), L("ln1_b"), L("ln2_w"), L("ln2_b"), L("time_shift").reshape(128), L("time_first"),
            rep(bb[:, 0]), rep(bb[:, 1]), E("attn_norm_w"), E("ffn_norm_w")] + [z] * 6
    D["vecs"] = np.stack(cols, axis=1)
    stack = lambda ws: np.stack(ws, axis=1)
    wck = L("Wck").T.reshape(128, 4, 128)
    wcv = L("Wcv").T.reshape(4, 128, 128).transpose(1, 0, 2)
    D["wL0"] = np.concatenate([stack([L("Wk").T, L("Wv").T, L("Wr").T, L("Wcr").T]), wck, wcv], axis=1)
    D["gate0"] = M("w_gate").T
    w1 = np.concatenate([M("w1_e").reshape(1024, 128), M("w1_s")]).T
    w3 = np.concatenate([M("w3_e").reshape(1024, 128), M("w3_s")]).T
    w2 = np.concatenate([M("w2_e").transpose(0, 2, 1).reshape(1024, 128), M("w2_s").T])
    D["w1"], D["w3"] = w1, w3
    D["w2"] = w2.reshape(9, 128, 128).transpose(1, 0, 2).reshape(128, 1152)
    sel = np.zeros((96, 8, 128), np.float32)
    for p in range(3):
        for e in range(16):
            sel[32 * p + e, e // 2, 64 * (e % 2):64 * (e % 2) + 64] = 1
    D["sel"] = sel.reshape(96, 1024).astype(bf)
    r = np.ones((128, 32, 16), np.float32)
    r[:, :, 0] = 0
    D["rst16"] = r.reshape(128, 512)
    D["rst8"] = r[:, :, :8].reshape(128, 256)
    D["rk0"] = np.broadcast_to(np.array([3, 2, 1, 0], np.float32), (128, 32, 4))
    perm = np.arange(128).reshape(16, 2, 4)[:, ::-1, :].reshape(128)
    wv = N("Wv").reshape(128, 16, 8)
    wvr = [np.repeat(wv[:, :, e], 8, axis=1) for e in range(8)]
    wb = N("Wbeta").reshape(128, 16, 2)
    wbr = [np.repeat(wb[:, :, c], 8, axis=1) for c in range(2)]
    D["wL1"] = stack([N("Wq"), N("Wq")[:, perm], N("Wk"), N("Wk")[:, perm]] + wvr + wbr)
    D["wo1"] = N("Wo")
    D["hsum"] = np.repeat(np.eye(16, 128, dtype=np.float32), 8, axis=0)
    D["rows"] = np.stack([np.broadcast_to(v, (128, 128)) for v in (N("bo"), N("ln_gamma"), N("ln_beta"))], axis=1)
    inv = (1.0 / 10000.0 ** (np.arange(0, 8, 2, dtype=np.float32) / np.float32(8))).astype(np.float32)
    fr = (np.arange(1024, dtype=np.float32)[:, None] * inv[None, :]).astype(np.float32)
    c, s = np.cos(fr).T, np.sin(fr).T
    D["rope"] = np.stack([np.tile(np.concatenate([c, c]), (16, 1)), np.tile(np.concatenate([-s, s]), (16, 1))],
                         axis=1).astype(np.float32)
    D["wqE"], D["wkE"], D["wvE"], D["woE"] = E("wq").T, E("wk").T, E("wv").T, E("wo").T
    D["gateE"] = E("gate_w").T
    D["wE"] = E("expert_w").transpose(2, 0, 1)
    low = np.arange(128)[:, None] >= np.arange(128)[None, :]
    D["msk"] = np.stack([np.where(low, 0, -1e30), np.where(low.T, 0, -1e30)], axis=1).astype(bf)
    D["zrow"] = np.zeros((3, 8, 1024), bf)
    D["zeros"], D["ones"] = np.zeros((8, 8, 1024), bf), np.ones((8, 4, 1024), bf)
    return {k: np.ascontiguousarray(v) for k, v in D.items()}


def kernel(**inputs):
    import concourse.bacc as bacc
    from concourse import mybir as mb
    from concourse.bass_utils import run_bass_kernel_spmd

    D = arrays(inputs)
    nc = bacc.Bacc("TRN2", target_bir_lowering=False, num_devices=1)
    I = {k: nc.dram_tensor(f"in_{k}", v.shape, mb.dt.from_np(v.dtype), kind="ExternalInput").ap()
         for k, v in D.items()}
    out = nc.dram_tensor("out_0_dram", (4096, 128), F32, kind="ExternalOutput").ap()
    build(nc, I, out, STOP)
    r = run_bass_kernel_spmd(nc, [{f"in_{k}": v for k, v in D.items()}], core_ids=[0])
    return r.results[0]["out_0_dram"].reshape(4, 1024, 128)
```

```python
from contextlib import ExitStack

import concourse.bass as bass
from concourse import mybir

F32 = mybir.dt.float32
BF = mybir.dt.bfloat16
ALU = mybir.AluOpType
ACT = mybir.ActivationFunctionType
AX = mybir.AxisListType.X

T = 4096
NT = 32
NG = 8


STOP = 9
SQA = (1, 3)
PGB, PUB, PDB = [2], [3], [1, 4, 5]
HGAP, H0, H1 = 7, 2, 3
GMOD, GSET, DL = 2, (0,), 3
P1B, PSB, OEB, PLAG = [2, 3, 4, 5], [0, 1], [6], 2
LAT, GC, MOST, PEN = 200, 950, 1.1, 400


class Line:

    def __init__(self, eng, sem):
        self.eng, self.sem, self.n, self.seen = eng, sem, 0, {}

    def on(self, *producers):
        need = {}
        for sem, count in producers:
            need[sem.num] = (sem, max(need.get(sem.num, (sem, 0))[1], count))
        for key, (sem, count) in need.items():
            if self.seen.get(key, 0) < count:
                self.eng.wait_ge(sem, count)
                self.seen[key] = count
        return self.eng

    def did(self, ins):
        self.n += 1
        ins.then_inc(self.sem, 1)
        return (self.sem, self.n)

    def last(self):
        return (self.sem, self.n)


class Ring:

    def __init__(self, bufs):
        self.bufs, self.i, self.freed = bufs, -1, [() for _ in bufs]
        self.when = [0.0] * len(bufs)

    def take(self):
        self.i = (self.i + 1) % len(self.bufs)
        return self.i, self.bufs[self.i], self.freed[self.i]

    def free(self, i, *readers, when=0.0):
        self.freed[i] = readers
        self.when[i] = when

    def next_free(self):
        return self.when[(self.i + 1) % len(self.bufs)]


def skewed(stages, n):
    most = max(lag for lag, _ in stages)
    for step in range(n + most):
        for lag, stage in reversed(stages):
            if 0 <= step - lag < n:
                stage(step - lag)


def build(nc, I, out, stop=9):
    ctx = ExitStack()
    with ctx:
        semn = [0]

        def sem(name):
            semn[0] += 1
            return ctx.enter_context(nc.semaphore(f"{name}_{semn[0]}"))

        def sb(name, shape, dt=F32):
            return ctx.enter_context(nc.sbuf_tensor(name, shape, dt))

        PE = Line(nc.tensor, sem("s_pe"))
        V = Line(nc.vector, sem("s_v"))
        A = Line(nc.scalar, sem("s_a"))
        G = Line(nc.gpsimd, sem("s_g"))
        SP = Line(nc.sync, sem("s_sp"))

        PS = ctx.enter_context(nc.psum_tensor("PS", [128, 8 * 512], F32))

        def bank(i, n=1):
            return PS[:, 512 * i:512 * (i + n)]

        def dma(dst, src, s, *producers):
            SP.on(*producers).dma_start(dst, src).then_inc(s, 16)
            return (s, 16)

        def barrier():
            marks = [x.last() for x in (PE, V, A, G) if x.n]
            for x in (PE, V, A, G, SP):
                x.on(*marks)

        s_c, s_c2 = sem("s_c"), sem("s_c2")
        loads = [0, 0]

        def load(name, shape, dt=F32, src=None):
            t = sb("w_" + name, shape, dt)
            k = 0 if name in ("ident", "vecs") else 1
            nc.scalar.dma_start(t[tuple(slice(None) for _ in shape)],
                                I[name] if src is None else src).then_inc((s_c, s_c2)[k], 16)
            loads[k] += 1
            return t

        X = sb("X", [128, NT, 128])
        XA = sb("XA", [128, NT, 128])
        B = [sb(f"B{i}", [128, 4096 + 4]) for i in range(6)]

        def full(i):
            return B[i][:, 0:4096]

        def tm(i):
            return B[i][:, 0:4096].rearrange("p (i c) -> p i c", c=128)

        def seq(i):
            return B[i][:, 0:4100].rearrange("p (b t) -> p b t", b=4)

        RB = sb("RB", [128, 16, 512])
        xin = I["x"].rearrange("(i p) c -> p i c", p=128)
        s_x = [sem("s_x") for _ in range(NG)]
        for g in range(NG):
            nc.sync.dma_start(X[:, 4 * g:4 * g + 4, :], xin[:, 4 * g:4 * g + 4, :]).then_inc(s_x[g], 16)
        ident = load("ident", [128, 128])
        vecs = load("vecs", [128, 16])
        WW = sb("WW", [128, 14, 128])
        wA, wck, wcv = WW[:, 0:4, :], WW[:, 4:8, :], WW[:, 8:12, :]
        nc.scalar.dma_start(WW[:, 0:12, :], I["wL0"]).then_inc(s_c, 16)
        loads[0] += 1
        gate0 = load("gate0", [128, 16])
        identb = load("identb", [128, 128], BF)
        rst16 = load("rst16", [128, NT * 16])
        rk0 = load("rk0", [128, NT, 4])
        wq4, wvr, wbr = WW[:, 0:4, :], WW[:, 4:12, :], WW[:, 12:14, :]
        wo1 = load("wo1", [128, 128])
        hsum = load("hsum", [128, 128])
        rows = load("rows", [128, 3, 128])
        wqE = load("wqE", [128, 128])
        wkE = load("wkE", [128, 32])
        wvE = load("wvE", [128, 32])
        woE = load("woE", [128, 128])
        gateE = load("gateE", [128, 8])
        wE = WW[:, 0:8, :]
        rst8 = load("rst8", [128, NT * 8])
        msk = load("msk", [128, 128], BF)
        W_READY, W_REST = (s_c, 16 * loads[0]), (s_c2, 16 * loads[1])
        dv = sb("dv", [128, 3])
        (LN1W, LN1B, LN2W, LN2B, TS, _, _, _, ANW, FNW) = [vecs[:, j:j + 1] for j in range(10)]
        HU, HBB0, HBB1 = [dv[:, j:j + 1] for j in range(3)]

        st = sb("st", [128, NT, 6])
        mv = [sb(f"mv{i}", [128, NT, 2]) for i in range(2)]
        rs = [sb(f"rs{i}", [128, NT, 6]) for i in range(2)]
        mhalf = sb("mhalf", [128, 8])
        G_half = G.did(nc.gpsimd.memset(mhalf[:, :], -0.5))
        for x in (PE, A, G):
            x.on(W_READY)

        def stats(g, src, k, *producers):
            toks = []
            for i in range(4 * g, 4 * g + 4):
                t = V.did(V.on(*producers).bn_stats(st[:, i, :], src(i)))
                toks.append(t)
            for i in range(4 * g, 4 * g + 4):
                t = V.did(V.on(toks[i - 4 * g]).bn_aggr(mv[k][:, i, :], st[:, i, :]))
            return t

        def rstd(g, k, eps, t_stats, then=None):
            s4 = slice(4 * g, 4 * g + 4)
            R = rs[k]
            v = mv[k][:, s4, 1]
            t = G.did(G.on(t_stats).tensor_scalar(R[:, s4, 3], v, eps, None, ALU.add))
            t = G.did(G.on(t, G_half).tensor_tensor(R[:, s4, 0], R[:, s4, 3], mhalf[:, 0:4], ALU.pow))
            t0 = t
            t = G.did(G.on(t).tensor_tensor(R[:, s4, 4], mv[k][:, s4, 0], R[:, s4, 0], ALU.mult))
            t = G.did(G.on(t).tensor_scalar(R[:, s4, 1], R[:, s4, 4], -1.0, None, ALU.mult))
            if then is not None:
                t = G.did(G.on(t0).tensor_tensor(R[:, s4, 5], v, R[:, s4, 0], ALU.mult))
                t = G.did(G.on(t).tensor_tensor(R[:, s4, 2], R[:, s4, 5], R[:, s4, 0], ALU.mult))
                t = G.did(G.on(t).tensor_scalar(R[:, s4, 5], R[:, s4, 2], then, None, ALU.add))
                t = G.did(G.on(t).tensor_tensor(R[:, s4, 2], R[:, s4, 5], mhalf[:, 0:4], ALU.pow))
            return t

        def normed(i, k, dst, src, *producers):
            return A.did(A.on(*producers).activation(dst, src, ACT.Identity, bias=rs[k][:, i, 1:2],
                                                     scale=rs[k][:, i, 0:1]))

        def transposes(dst, src, idn, *producers):
            for j in range(4):
                t = PE.did(PE.on(*producers).transpose(dst[:, 128 * j:128 * j + 128], src(j), idn[:, :]))
            return t

        def rb(i, n=1):
            return RB[:, i:i + n, :]

        HF, XXX, KF, VF, RF, MM = 0, 1, 2, 3, 4, 5
        hf, mm_ = seq(HF), seq(MM)
        SS = ctx.enter_context(nc.sbuf_tensor("SS", [128, 4100], F32))
        ss = SS[:, :].rearrange("p (b t) -> p b t", b=4)
        rHN = Ring([rb(0), rb(1)])
        rD = Ring([rb(2, 2), rb(4, 2)])
        rE = Ring([rb(6, 2), rb(8, 2)])
        pT = Ring([bank(0), bank(1)])
        pP = Ring([bank(i) for i in range(2, 8)])

        def ch(ap4, g, shift=0):
            b, h = g // 2, g % 2
            o = 1 + 512 * h - shift
            return ap4[:, b, o:o + 512]

        def cf(i, g):
            return B[i][:, 512 * g:512 * g + 512]

        t_init = []
        for b in range(4):
            t_init.append(G.did(G.on().tensor_copy(hf[:, b, 0:1], TS)))
            t_init.append(G.did(nc.gpsimd.memset(mm_[:, b, 0:1], 0.0)))
            t_init.append(G.did(nc.gpsimd.memset(ss[:, b, 0:1], 1.0)))
        t_init = t_init[-1]
        K = {}

        def a_stats(g):
            K["st", g] = rstd(g, 0, 1e-5, stats(g, lambda i: X[:, i, :], 0, (s_x[g], 16)), then=1e-5)

        def a_norm(g):
            ib, buf, fr = rHN.take()
            for j in range(4):
                i = 4 * g + j
                t = V.did(V.on(K["st", g]).tensor_scalar(XA[:, i, :], X[:, i, :], mv[0][:, i, 0:1],
                                                         rs[0][:, i, 0:1], ALU.subtract, ALU.mult))
                t = A.did(A.on(t, *fr).activation(buf[:, 0, 128 * j:128 * j + 128], XA[:, i, :], ACT.Copy,
                                                  scale=rs[0][:, i, 2:3]))
            K["hn", g] = (ib, buf, t)

        def a_turn(g):
            ib, buf, t = K["hn", g]
            pi, p, fr = pT.take()
            t = transposes(p, lambda j: buf[:, 0, 128 * j:128 * j + 128], ident, t, *fr)
            rHN.free(ib, t)
            t = V.did(V.on(t, t_init, W_READY).tensor_scalar(ch(hf, g), p, LN1W, LN1B, ALU.mult, ALU.add))
            pT.free(pi, t)
            K["hf", g] = t

        def a_mix(g):
            ib, buf, fr = rD.take()
            t = V.did(V.on(K["hf", g], *fr).tensor_tensor(buf[:, 0, :], ch(hf, g), ch(hf, g, 1), ALU.subtract))
            t = V.did(V.on(t).scalar_tensor_tensor(cf(XXX, g), buf[:, 0, :], TS, ch(hf, g), ALU.mult, ALU.add))
            rD.free(ib, t)
            K["xxx", g] = t

        def a_proj(g):
            for w in range(3):
                pi, p, fr = pP.take()
                t = PE.did(PE.on(K["xxx", g], *fr).matmul(p, wA[:, w, :], cf(XXX, g), start=True, stop=True))
                if w < 2:
                    t = A.did(A.on(t).activation(cf((KF, VF)[w], g), p, ACT.Copy))
                else:
                    t = A.did(A.on(t).activation(cf(RF, g), p, ACT.Tanh, scale=0.5))
                pP.free(pi, t)
                K["krv"[w], g] = t
            K["kv", g] = t

        def a_scan(g):
            b, h = g // 2, g % 2
            o = 512 * h
            k = cf(KF, g)
            t = V.did(V.on(K["k", g], t_init, *([K["m", g - 1]] if h else [])).tensor_tensor_scan(
                ch(mm_, g), k, k, mm_[:, b, o:o + 1], ALU.max, ALU.max))
            K["m", g] = t
            ib, buf, fr = rD.take()
            V.did(V.on(t, *fr).tensor_tensor(buf[:, 0, :], ch(mm_, g, 1), ch(mm_, g), ALU.subtract))
            t = V.did(V.on(t).tensor_tensor(buf[:, 1, :], k, ch(mm_, g), ALU.subtract))
            ie, eb, fr = rE.take()
            t = A.did(A.on(t, *fr).activation(eb, buf, ACT.Exp))
            rD.free(ib, t)
            K["ex", g] = (ie, eb, t)

        def a_sum(g):
            b, h = g // 2, g % 2
            o = 512 * h
            ie, eb, t = K["ex", g]
            t = V.did(V.on(t, *([K["s", g - 1]] if h else [])).tensor_tensor_scan(
                ch(ss, g), eb[:, 0, :], eb[:, 1, :], ss[:, b, o:o + 1], ALU.mult, ALU.add))
            K["s", g] = t
            rE.free(ie, t)

        skewed([(0, a_stats), (1, a_norm), (2, a_turn), (3, a_mix), (4, a_proj), (6, a_scan), (7, a_sum)], NG)

        for x in (PE, V, A, G):
            x.on(W_REST)
        t_dv = V.did(nc.vector.tensor_scalar(dv[:, :], vecs[:, 5:8], 0.5, None, ALU.mult))
        A.on(t_dv)

        for b in range(4):
            t = A.did(A.on(K["s", 2 * b + 1]).activation(ss[:, b, :], ss[:, b, :], ACT.Ln))
            K["bb", b] = V.did(V.on(t, K["m", 2 * b + 1]).tensor_tensor(mm_[:, b, :], mm_[:, b, :], ss[:, b, :], ALU.add))
        t_aa0 = []
        for b in range(4):
            t_aa0 = G.did(G.on(K["bb", b]).memset(ss[:, b, 0:1], 0.0))

        rY = Ring([rb(10), rb(11)])
        rT = Ring([rb(12), rb(13)])
        rHN.freed = [(A.last(),), (A.last(),)]

        def b_decay(g):
            b = g // 2
            ib, buf, fr = rD.take()
            ie, eb, fe = rE.take()
            it, tb, ft = rT.take()
            t = V.did(V.on(K["bb", b], *fe).tensor_tensor(eb[:, 0, :], cf(KF, g), ch(mm_, g, 1), ALU.subtract))
            tt = A.did(A.on(t, *ft).activation(tb[:, 0, :], eb[:, 0, :], ACT.Tanh, scale=0.5, bias=HU))
            V.did(V.on(t, *fr).tensor_scalar(buf[:, 0, :], eb[:, 0, :], 0.0, None, ALU.min))
            t = V.did(V.on(t).tensor_scalar(buf[:, 1, :], eb[:, 0, :], 0.0, -1.0, ALU.max, ALU.mult))
            t = A.did(A.on(t, tt).activation(eb, buf, ACT.Exp))
            rD.free(ib, t)
            K["e", g] = (ie, eb, t, it, tb, tt)

        def b_wkv(g):
            b, h = g // 2, g % 2
            o = 512 * h
            ie, eb, t, it, tb, tt = K["e", g]
            ib, buf, fr = rD.take()
            iy, yb, fy = rY.take()
            t = V.did(V.on(t, *fr).tensor_tensor(buf[:, 0, :], eb[:, 0, :], cf(VF, g), ALU.mult))
            t = V.did(V.on(t, t_aa0, *([K["aa", g - 1]] if h else [])).tensor_tensor_scan(
                ch(ss, g), eb[:, 1, :], buf[:, 0, :], ss[:, b, o:o + 1], ALU.mult, ALU.add))
            K["aa", g] = t
            rE.free(ie, t)
            t = V.did(V.on(t).tensor_tensor(buf[:, 1, :], cf(VF, g), ch(ss, g, 1), ALU.subtract))
            t = V.did(V.on(t, tt).scalar_tensor_tensor(buf[:, 0, :], tb[:, 0, :], 1.0, buf[:, 1, :], ALU.add, ALU.mult))
            rT.free(it, t)
            t = V.did(V.on(t).scalar_tensor_tensor(buf[:, 1, :], buf[:, 0, :], 0.5, ch(ss, g, 1), ALU.mult, ALU.add))
            t = V.did(V.on(t, *fy).scalar_tensor_tensor(yb[:, 0, :], cf(RF, g), 1.0, buf[:, 1, :], ALU.add, ALU.mult))
            rD.free(ib, t)
            K["y", g] = (iy, yb, t)
            K["wkv", g] = K["done"] = t

        def b_res(g):
            iy, yb, t = K["y", g]
            pi, p, fr = pT.take()
            t = transposes(p, lambda j: yb[:, 0, 128 * j:128 * j + 128], ident, t, *fr)
            rY.free(iy, t)
            xa = XA[:, 4 * g:4 * g + 4, :].rearrange("p i c -> p (i c)")
            t = V.did(V.on(t).scalar_tensor_tensor(xa, p, 0.5, xa, ALU.mult, ALU.add))
            pT.free(pi, t)
            K["st", g] = rstd(g, 0, 1e-5, stats(g, lambda i: XA[:, i, :], 0, t))

        def b_norm(g):
            ib, buf, fr = rHN.take()
            for j in range(4):
                i = 4 * g + j
                t = normed(i, 0, buf[:, 0, 128 * j:128 * j + 128], XA[:, i, :], K["st", g], *fr)
            K["hn", g] = (ib, buf, t)

        def b_turn(g):
            ib, buf, t = K["hn", g]
            pi, p, fr = pT.take()
            t = transposes(p, lambda j: buf[:, 0, 128 * j:128 * j + 128], ident, t, *fr)
            rHN.free(ib, t)
            t = V.did(V.on(t).tensor_scalar(ch(hf, g), p, LN2W, LN2B, ALU.mult, ALU.add))
            pT.free(pi, t)
            if g % 2:
                b = g // 2
                t = V.did(V.on(t).tensor_copy(hf[:, b, 0:1], hf[:, b, 1024:1025]))
            K["hf", g] = t

        def b_mix(g):
            ib, buf, fr = rD.take()
            t = V.did(V.on(K["hf", g | 1], *fr).tensor_tensor(buf[:, 0, :], ch(hf, g, 1), ch(hf, g), ALU.subtract))
            t = V.did(V.on(t).scalar_tensor_tensor(cf(XXX, g), buf[:, 0, :], TS, ch(hf, g), ALU.mult, ALU.add))
            rD.free(ib, t)
            K["xxx", g] = t
            K["mixed", max(g - 1, 0)] = K["mixed", g] = (t,)

        def b_kc(g):
            o = (g % 2) * 2048
            rl = B[KF][:, o:o + 2048]
            sq = B[VF][:, o:o + 2048]
            for c in range(4):
                pi, p, fr = pP.take()
                t = PE.did(PE.on(K["xxx", g], *fr).matmul(p, wck[:, c, :], cf(XXX, g), start=True, stop=True))
                t = A.did(A.on(t, K["aa", NG - 1 if g else 3], *K.get(("sqd", g - 2), ())).activation(
                    rl[:, 512 * c:512 * c + 512], p, ACT.Relu))
                pP.free(pi, t)
                part = slice(512 * c, 512 * c + 512)
                need = (K["done"] if g else K["wkv", 3], *K.get(("vvd", g - 2), ()))
                if c in SQA:
                    t = A.did(A.on(t, *need).activation(sq[:, part], rl[:, part], ACT.Square))
                else:
                    t = G.did(G.on(t, *need).tensor_tensor(sq[:, part], rl[:, part], rl[:, part], ALU.mult))
                K["sq", g, c] = t
            K["sqd", g] = (G.last(),)
            pi, p, fr = pP.take()
            t = PE.did(PE.on(*fr).matmul(p, wA[:, 3, :], cf(XXX, g), start=True, stop=True))
            it, tb, ft = rT.take()
            t = A.did(A.on(t, *ft).activation(tb[:, 0, :], p, ACT.Tanh, scale=0.5))
            pP.free(pi, t)
            K["rc", g] = (it, tb, t)

        def b_vv(g):
            o = (g % 2) * 2048
            sq = B[VF][:, o:o + 2048]
            pi, p, fr = pP.take()
            for c in range(4):
                t = PE.did(PE.on(K["sq", g, c], *fr).matmul(p, wcv[:, c, :], sq[:, 512 * c:512 * c + 512],
                                                            start=(c == 0), stop=(c == 3)))
            K["vvd", g] = (t,)
            it, tb, tt = K["rc", g]
            iy, yb, fy = rY.take()
            t = V.did(V.on(t, tt, *fy).scalar_tensor_tensor(yb[:, 0, :], tb[:, 0, :], 1.0, p, ALU.add, ALU.mult))
            pP.free(pi, t)
            rT.free(it, t)
            K["y", g] = (iy, yb, t)

        def b_ret(g):
            iy, yb, t = K["y", g]
            pi, p, fr = pT.take()
            t = transposes(p, lambda j: yb[:, 0, 128 * j:128 * j + 128], ident, t, *fr)
            rY.free(iy, t)
            xa = XA[:, 4 * g:4 * g + 4, :].rearrange("p i c -> p (i c)")
            t = V.did(V.on(t).scalar_tensor_tensor(xa, p, 0.5, xa, ALU.mult, ALU.add))
            pT.free(pi, t)
            K["st", g] = rstd(g, 1, 1e-5, stats(g, lambda i: XA[:, i, :], 1, t))

        rX = Ring([rb(14), rb(15)])

        def add_normed(g, k, src, *producers):
            ix, xb, fr = rX.take()
            for j in range(4):
                t = normed(4 * g + j, k, xb[:, 0, 128 * j:128 * j + 128], src(4 * g + j), *producers, *fr)
            ta = t
            x = X[:, 4 * g:4 * g + 4, :].rearrange("p i c -> p (i c)")
            t = G.did(G.on(t).tensor_tensor(x, x, xb[:, 0, :], ALU.add))
            rX.free(ix, t)
            K["x", g] = t
            return ta

        def b_add(g):
            add_normed(g, 1, lambda i: XA[:, i, :], K["st", g])

        s_wm = sem("s_wm")
        T_WM = (s_wm, 64)
        C3 = B[5][:, 2048:3584].bitcast(BF).rearrange("p (i a e) -> p i a e", a=3, e=32)

        def b_load(g):
            if g == 0:
                for i, name in enumerate(("w1", "w3", "w2")):
                    dma(B[4][:, 1152 * i:1152 * i + 1152], I[name], s_wm, K["done"])
                dma(B[4][0:96, 3456:3968].bitcast(BF), I["sel"], s_wm)
                K["c3"] = G.did(G.on(K["done"]).memset(C3[:, :, :, :].rearrange("p i a e -> p (i a e)"), 0.0))

        b_stages = [(0, b_decay), (1, b_wkv), (2, b_res), (3, b_norm), (4, b_turn), (6, b_mix), (8, b_kc), (9, b_load),
                    (9, b_vv), (10, b_ret), (11, b_add)]

        def finish():
            s_o = [sem("s_o") for _ in range(NG)]
            oo = out.rearrange("(i p) c -> p i c", p=128)
            for g in range(NG):
                dma(oo[:, 4 * g:4 * g + 4, :], X[:, 4 * g:4 * g + 4, :], s_o[g], K["x", g])
            for g in range(NG):
                SP.on((s_o[g], 16))

        if stop == 1:
            skewed(b_stages, NG)
            finish()
            return

        XF = 0
        t_lg = [pP.freed[0], pP.freed[1]]
        freed = pP.freed[2:]
        pP = Ring([bank(i) for i in range(4, 8)])
        pP.freed = freed

        def n_stats(g):
            K["st", g] = rstd(g, 0, 1e-5, stats(g, lambda i: X[:, i, :], 0, K["x", g]))

        def n_norm(g):
            ib, buf, fr = rHN.take()
            for j in range(4):
                i = 4 * g + j
                t = normed(i, 0, buf[:, 0, 128 * j:128 * j + 128], X[:, i, :], K["st", g], *fr)
            K["hn", g] = (ib, buf, t)

        def n_turn(g):
            ib, buf, t = K["hn", g]
            pi, p, fr = pT.take()
            t = transposes(p, lambda j: buf[:, 0, 128 * j:128 * j + 128], ident, t, *fr)
            rHN.free(ib, t)
            t = A.did(A.on(t, *K.get(("mixed", g), ())).activation(cf(XF, g), p, ACT.Copy))
            pT.free(pi, t)
            K["xf", g] = t

        SC = sb("SC", [128, NT, 16])
        small = [SS[:, 512 * i:512 * i + 512].rearrange("p (i e) -> p i e", e=16) for i in range(4)]
        sv = SS[:, 2048:3584].rearrange("p (n i q) -> p n i q", i=NT, q=4)
        T8 = SS[:, 3584:3840].rearrange("p (i e) -> p i e", e=8)
        CFb = B[5][0:96, 0:2048].bitcast(BF)
        wm = [B[4][:, 1152 * i:1152 * i + 1152].rearrange("p (j c) -> p j c", c=128) for i in range(3)]
        w1, w3, w2 = wm
        sel = B[4][0:96, 3456:3968].bitcast(BF).rearrange("p (j c) -> p j c", c=128)

        def n_gate(g):
            for j in range(4):
                t = PE.did(PE.on(K["xf", g], *t_lg[g // 4]).matmul(
                                                    bank(2 + g // 4)[:, 16 * (4 * (g % 4) + j):][:, 0:16],
                                                    cf(XF, g)[:, 128 * j:128 * j + 128], gate0[:, :],
                                                    start=True, stop=True, skip_group_check=True))
            K["lg", g] = t

        def vt(o, a, b, op, *w):
            return V.did(V.on(*w).tensor_tensor(o, a, b, op))

        def pick(S, th, k, E, reset, tmp, left, need, t, nt=NT):
            f = lambda z: z.rearrange("p i e -> p (i e)")
            thb = th.to_broadcast([128, nt, E])
            gt, eq, pc = tmp
            t = vt(gt, S, thb, ALU.is_gt, t)
            t = V.did(V.on(t).tensor_reduce(left.rearrange("p i a -> p (i a)"), gt, AX, ALU.add))
            t = V.did(V.on(t).tensor_scalar(need, left, -1.0, float(k), ALU.mult, ALU.add))
            t2 = vt(eq, S, thb, ALU.is_equal, t)
            t = V.did(V.on(t2).tensor_tensor_scan(f(pc), reset[:, 0:nt * E], f(eq), 0.0, ALU.mult, ALU.add))
            t = vt(pc, pc, need.to_broadcast([128, nt, E]), ALU.is_le, t)
            t = vt(eq, eq, pc, ALU.mult, t)
            return vt(gt, gt, eq, ALU.add, t)

        def route(r):
            sl = slice(16 * r, 16 * r + 16)
            S = SC[:, sl, :]
            fl = lambda z: z.rearrange("p i e -> p (i e)")
            t_sc = A.did(A.on(K["lg", 4 * r + 3]).activation(fl(S), bank(2 + r)[:, 0:256], ACT.Sigmoid))
            K["sc", r] = t_sc
            yield
            sm = [small[q][:, sl, :] for q in range(4)]
            sp = S.rearrange("p i (q a b) -> p (i q) a b", a=2, b=2)
            pr = fl(sm[0])
            hi = pr[:, 0:128].rearrange("p (n a) -> p n a", a=2)
            lo = pr[:, 128:256].rearrange("p (n a) -> p n a", a=2)
            svf = lambda n: sv[:, n, sl, :].rearrange("p i q -> p (i q)")
            vt(hi, sp[:, :, :, 0], sp[:, :, :, 1], ALU.max, t_sc)
            t = vt(lo, sp[:, :, :, 0], sp[:, :, :, 1], ALU.min, t_sc)
            vt(svf(0), hi[:, :, 0], hi[:, :, 1], ALU.max, t)
            vt(svf(1), hi[:, :, 0], hi[:, :, 1], ALU.min, t)
            t = vt(svf(2), lo[:, :, 0], lo[:, :, 1], ALU.max, t)
            yield
            t = vt(svf(3), svf(1), svf(2), ALU.max, t)
            t = vt(svf(4), svf(0), svf(3), ALU.add, t)
            gs = sv[:, 4, sl, :]
            for d in (1, 2, 3):
                t = vt(sv[:, 4 + d, sl, 0:4 - d], gs[:, :, 0:4 - d], gs[:, :, d:4], ALU.is_ge, t)
            yield
            t = V.did(V.on(t).tensor_copy(sv[:, 8, sl, :], rk0[:, 0:16, :]))
            for d in (1, 2, 3):
                t = vt(sv[:, 8, sl, d:4], sv[:, 8, sl, d:4], sv[:, 4 + d, sl, 0:4 - d], ALU.add, t)
                t = vt(sv[:, 8, sl, 0:4 - d], sv[:, 8, sl, 0:4 - d], sv[:, 4 + d, sl, 0:4 - d], ALU.subtract, t)
                yield
            t = V.did(V.on(t).tensor_scalar(svf(9), svf(8), 2.0, None, ALU.is_lt))
            t = V.did(V.on(t).tensor_scalar(svf(0), svf(9), -1.0, None, ALU.add))
            four = lambda z: z.rearrange("p i (q e) -> p (i q) e", e=4)
            bc4 = lambda n: svf(n).unsqueeze(2).to_broadcast([128, 64, 4])
            t = vt(four(sm[1]), four(S), bc4(9), ALU.mult, t)
            t = vt(four(sm[1]), four(sm[1]), bc4(0), ALU.add, t)
            for i in range(16):
                if i % 4 == 0:
                    yield
                tm8 = V.did(V.on(t).max(T8[:, 16 * r + i, :], sm[1][:, i, :]))
            yield
            t = pick(sm[1], T8[:, sl, 3:4], 4, 16, rst16, (sm[0], sm[2], sm[3]),
                     sv[:, 10, sl, 0:1], sv[:, 11, sl, 0:1], tm8, nt=16)
            yield
            t = vt(sm[2], sm[0], S, ALU.mult, t)
            wsum = sv[:, 0, sl, 0:1]
            t = V.did(V.on(t).tensor_reduce(wsum.rearrange("p i a -> p (i a)"), sm[2], AX, ALU.add))
            t = V.did(V.on(t).tensor_scalar(sv[:, 1, sl, 0:1], wsum, 1e-6, None, ALU.add))
            t = V.did(V.on(t).reciprocal(sv[:, 2, sl, 0:1], sv[:, 1, sl, 0:1]))
            t = vt(sm[1], sm[2], sv[:, 2, sl, 0:1].to_broadcast([128, 16, 16]), ALU.mult, t)
            yield
            t = V.did(V.on(t, K["c3"]).tensor_copy(C3[:, sl, 0, 0:16], sm[1]))
            t = vt(sm[2], sm[1], C3[:, sl, 0, 0:16], ALU.subtract, t)
            t = V.did(V.on(t).tensor_copy(C3[:, sl, 1, 0:16], sm[2]))
            t = vt(sm[3], sm[2], C3[:, sl, 1, 0:16], ALU.subtract, t)
            t_cut = V.did(V.on(t).tensor_copy(C3[:, sl, 2, 0:16], sm[3]))
            yield
            for g in range(4 * r, 4 * r + 4):
                ring = pC if "moe" in K else pT
                pi, p, fr = ring.take()
                pb = p.bitcast(BF)
                for j in range(4):
                    i = 4 * g + j
                    t = PE.did(PE.on(t_cut, *fr).transpose(pb[0:96, 128 * j:128 * j + 128],
                                                           C3[:, i, :, :].rearrange("p a e -> p (a e)"), identb[:, :]))
                t = V.did(V.on(t).tensor_copy(CFb[:, 512 * g:512 * g + 512], pb[0:96, 0:512]))
                ring.free(pi, t)
                K["cf", g] = t
                yield

        routes = [route(0), route(1)]

        def n_route(g):
            if g >= 3:
                for _ in range(4):
                    next(routes[0], None)

        skewed(b_stages + [(12, n_stats), (13, n_norm), (14, n_turn), (15, n_gate), (16, n_route)], NG)
        t_ww = dma(WW[:, :, :], I["wL1"], sem("s_ww"), PE.last())
        for _ in routes[0]:
            pass
        next(routes[1])
        barrier()
        K["moe"] = True

        pG = Ring([bank(i) for i in PGB])
        pU = Ring([bank(i) for i in PUB])
        pC = Ring([bank(0)])
        pD = Ring([bank(i) for i in PDB])
        pO = Ring([bank(6), bank(7)])
        rS = Ring([rb(0), rb(1), rb(2)])
        rT1 = Ring([rb(3), rb(4)])
        rT2 = Ring([rb(5), rb(6), rb(7)])

        def m_gu(n):
            g, j = divmod(n, 9)
            gi, pg, fr = pG.take()
            tg = PE.did(PE.on(T_WM, *fr).matmul(pg, w1[:, j, :], cf(XF, g), start=True, stop=True))
            ui, pu, fr = pU.take()
            tu = PE.did(PE.on(*fr).matmul(pu, w3[:, j, :], cf(XF, g), start=True, stop=True))
            si, sbuf, fr = rS.take()
            t = A.did(A.on(tg, *fr).activation(sbuf[:, 0, :], pg, ACT.Silu))
            pG.free(gi, t)
            if j < 8:
                ci, pc, fr = pC.take()
                tc = PE.did(PE.on(K["cf", g], *fr).matmul(pc, sel[:, j, :], CFb[:, 512 * g:512 * g + 512],
                                                          start=True, stop=True))
                i1, b1, f1 = rT1.take()
                t = V.did(V.on(t, tu, *f1).tensor_tensor(b1[:, 0, :], sbuf[:, 0, :], pu, ALU.mult))
                rS.free(si, t)
                pU.free(ui, t)
                i2, b2, f2 = rT2.take()
                t = V.did(V.on(t, tc, *f2).tensor_tensor(b2[:, 0, :], b1[:, 0, :], pc, ALU.mult))
                pC.free(ci, t)
            else:
                i2, b2, f2 = rT2.take()
                t = V.did(V.on(t, tu, *f2).tensor_tensor(b2[:, 0, :], sbuf[:, 0, :], pu, ALU.mult))
                rS.free(si, t)
                pU.free(ui, t)
            K["t2", n] = (i2, b2, t)

        def m_out(n):
            g, j = divmod(n, 9)
            if j == 0:
                K["o", g] = pO.take()
            oi, po, fr = K["o", g]
            i2, b2, t = K["t2", n]
            for q in range(4):
                tp = PE.did(PE.on(t, *(fr if j == 0 else ())).matmul(
                    po[:, 128 * q:128 * q + 128], b2[:, 0, 128 * q:128 * q + 128], w2[:, j, :],
                    start=(j == 0 and q == 0), stop=(j == 8), skip_group_check=True))
            rT2.free(i2, tp)
            if j == 8:
                ts_ = stats(g, lambda i: po[:, 128 * (i - 4 * g):128 * (i - 4 * g) + 128], 1, tp)
                t = rstd(g, 1, 1e-5, ts_)
                t = add_normed(g, 1, lambda i: po[:, 128 * (i - 4 * g):128 * (i - 4 * g) + 128], t)
                pO.free(oi, t)
                K["x1", g] = True

        rHN = Ring([rb(8), rb(9)])
        QF, KF, NUM = 1, 2, 5
        BETA = [B[3], SS]
        cs = B[5][:, 2048:4096].rearrange("p (a t) -> p a t", a=2)
        rq = Ring([rb(10, 2), rb(12, 2)])

        def d_head(g):
            h = g % 2
            c5 = slice(512 * g, 512 * g + 512)
            for _ in range(H0):
                yield
            n_stats(g)
            for _ in range(H1):
                yield
            n_norm(g)
            ib, buf, t = K["hn", g]
            tg = t
            for j in range(4):
                tg = G.did(G.on(tg).tensor_tensor(XA[:, 4 * g + j, :], buf[:, 0, 128 * j:128 * j + 128],
                                                  rows[:, 0, :], ALU.add))
            K["xb", g] = tg
            yield
            pi, p, fr = pD.take()
            t = transposes(p, lambda j: buf[:, 0, 128 * j:128 * j + 128], ident, t, *fr)
            rHN.free(ib, t, tg)
            t = A.did(A.on(t).activation(cf(XF, g), p, ACT.Copy))
            pD.free(pi, t)
            K["xf", g] = t
            yield
            late = []
            for w in range(2):
                iq, qb, fq = rq.take()
                pi, p, fr = pD.take()
                t = PE.did(PE.on(K["xf", g], t_ww, *fr).matmul(p, wq4[:, 2 * w, :], cf(XF, g), start=True, stop=True))
                t1 = vt(qb[:, 0, :], p, cs[:, 0, 512 * h:512 * h + 512], ALU.mult, t, K["cs"], *fq)
                pD.free(pi, t1)
                while late:
                    late.pop()()
                yield
                pi, p, fr = pD.take()
                t = PE.did(PE.on(*fr).matmul(p, wq4[:, 2 * w + 1, :], cf(XF, g), start=True, stop=True))
                t2 = vt(qb[:, 1, :], p, cs[:, 1, 512 * h:512 * h + 512], ALU.mult, t)
                pD.free(pi, t2)
                t = vt(qb[:, 0, :], qb[:, 0, :], qb[:, 1, :], ALU.add, t1, t2)
                te = A.did(A.on(t).activation(qb[:, 1, :], qb[:, 0, :], ACT.Exp))
                te = A.did(A.on(te).activation(qb[:, 0, :], qb[:, 0, :], ACT.Relu))

                def feature(w=w, iq=iq, qb=qb, te=te):
                    t = V.did(V.on(te).scalar_tensor_tensor(cf((QF, KF)[w], g), qb[:, 1, :], 1.0, qb[:, 0, :],
                                                            ALU.min, ALU.add))
                    rq.free(iq, t)
                late.append(feature)
                yield
            for w in range(2):
                pi, p, fr = pD.take()
                t = PE.did(PE.on(*fr).matmul(p, wbr[:, w, :], cf(XF, g), start=True, stop=True))
                d = BETA[w][:, c5]
                tb = A.did(A.on(t, K["route"]).activation(d, p, ACT.Tanh, scale=0.5, bias=(HBB0, HBB1)[w]))
                pD.free(pi, tb)
                while late:
                    late.pop()()

                def gate(d=d, tb=tb):
                    t = V.did(V.on(tb).tensor_scalar(d, d, 0.5, 0.5, ALU.mult, ALU.add))
                    V.did(V.on(t).tensor_scalar(d, d, 0.001, 0.999, ALU.max, ALU.min))
                late.append(gate)
                yield
            while late:
                late.pop()()

        heads_d, done_d = [], [0]

        def m_route(n):
            if n >= 4:
                for _ in range(2):
                    if "route" not in K and next(routes[1], "end") == "end":
                        K["route"] = V.last()
                        K["cs"] = dma(cs, I["rope"], sem("s_cs"), PE.last(), V.last())
            step_heads(n)

        def step_heads(n):
            g = done_d[0]
            if "route" in K and g < NG and ("x1", g) in K and n >= K.get("head at", 0):
                heads_d.append(d_head(g))
                done_d[0] += 1
                K["head at"] = n + HGAP
            for z in list(heads_d):
                if next(z, "end") == "end":
                    heads_d.remove(z)

        if stop > 2:
            skewed([(0, m_gu), (1, m_route), (2, m_out)], 9 * NG)
        else:
            def only_route(n):
                if n >= 4:
                    next(routes[1], None)
            skewed([(0, m_gu), (1, only_route), (2, m_out)], 9 * NG)
            finish()
            return
        old_d = pD.freed
        pD = Ring(pD.bufs + pG.bufs + pU.bufs + pC.bufs)
        pD.freed = old_d + pG.freed + pU.freed + pC.freed
        last = []
        while heads_d or last or done_d[0] < NG:
            if heads_d:
                last.append(heads_d.pop(0))
            if done_d[0] < NG and len(last) < 2:
                last.append(d_head(done_d[0]))
                done_d[0] += 1
            for z in list(last):
                if next(z, "end") == "end":
                    last.remove(z)

        num = full(NUM).rearrange("p (i h e) -> p i h e", h=16, e=8)
        DEN = SC
        ring2 = lambda a: Ring([rb(a, 2).rearrange("p a t -> p (a t)"), rb(a + 2, 2).rearrange("p a t -> p (a t)")])
        rO = Ring(ring2(0).bufs + [B[4][:, 2048:3072], B[4][:, 3072:4096]])
        rM0 = ring2(4)
        rM1 = ring2(8)
        rP = ring2(12)
        rQ = Ring([B[4][:, 0:1024], B[4][:, 1024:2048]])
        pV = Ring([bank(4, 2), bank(6, 2)])
        pN = Ring([bank(0, 2), bank(2, 2)])
        barrier()

        def d_value(n):
            e, b = divmod(n, 4)
            if e == 8:
                return
            pi, p, fr = pV.take()
            for h in range(2):
                t = PE.did(PE.on(*fr).matmul(p[:, 512 * h:512 * h + 512], wvr[:, e, :],
                                             B[XF][:, 1024 * b + 512 * h:1024 * b + 512 * h + 512],
                                             start=True, stop=True))
            K["vr", n] = (pi, p, t)

        def d_kv(n):
            e, b = divmod(n, 4)
            if e == 8:
                return
            c = slice(1024 * b, 1024 * b + 1024)
            pi, p, t = K["vr", n]
            io, ob, fo = rO.take()
            if n % GMOD in GSET:
                t = A.did(A.on(t, *fo).activation(ob, p, ACT.Copy))
                pV.free(pi, t)
                t = G.did(G.on(t).tensor_tensor(ob, ob, B[KF][:, c], ALU.mult))
            else:
                t = vt(ob, B[KF][:, c], p, ALU.mult, t, *fo)
                pV.free(pi, t)
            K["kv", n] = (io, ob, t)

        def d_outer(n):
            e, b = divmod(n, 4)
            c = slice(1024 * b, 1024 * b + 1024)
            io, ob, t = K["kv", n] if e < 8 else (None, B[KF][:, c], (V.sem, 0))
            i0, m0, f0 = rM0.take()
            i1, m1, f1 = rM1.take()
            V.did(V.on(t, *f0).tensor_tensor_scan(m0, BETA[0][:, c], ob, 0.0, ALU.mult, ALU.add))
            t = V.did(V.on(t, *f1).tensor_tensor_scan(m1, BETA[1][:, c], ob, 0.0, ALU.mult, ALU.add))
            if io is not None:
                rO.free(io, t)
            ip, pb, fp = rP.take()
            t = G.did(G.on(t, *fp).tensor_tensor(pb, m0, m1, ALU.add))
            rM0.free(i0, t)
            rM1.free(i1, t)
            K["sum", n] = (ip, pb, t)

        def d_query(n):
            e, b = divmod(n, 4)
            c = slice(1024 * b, 1024 * b + 1024)
            ip, pb, t = K["sum", n]
            iq, qb, fq = rQ.take()
            t = vt(qb, pb, B[QF][:, c], ALU.mult, t, *fq)
            rP.free(ip, t)
            pi, p, fr = pN.take()
            for q in range(8):
                tp = PE.did(PE.on(t, *fr).matmul(p[:, 128 * q:128 * q + 128], qb[:, 128 * q:128 * q + 128], hsum[:, :],
                                                 start=True, stop=True, skip_group_check=True))
            rQ.free(iq, tp)
            src = p.rearrange("p (i h) -> p i h", h=128)[:, :, 0:16]
            dst = num[:, 8 * b:8 * b + 8, :, e] if e < 8 else DEN[:, 8 * b:8 * b + 8, :]
            t = A.did(A.on(tp).activation(dst, src, ACT.Copy))
            pN.free(pi, t)
            K["num", n] = t

        skewed([(0, d_value), (1, d_kv), (DL, d_outer), (DL + 2, d_query)], 36)
        barrier()
        t_we = dma(WW[:, 0:8, :], I["wE"], sem("s_we"))
        one = lambda z: z.rearrange("p (a t) -> p a t", a=1)
        unit = lambda n: one(SS[:, 512 * n:512 * n + 512])
        pT = Ring([bank(0), bank(1)])
        pP = Ring([bank(i) for i in range(2, 8)])
        rHF = Ring([unit(2), unit(3)])
        rYF = Ring([unit(4), unit(5)])
        rZ = Ring([unit(6), unit(7)])
        den = [SS[:, 512 * n:512 * n + 512].rearrange("p (i e) -> p i e", e=16) for n in range(2)]
        t = V.did(V.on().tensor_scalar(den[0], DEN[:, :, :], 1e-6, None, ALU.add))
        t_rd = V.did(V.on(t).reciprocal(den[1], den[0]))
        rX = Ring([rb(15), one(SC[:, :, :].rearrange("p i e -> p (i e)"))])
        rX.freed = [(), (t,)]

        def f_div(g):
            s4 = slice(4 * g, 4 * g + 4)
            ib, buf, fr = rHF.take()
            o = buf[:, 0, :].rearrange("p (n e) -> p n e", e=8)
            a = num[:, s4, :, :].rearrange("p i h e -> p (i h) e")
            r = den[1][:, s4, :].rearrange("p i h -> p (i h)").unsqueeze(2).to_broadcast([128, 64, 8])
            t = vt(o, a, r, ALU.mult, t_rd, *fr)
            K["div", g] = t
            pi, p, fr = pT.take()
            t = transposes(p, lambda j: buf[:, 0, 128 * j:128 * j + 128], ident, t, *fr)
            rHF.free(ib, t)
            iy, yb, fy = rYF.take()
            t = A.did(A.on(t, *fy).activation(yb[:, 0, :], p, ACT.Copy))
            pT.free(pi, t)
            K["yf", g] = (iy, yb, t)

        def f_out(g):
            iy, yb, t = K["yf", g]
            pi, p, fr = pP.take()
            for j in range(4):
                t = PE.did(PE.on(t, *fr).matmul(p[:, 128 * j:128 * j + 128], yb[:, 0, 128 * j:128 * j + 128], wo1[:, :],
                                                start=True, stop=True, skip_group_check=True))
            rYF.free(iy, t)
            K["po", g] = (pi, p, t)

        def f_res(g):
            pi, p, t = K["po", g]
            xa = XA[:, 4 * g:4 * g + 4, :].rearrange("p i c -> p (i c)")
            t = vt(xa, xa, p, ALU.add, t)
            pP.free(pi, t)
            K["st", g] = rstd(g, 0, 1e-5, stats(g, lambda i: XA[:, i, :], 0, t))

        def f_norm(g):
            iz, zb, fz = rZ.take()
            for j in range(4):
                i = 4 * g + j
                t = normed(i, 0, zb[:, 0, 128 * j:128 * j + 128], XA[:, i, :], K["st", g], *fz)
            K["z", g] = (iz, zb, t)

        def f_aff(g):
            iz, zb, t = K["z", g]
            z = zb[:, 0, :].rearrange("p (i c) -> p i c", c=128)
            row = lambda r: rows[:, r, :].unsqueeze(1).to_broadcast([128, 4, 128])
            t = vt(z, z, row(1), ALU.mult, t)
            t = vt(XA[:, 4 * g:4 * g + 4, :], z, row(2), ALU.add, t)
            rZ.free(iz, t)
            K["st1", g] = rstd(g, 1, 1e-5, stats(g, lambda i: XA[:, i, :], 1, t))

        def f_add(g):
            add_normed(g, 1, lambda i: XA[:, i, :], K["st1", g])

        if stop == 3:
            skewed([(0, f_div), (1, f_out), (2, f_res), (3, f_norm), (4, f_aff), (5, f_add)], NG)
            finish()
            return

        rHN = Ring([rb(0), rb(1)])
        XF = 0
        scrQ = nc.dram_tensor("scrQ", [4, 3, 128, 1024], BF, kind="Internal").ap()
        scrK = nc.dram_tensor("scrK", [3, 32, T], BF, kind="Internal").ap()
        scrM = nc.dram_tensor("scrM", [8, 24, 1024], BF, kind="Internal").ap()
        qs = [B[i][0:96, 0:4096].bitcast(BF).rearrange("p (h t) -> p h t", h=8) for i in (1, 5, 3)]
        kst = [B[2][0:96, 2048 * i:2048 * i + 2048].bitcast(BF).rearrange("p (k t) -> p k t", k=4) for i in range(2)]
        VA = B[4][:, 0:4096].rearrange("p (i k e) -> p i k e", k=4, e=32)
        s_fill = sem("s_fill")

        def fill(z, src, *producers):
            for a in range(3):
                dma(z[32 * a + 24:32 * a + 32, :, :], src, s_fill, *producers)

        for z in (qs[0], qs[2]):
            fill(z, I["zeros"])
        for z in kst:
            fill(z, I["ones"])

        def e_values(g):
            t = V.did(V.on().memset(cf(4, g), 0.0))
            K["va", g] = V.did(V.on(t).memset(VA[:, 4 * g:4 * g + 4, :, 8:9].rearrange("p i k e -> p (i k) e"), 1.0))

        rB = [RB[:, :, :].rearrange("p n t -> p (n t)")[:, 5120 + 768 * i:5888 + 768 * i].bitcast(BF).rearrange(
            "p (a t) -> p a t", a=3) for i in range(2)]
        rKb = [RB[0:32, :, :].rearrange("p n t -> p (n t)")[:, 6656 + 768 * i:7424 + 768 * i].bitcast(BF).rearrange(
            "p (a t) -> p a t", a=3) for i in range(1)]
        rBq, rBk = Ring([z for z in rB]), Ring([z for z in rKb])
        rR = Ring([rb(2, 4), rb(6, 4)])

        def e_stats(g):
            K["st", g] = rstd(g, 0, 1e-5, stats(g, lambda i: X[:, i, :], 0, K["x", g]), then=1e-6)

        def e_norm(g):
            ib, buf, fr = rHN.take()
            for j in range(4):
                i = 4 * g + j
                t = V.did(V.on(K["st", g]).tensor_scalar(XA[:, i, :], X[:, i, :], mv[0][:, i, 0:1],
                                                         rs[0][:, i, 0:1], ALU.subtract, ALU.mult))
                t = A.did(A.on(t, *fr).activation(buf[:, 0, 128 * j:128 * j + 128], XA[:, i, :], ACT.Copy,
                                                  scale=rs[0][:, i, 2:3]))
            K["hn", g] = (ib, buf, t)

        def turn_scaled(g, col):
            ib, buf, t = K["hn", g]
            pi, p, fr = pT.take()
            t = transposes(p, lambda j: buf[:, 0, 128 * j:128 * j + 128], ident, t, *fr)
            rHN.free(ib, t)
            t = A.did(A.on(t).activation(cf(XF, g), p, ACT.Copy, scale=col))
            pT.free(pi, t)
            K["xf", g] = t

        def e_turn(g):
            turn_scaled(g, ANW)

        def split3(ring, np_, r, t, out_dma):
            ib, o, fo = ring.take()
            P_ = slice(0, np_)
            t = V.did(V.on(t, *fo).tensor_copy(o[P_, 0, :], r[P_, 0, :]))
            t = vt(r[P_, 1, :], r[P_, 0, :], o[P_, 0, :], ALU.subtract, t)
            t = V.did(V.on(t).tensor_copy(o[P_, 1, :], r[P_, 1, :]))
            t = vt(r[P_, 2, :], r[P_, 1, :], o[P_, 1, :], ALU.subtract, t)
            t = V.did(V.on(t).tensor_copy(o[P_, 2, :], r[P_, 2, :]))
            td = out_dma(o, t)
            ring.free(ib, td)
            return t, td

        def e_proj(g):
            for name, w, np_, scale in (("q", wqE, 128, 8.0 ** -0.5), ("k", wkE, 32, 1.0)):
                pi, p, fr = pP.take()
                t = PE.did(PE.on(K["xf", g], *fr).matmul(p[0:np_, :], w[:, :], cf(XF, g), start=True, stop=True))
                ir, r, fr = rR.take()
                t = A.did(A.on(t, *fr).activation(r[0:np_, 0, :], p[0:np_, :], ACT.Copy, scale=scale))
                pP.free(pi, t)
                K[name, g] = (ir, r, t)
            pi, p, fr = pP.take()
            for j in range(4):
                t = PE.did(PE.on(*fr).matmul(p[:, 32 * j:32 * j + 32], cf(XF, g)[:, 128 * j:128 * j + 128], wvE[:, :],
                                             start=True, stop=True, skip_group_check=True))
            for j in range(4):
                t2 = A.did(A.on(t, K["va", g]).activation(VA[:, 4 * g + j, :, 0:8],
                                                          p[:, 32 * j:32 * j + 32].rearrange("p (k e) -> p k e", e=8),
                                                          ACT.Copy))
            pP.free(pi, t2)

        def e_cut(g):
            b, h = g // 2, g % 2
            c = slice(512 * h, 512 * h + 512)
            ir, r, t = K["q", g]
            t, K["dq", g] = split3(rBq, 128, r, t, lambda o, t: dma(
                scrQ[b, :, :, c].rearrange("a p t -> p a t"), o[:, :, :], sem("s_sq"), t))
            rR.free(ir, t)
            ir, r, t = K["k", g]
            t, K["dk", g] = split3(rBk, 32, r, t, lambda o, t: dma(
                scrK[:, :, 512 * g:512 * g + 512].rearrange("a p t -> p a t"), o[:, :, :], sem("s_sk"), t))
            rR.free(ir, t)

        def load_k(b, *producers):
            s_ks = sem("s_ks")
            for a in range(3):
                for c in range(3):
                    SP.on(K["dk", 2 * b], K["dk", 2 * b + 1], *producers).dma_start(
                        kst[b % 2][32 * a + 8 * c:32 * a + 8 * c + 8, :, :],
                        scrK[c, :, 1024 * b:1024 * b + 1024].rearrange("(k d) t -> d k t", d=8)).then_inc(s_ks, 16)
            K["keys", b] = (s_ks, 144)

        clock = {"PE": 0.0, "V": 0.0, "A": 0.0, "G": 0.0}

        def load_q(u, *producers):
            s, n, b, hh = sem("s_q"), 0, u // 2, u % 2
            for a in range(3):
                for c in range(3):
                    SP.on(K["dq", 2 * b], K["dq", 2 * b + 1], *producers).dma_start(
                        qs[u % 3][32 * a + 8 * c:32 * a + 8 * c + 8, :, :],
                        scrQ[b, a, 64 * hh:64 * hh + 64, :].rearrange("(h d) t -> d h t", d=8)).then_inc(s, 16)
                    n += 16
            if u >= 3:
                SP.eng.dma_start(qs[u % 3][24:27, :, :], I["zrow"]).then_inc(s, 16)
                n += 16
            K["queries", u] = (s, n)
            K["queries at", u] = clock["PE"] + 5000

        T_FILL = (s_fill, 16 * 15)

        def e_load(g):
            if g == 1:
                fill(qs[1], I["zeros"], K["div", NG - 1])
                load_k(0)
                load_q(0)
                load_q(1, K["div", NG - 1])
            if g == 3:
                load_k(1)
                load_q(2)

        skewed([(0, f_div), (1, f_out), (2, f_res), (3, f_norm), (4, f_aff), (5, f_add), (6, e_stats), (6, e_values),
                (7, e_norm), (8, e_turn), (9, e_proj), (10, e_cut), (11, e_load)], NG)
        MX = SS[:, 0:256].rearrange("p (r i h c) -> p r i h c", r=2, i=8, c=2)
        NM = SS[:, 256:640].rearrange("p (r a n) -> p r a n", r=2, a=3)
        M3 = SS[:, 640:832].bitcast(BF).rearrange("p (r i n) -> p r i n", r=2, i=8)
        RC = SS[:, 832:896].rearrange("p (r n) -> p r n", r=4)
        MF = SS[0:24, 1024:2048].bitcast(BF).rearrange("p (r t) -> p r t", r=2)
        p1 = Ring([bank(i) for i in P1B])
        pS2 = Ring([bank(i) for i in PSB])
        pOE = Ring([bank(i) for i in OEB])
        pX = Ring([bank(7)])
        barrier()

        def head(u, h):
            b, hh = u // 2, u % 2
            return qs[u % 3][:, h, :], kst[b % 2][:, 2 * hh + h // 4, :]

        def spend(engine, ns, after=0.0):
            clock[engine] = max(clock[engine], after) + ns
            return clock[engine]


        def pass1(u):
            mx = MX[:, u % 2, :, :, :]
            while ("queries", u) not in K or ("keys", u // 2) not in K:
                yield None
            for h in range(8):
                Q, Kk = head(u, h)
                for i in range(8):
                    for c in range(i // 4 + 1):
                        yield max(p1.next_free(), K["queries at", u])
                        pi, p, fr = p1.take()
                        n = 512 if c < i // 4 else 128 * (i % 4 + 1)
                        dg = c == i // 4
                        t = PE.did(PE.on(T_FILL, K["queries", u], K["keys", u // 2], *fr).matmul(
                            p[:, 0:n], Q[:, 128 * i:128 * i + 128], Kk[:, 512 * c:512 * c + n],
                            start=True, stop=not dg))
                        if dg:
                            t = PE.did(PE.on().matmul(p[:, n - 128:n], identb[:, :], msk[:, :],
                                                      start=False, stop=True))
                        t = V.did(V.on(t).tensor_reduce(mx[:, i, h, c:c + 1], p[:, 0:n], AX, ALU.max))
                        w = spend("PE", 0.417 * n + 3 + 56 * dg)
                        p1.free(pi, t, when=spend("V", 1.04 * n + 65, w + LAT) + LAT)
            nm = NM[:, u % 2, :, :]
            v = lambda a: nm[:, a, :].rearrange("p (i h) -> p i h", h=8)
            m3 = M3[:, u % 2, :, :].rearrange("p i (a h) -> p i a h", a=3)
            t = V.did(V.on(t).tensor_scalar(v(0)[:, 0:4, :], mx[:, 0:4, :, 0], -1.0, None, ALU.mult))
            t = vt(v(1)[:, 4:8, :], mx[:, 4:8, :, 0], mx[:, 4:8, :, 1], ALU.max, t)
            t = V.did(V.on(t).tensor_scalar(v(0)[:, 4:8, :], v(1)[:, 4:8, :], -1.0, None, ALU.mult))
            t = V.did(V.on(t).tensor_copy(m3[:, :, 0, :], v(0)))
            t = vt(v(1), v(0), m3[:, :, 0, :], ALU.subtract, t)
            t = V.did(V.on(t).tensor_copy(m3[:, :, 1, :], v(1)))
            t = vt(v(2), v(1), m3[:, :, 1, :], ALU.subtract, t)
            t = V.did(V.on(t).tensor_copy(m3[:, :, 2, :], v(2)))
            tasks.append(guard(u, t, spend("V", 900)))

        def guard(u, t, at):
            while held:
                yield None
            held.append(u)
            yield max(at + LAT, pX.next_free())
            pi, p, fr = pX.take()
            pb = p.bitcast(BF)
            for i in range(8):
                tp = PE.did(PE.on(t, *fr).transpose(pb[0:24, 128 * i:128 * i + 128], M3[:, u % 2, i, :], identb[:, :]))
            t = V.did(V.on(tp, *K.get(("md", u - 2), ())).tensor_copy(MF[:, u % 2, :], pb[0:24, 0:1024]))
            w = spend("V", 1130, spend("PE", 8 * 60) + LAT)
            pX.free(pi, t, when=w + LAT)
            held.pop()
            td = dma(scrM[u, :, :], MF[:, u % 2, :], sem("s_sm"), t)
            K["md", u] = (td,)
            K["guard", u] = dma(qs[u % 3][24:27, :, :], scrM[u, :, :].rearrange("(a h) t -> a h t", h=8),
                            sem("s_m"), td, tp)
            K["guard at", u] = w + 5000

        rP4 = Ring([rb(0, 4), rb(4, 4), rb(8, 4)])
        rOS = Ring([rb(12), rb(13)])
        AT = XF

        def normalise(u, kl, qc, oi, po, tp, at):
            b, kv = u // 2, 2 * (u % 2) + kl
            io, ob, fr = rOS.take()
            t = A.did(A.on(tp, *fr).activation(ob[:, 0, :], po, ACT.Copy))
            w = spend("A", 480, at + LAT)
            pOE.free(oi, t, when=w + LAT)
            yield w
            while held:
                yield None
            held.append(u)
            yield max(w + LAT, pX.next_free())
            pi, p, fr = pX.take()
            t = transposes(p, lambda j: ob[:, 0, 128 * j:128 * j + 128], ident, t, *fr)
            w = spend("PE", 4 * 218)
            rOS.free(io, t)
            yield w
            p3 = p.rearrange("p (n e) -> p n e", e=32)
            rc = RC[:, (2 * kl + qc), :].unsqueeze(2)
            t = V.did(V.on(t).reciprocal(rc, p3[:, :, 8:9]))
            dst = B[AT][:, 1024 * b + 512 * qc:1024 * b + 512 * qc + 512].rearrange(
                "p (i k j e) -> p k i j e", i=4, k=4, j=4)[:, kv, :, :, :]
            four = lambda z: z.rearrange("p (i j) e -> p i j e", j=4)
            t2 = vt(dst, four(p3[:, :, 0:8]), four(rc).to_broadcast([128, 4, 4, 8]), ALU.mult, t)
            pX.free(pi, t2, when=spend("V", 650, w + LAT) + LAT)
            held.pop()
            if u % 2 == 1 and kl == 1:
                K["at", 2 * b + qc] = t2
                ready.append(2 * b + qc)

        tasks, held, ready = [], [], []

        GROUPS = [(u, kl, qc) for u in range(8) for qc in range(2) for kl in range(2)]
        STEPS = [(n, kt) for n, (u, kl, qc) in enumerate(GROUPS) for kt in range(4 * qc + 4)]

        def scores(n, kt):
            u, kl, qc = GROUPS[n]
            while ("guard", u) not in K:
                yield None
            if (n, kt) == (0, 0):
                for x in (A, V):
                    x.on(*[K["dq", g] for g in range(NG)], *[K["dk", g] for g in range(NG)])
            off = max(0, 128 * (kt - 4 * qc))
            w = 512 - off
            for z in range(4):
                ring = pS6 if done1 else pS2
                yield max(ring.next_free(), K["guard at", u])
                ring = pS6 if done1 else pS2
                if z == 0:
                    ip, pb, fp = rP4.take()
                si, ps, fr = ring.take()
                Q, Kk = head(u, 4 * kl + z)
                dg = kt >= 4 * qc
                t = PE.did(PE.on(K["guard", u], *fr).matmul(
                    ps[:, 0:w], Kk[:, 128 * kt:128 * kt + 128],
                    Q[:, 512 * qc + off:512 * qc + 512], start=True, stop=True))
                t = A.did(A.on(t, *fp).activation(pb[:, z, 0:w], ps[:, 0:w], ACT.Exp))
                at = spend("A", 0.83 * w + 53, spend("PE", 0.417 * w + 3) + LAT)
                ring.free(si, t, when=at + LAT)
            if dg:
                t = G.did(G.on(t).affine_select(
                    out=pb[:, :, 0:128], in_=pb[:, :, 0:128], compare_op=ALU.is_ge, fill=0.0, base=0,
                    pattern=[[0, 4], [1, 128]], channel_multiplier=-1))
                at = spend("G", GC, at + LAT)
            K["exp", n, kt] = (ip, pb, t, off, w, at)
            if (kl, qc, kt) == (1, 1, 7):
                K["p2", u] = PE.last()
                if u + 3 < 8:
                    load_q(u + 3, K["p2", u])
                if u % 2 == 1 and u // 2 + 2 < 4:
                    load_k(u // 2 + 2, K["p2", u])

        def products(n, kt):
            u, kl, qc = GROUPS[n]
            b, kv = u // 2, 2 * (u % 2) + kl
            at = K["exp", n, kt][5] + LAT
            yield max(at, pOE.next_free()) if kt == 0 else at
            if kt == 0:
                K["oe"] = pOE.take()
            oi, po, fo = K["oe"]
            ip, pb, t, off, w, _ = K["exp", n, kt]
            for j in range(4):
                tp = PE.did(PE.on(t, *fo).matmul(
                    po[32 * j:32 * j + 32, off:off + w], VA[:, 8 * b + kt, kv, :], pb[:, j, 0:w],
                    start=(kt == 0), stop=(kt == 4 * qc + 3), skip_group_check=True))
            rP4.free(ip, tp)
            at = spend("PE", 1.667 * w + 60)
            if kt == 4 * qc + 3:
                tasks.append(normalise(u, kl, qc, oi, po, tp, at))

        def pass2():
            for s in range(len(STEPS) + PLAG):
                if s < len(STEPS):
                    yield from scores(*STEPS[s])
                if s >= PLAG:
                    yield from products(*STEPS[s - PLAG])

        for u in range(3):
            K["queries at", u] = 0.0
        pS6 = Ring([bank(i) for i in PSB + P1B])
        done1 = []

        rYF = Ring([unit(4), unit(5)])
        rHN = Ring([unit(6), unit(7)])
        rX = Ring([rb(14), rb(15)])
        HB = XF
        scf = SC[:, :, :].rearrange("p i e -> p (i e)")
        K["hx", -2] = K["hx", -1] = (V.sem, 0)
        flat8 = lambda z: z.rearrange("p i e -> p (i e)")

        def banks():
            return pS6 if done1 else p1

        def post(g):
            s4 = slice(4 * g, 4 * g + 4)
            scr = lambda o, e: scf[:, 256 * (g % 2) + o:256 * (g % 2) + o + 4 * e].rearrange("p (i e) -> p i e", e=e)
            LG, comb, T8, s0, s1, s2, s3 = [scr(32 * q, 8) for q in range(7)]
            c0, c1, c2, c3, left, need = [scr(224 + 4 * q, 1) for q in range(6)]
            yield banks().next_free()
            ring = banks()
            pi, p, fr = ring.take()
            t = transposes(p, lambda j: cf(AT, g)[:, 128 * j:128 * j + 128], ident, K["at", g], *fr)
            iy, yb, fy = rYF.take()
            t = A.did(A.on(t, *fy).activation(yb[:, 0, :], p, ACT.Copy))
            w = spend("A", 480, spend("PE", 4 * 218) + LAT)
            ring.free(pi, t, when=w + LAT)
            yield max(w + LAT, banks().next_free())
            ring = banks()
            pi, p, fr = ring.take()
            for j in range(4):
                t = PE.did(PE.on(t, *fr).matmul(p[:, 128 * j:128 * j + 128], yb[:, 0, 128 * j:128 * j + 128],
                                                woE[:, :], start=True, stop=True, skip_group_check=True))
            rYF.free(iy, t)
            xa = XA[:, s4, :].rearrange("p i c -> p (i c)")
            t = vt(xa, xa, p, ALU.add, t)
            w = spend("V", 600, spend("PE", 4 * 218) + LAT)
            ring.free(pi, t, when=w + LAT)
            yield w
            t = stats(g, lambda i: XA[:, i, :], 0, t)
            R = rs[0]
            t = G.did(G.on(t).tensor_tensor(R[:, s4, 3], mv[0][:, s4, 0], mv[0][:, s4, 0], ALU.mult))
            t = G.did(G.on(t).tensor_tensor(R[:, s4, 4], R[:, s4, 3], mv[0][:, s4, 1], ALU.add))
            t = G.did(G.on(t).tensor_scalar(R[:, s4, 5], R[:, s4, 4], 1e-6, None, ALU.add))
            t = G.did(G.on(t).tensor_tensor(R[:, s4, 0], R[:, s4, 5], mhalf[:, 0:4], ALU.pow))
            yield spend("V", 1300) + 2500
            ib, buf, fr = rHN.take()
            for j in range(4):
                i = 4 * g + j
                t2 = A.did(A.on(t, *fr).activation(buf[:, 0, 128 * j:128 * j + 128], XA[:, i, :], ACT.Copy,
                                                   scale=rs[0][:, i, 0:1]))
            w = spend("A", 4 * 250)
            yield max(w + LAT, banks().next_free())
            ring = banks()
            pi, p, fr = ring.take()
            t = transposes(p, lambda j: buf[:, 0, 128 * j:128 * j + 128], ident, t2, *fr)
            rHN.free(ib, t)
            t = A.did(A.on(t).activation(cf(HB, g), p, ACT.Copy, scale=FNW))
            w = spend("A", 570, spend("PE", 4 * 218) + LAT)
            ring.free(pi, t, when=w + LAT)
            yield max(w + LAT, banks().next_free())
            ring = banks()
            pi, p, fr = ring.take()
            for j in range(4):
                t = PE.did(PE.on(t, *fr).matmul(p[:, 8 * j:8 * j + 8], cf(HB, g)[:, 128 * j:128 * j + 128],
                                                gateE[:, :], start=True, stop=True, skip_group_check=True))
            t = V.did(V.on(t).tensor_copy(flat8(LG), p[:, 0:32]))
            ring.free(pi, t, when=spend("V", 100, spend("PE", 4 * 430) + LAT) + LAT)
            for j in range(4):
                tm = V.did(V.on(t).max(T8[:, j, :], LG[:, j, :]))
            bc8 = lambda z: z.to_broadcast([128, 4, 8])
            tx = vt(s3, LG, bc8(T8[:, :, 0:1]), ALU.subtract, tm)
            ty = vt(c0, T8[:, :, 1:2], T8[:, :, 0:1], ALU.subtract, tm)
            tx = A.did(A.on(tx, K["hx", g - 2]).activation(comb, s3, ACT.Exp))
            ty = A.did(A.on(ty).activation(c1, c0, ACT.Exp))
            yield spend("A", 200, spend("V", 900) + LAT) + LAT
            t = pick(LG, T8[:, :, 1:2], 2, 8, rst8, (s0, s1, s2), left, need, tm, nt=4)
            yield spend("V", 1900)
            t = V.did(V.on(t, ty).tensor_scalar(c2, c1, 1.0, None, ALU.add))
            t = V.did(V.on(t).reciprocal(c3, c2))
            t = vt(s1, s0, comb, ALU.mult, t, tx)
            t = vt(comb, s1, bc8(c3), ALU.mult, t)
            spend("V", 900)
            for j in range(4):
                x = XA[:, 4 * g + j, :]
                for half in range(2):
                    yield banks().next_free()
                    ring = banks()
                    pi, p, fr = ring.take()
                    tp = PE.did(PE.on(t_we, *fr).matmul(p, cf(HB, g)[:, 128 * j:128 * j + 128],
                                                        wE[:, 4 * half:4 * half + 4, :].rearrange("p e c -> p (e c)"),
                                                        start=True, stop=True))
                    for q in range(4):
                        e = 4 * half + q
                        t = V.did(V.on(t, tp).scalar_tensor_tensor(x, p[:, 128 * q:128 * q + 128], comb[:, j, e:e + 1],
                                                                   x, ALU.mult, ALU.add))
                    ring.free(pi, t, when=spend("V", 4 * 263, spend("PE", 856) + LAT) + LAT)
            K["hx", g] = t
            t = rstd(g, 1, 1e-5, stats(g, lambda i: XA[:, i, :], 1, t))
            yield spend("V", 1300) + 2500
            add_normed(g, 1, lambda i: XA[:, i, :], t)
            spend("A", 4 * 340)

        first = (z for u in range(8) for z in pass1(u))
        second = (z for s in range(len(STEPS) + PLAG) for z in [
            *([scores(*STEPS[s])] if s < len(STEPS) else []), *([products(*STEPS[s - PLAG])] if s >= PLAG else [])])
        second = (z for stream in second for z in stream)
        END = object()
        heads = {}

        def look(stream):
            if stream not in heads or heads[stream] is None:
                heads[stream] = next(stream, END)
            return heads[stream]

        posts, count = [], {"first": 0, "second": 0}
        live = [second, first]
        while live or tasks or posts or ready:
            if ready and len(posts) < 2:
                posts.append(post(ready.pop(0)))
            best = None
            for z in [*tasks, *live[::-1], *posts]:
                at = look(z)
                if at is END:
                    for group in (tasks, live, posts):
                        if z in group:
                            group.remove(z)
                    if z is first:
                        done1.append(True)
                        pS6.freed, pS6.when = pS2.freed + p1.freed, pS2.when + p1.when
                    best = None
                    break
                if at is None:
                    continue
                if z is first and (count["first"] - count["second"]) / 96 > MOST:
                    at += PEN
                at = max(at, clock["PE"])
                if best is None or at < best[0]:
                    best = (at, z)
            if best is not None:
                at, z = best
                clock["PE"] = max(clock["PE"], heads[z])
                heads[z] = None
                if z in live:
                    count["first" if z is first else "second"] += 1 if z is first else 4 / 5
                look(z)
        finish()


def arrays(inputs):
    import numpy as np

    bf = mybir.dt.np(BF)
    a = {k: np.asarray(v) for k, v in inputs.items()}
    L = lambda n: a["L0_attn_" + n]
    M = lambda n: a["L0_ffn_" + n]
    N = lambda n: a["L1_attn_" + n]
    E = lambda n: a["L1_ffn_" + n]
    D = {"x": L("x").reshape(4096, 128)}
    eye = np.eye(128, dtype=np.float32)
    D["ident"], D["identb"] = eye, eye.astype(bf)
    z = np.zeros(128, np.float32)
    rep = lambda v: np.repeat(v, 8)
    bb = N("bbeta").reshape(16, 2)
    cols = [L("ln1_w"), L("ln1_b"), L("ln2_w"), L("ln2_b"), L("time_shift").reshape(128), L("time_first"),
            rep(bb[:, 0]), rep(bb[:, 1]), E("attn_norm_w"), E("ffn_norm_w")] + [z] * 6
    D["vecs"] = np.stack(cols, axis=1)
    stack = lambda ws: np.stack(ws, axis=1)
    wck = L("Wck").T.reshape(128, 4, 128)
    wcv = L("Wcv").T.reshape(4, 128, 128).transpose(1, 0, 2)
    D["wL0"] = np.concatenate([stack([L("Wk").T, L("Wv").T, L("Wr").T, L("Wcr").T]), wck, wcv], axis=1)
    D["gate0"] = M("w_gate").T
    w1 = np.concatenate([M("w1_e").reshape(1024, 128), M("w1_s")]).T
    w3 = np.concatenate([M("w3_e").reshape(1024, 128), M("w3_s")]).T
    w2 = np.concatenate([M("w2_e").transpose(0, 2, 1).reshape(1024, 128), M("w2_s").T])
    D["w1"], D["w3"] = w1, w3
    D["w2"] = w2.reshape(9, 128, 128).transpose(1, 0, 2).reshape(128, 1152)
    sel = np.zeros((96, 8, 128), np.float32)
    for p in range(3):
        for e in range(16):
            sel[32 * p + e, e // 2, 64 * (e % 2):64 * (e % 2) + 64] = 1
    D["sel"] = sel.reshape(96, 1024).astype(bf)
    r = np.ones((128, 32, 16), np.float32)
    r[:, :, 0] = 0
    D["rst16"] = r.reshape(128, 512)
    D["rst8"] = r[:, :, :8].reshape(128, 256)
    D["rk0"] = np.broadcast_to(np.array([3, 2, 1, 0], np.float32), (128, 32, 4))
    perm = np.arange(128).reshape(16, 2, 4)[:, ::-1, :].reshape(128)
    wv = N("Wv").reshape(128, 16, 8)
    wvr = [np.repeat(wv[:, :, e], 8, axis=1) for e in range(8)]
    wb = N("Wbeta").reshape(128, 16, 2)
    wbr = [np.repeat(wb[:, :, c], 8, axis=1) for c in range(2)]
    D["wL1"] = stack([N("Wq"), N("Wq")[:, perm], N("Wk"), N("Wk")[:, perm]] + wvr + wbr)
    D["wo1"] = N("Wo")
    D["hsum"] = np.repeat(np.eye(16, 128, dtype=np.float32), 8, axis=0)
    D["rows"] = np.stack([np.broadcast_to(v, (128, 128)) for v in (N("bo"), N("ln_gamma"), N("ln_beta"))], axis=1)
    inv = (1.0 / 10000.0 ** (np.arange(0, 8, 2, dtype=np.float32) / np.float32(8))).astype(np.float32)
    fr = (np.arange(1024, dtype=np.float32)[:, None] * inv[None, :]).astype(np.float32)
    c, s = np.cos(fr).T, np.sin(fr).T
    D["rope"] = np.stack([np.tile(np.concatenate([c, c]), (16, 1)), np.tile(np.concatenate([-s, s]), (16, 1))],
                         axis=1).astype(np.float32)
    D["wqE"], D["wkE"], D["wvE"], D["woE"] = E("wq").T, E("wk").T, E("wv").T, E("wo").T
    D["gateE"] = E("gate_w").T
    D["wE"] = E("expert_w").transpose(2, 0, 1)
    low = np.arange(128)[:, None] >= np.arange(128)[None, :]
    D["msk"] = np.where(low, 0, -1e30).astype(bf)
    D["zrow"] = np.zeros((3, 8, 1024), bf)
    D["zeros"], D["ones"] = np.zeros((8, 8, 1024), bf), np.ones((8, 4, 1024), bf)
    return {k: np.ascontiguousarray(v) for k, v in D.items()}


def kernel(**inputs):
    import concourse.bacc as bacc
    from concourse import mybir as mb
    from concourse.bass_utils import run_bass_kernel_spmd

    D = arrays(inputs)
    nc = bacc.Bacc("TRN2", target_bir_lowering=False, num_devices=1)
    I = {k: nc.dram_tensor(f"in_{k}", v.shape, mb.dt.from_np(v.dtype), kind="ExternalInput").ap()
         for k, v in D.items()}
    out = nc.dram_tensor("out_0_dram", (4096, 128), F32, kind="ExternalOutput").ap()
    build(nc, I, out, STOP)
    r = run_bass_kernel_spmd(nc, [{f"in_{k}": v for k, v in D.items()}], core_ids=[0])
    return r.results[0]["out_0_dram"].reshape(4, 1024, 128)
```
